# Optimizing a Trainium2 kernel written in Bass

```python
import numpy as np
import jax
import jax.numpy as jnp

def _softmax(x, axis=-1):
    return jax.nn.softmax(x, axis=axis)

def _gelu(x):
    return jax.nn.gelu(x, approximate=True)

def _silu(x):
    return jax.nn.silu(x)

def _sigmoid(x):
    return jax.nn.sigmoid(x)

def _layernorm(x, axis=-1, eps=1e-05):
    m = jnp.mean(x, axis=axis, keepdims=True)
    v = jnp.var(x, axis=axis, keepdims=True)
    return (x - m) / jnp.sqrt(v + eps)

def _scatter_add(tgt, idx, src, axis=0):
    return tgt.at[idx].add(src)

def _segment_sum(src, seg, n):
    return jax.ops.segment_sum(src, seg, n)
kernel_name = 'mk_xattn_ffn_d2_seqx_r8_d75ab4'

def setup_inputs(seed: int=0):
    np.random.seed(seed)
    _w = jnp.asarray

    def _rec_inputs():
        import jax
        import jax.numpy as jnp
        _rk = jax.random.key(seed)
        x = -0.0003929 + 0.9999 * jax.random.normal(jax.random.fold_in(_rk, 1), (4, 512, 128), jnp.float32)
        _lenS = 512 - jax.random.randint(jax.random.fold_in(_rk, 7), (4,), 0, max(1, 512 // 4) + 1, jnp.int32)
        _lenS2 = 77 - jax.random.randint(jax.random.fold_in(_rk, 8), (4,), 0, max(1, 77 // 4) + 1, jnp.int32)
        _ctx_1024P = jax.random.normal(jax.random.fold_in(_rk, 11), (4, 16, 128), jnp.float32)
        _ctx_1024c = jax.random.dirichlet(jax.random.fold_in(_rk, 511), 0.3 * jnp.ones((16,), jnp.float32), (4, 77))
        _ctx_1024t = jnp.einsum('bsk,bkd->bsd', _ctx_1024c, _ctx_1024P)
        _ctx_1024t = _ctx_1024t * jax.lax.rsqrt(jnp.mean(jnp.square(_ctx_1024t)) + 1e-12) * 0.953939
        ctx_1024 = -0.000514642 + 1.00011 * (_ctx_1024t + 0.3 * jax.random.normal(jax.random.fold_in(_rk, 611), (4, 77, 128), jnp.float32))
        return (x, ctx_1024)
    x, ctx_1024 = _rec_inputs()

    def _L0_xattn_setup():
        import jax, jax.numpy as jnp
        import numpy as np
        DIM = 128
        H = 16
        DH = 64
        INNER = H * DH
        SCALE = DH ** (-0.5)
        key = jax.random.key(seed)
        ks = jax.random.split(key, 6)
        B, L, R = (4, 512, 64)
        x = jax.random.normal(ks[0], (B, L, DIM), dtype=jnp.float32)
        context = jax.random.normal(ks[1], (B, R, DIM), dtype=jnp.float32)
        s = DIM ** (-0.5)
        Wq = jax.random.normal(ks[2], (DIM, INNER), dtype=jnp.float32) * s
        Wk = jax.random.normal(ks[3], (DIM, INNER), dtype=jnp.float32) * s
        Wv = jax.random.normal(ks[4], (DIM, INNER), dtype=jnp.float32) * s
        Wo = jax.random.normal(ks[5], (INNER, DIM), dtype=jnp.float32) * INNER ** (-0.5)
        return {'x': x, 'context': context, 'Wq': Wq, 'Wk': Wk, 'Wv': Wv, 'Wo': Wo}
    _L0_xattn_all = _L0_xattn_setup()
    _L0_xattn_in = {k: v for k, v in _L0_xattn_all.items() if k in ('Wq', 'Wk', 'Wv', 'Wo')}
    del _L0_xattn_all

    def _L0_ffn_setup():
        import jax, jax.numpy as jnp
        import numpy as np
        HID = 128
        INTER = 512
        RDIM = 128
        HEADS = 4
        NUM_EXPERTS = 2048
        NUM_KEYS = 128
        TOPK = 8
        B, T = (2, 256)
        key = jax.random.key(seed)
        ks = jax.random.split(key, 8)
        s = lambda fan_in: 1.0 / np.sqrt(fan_in)
        return {'hidden_states': jax.random.normal(ks[0], (B, T, HID), jnp.float32), 'Wq': jax.random.normal(ks[1], (HEADS * RDIM, HID), jnp.float32) * s(HID), 'keys': jax.random.normal(ks[2], (HEADS, NUM_KEYS, 2, RDIM // 2), jnp.float32) * s(RDIM // 2), 'down_embed': jax.random.normal(ks[3], (NUM_EXPERTS, HID), jnp.float32) * 0.02, 'up_embed': jax.random.normal(ks[4], (NUM_EXPERTS, HID), jnp.float32) * 0.02, 'Wg': jax.random.normal(ks[5], (INTER, HID), jnp.float32) * s(HID), 'Wu': jax.random.normal(ks[6], (INTER, HID), jnp.float32) * s(HID), 'Wd': jax.random.normal(ks[7], (HID, INTER), jnp.float32) * s(INTER)}
    _L0_ffn_all = _L0_ffn_setup()
    _L0_ffn_in = {k: v for k, v in _L0_ffn_all.items() if k in ('Wq', 'keys', 'down_embed', 'up_embed', 'Wg', 'Wu', 'Wd')}
    del _L0_ffn_all

    def _L1_xattn_setup():
        import jax, jax.numpy as jnp
        import numpy as np
        EMBED = 128
        HEADS = 16
        HEAD_DIM = EMBED // HEADS
        EXP_DIM = 2 * HEAD_DIM

        def _feature_map(x, fm_w, fm_b):
            z = jnp.einsum('nshd,ed->nshe', x, fm_w) + fm_b
            return jnp.concatenate([jnp.exp(z), jnp.exp(-z)], axis=-1)
        key = jax.random.key(seed)
        ks = jax.random.split(key, 7)
        N, S = (4, 256)
        values = jax.random.normal(ks[0], (N, S, EMBED), dtype=jnp.float32)
        keys_ = jax.random.normal(ks[1], (N, S, EMBED), dtype=jnp.float32)
        query = jax.random.normal(ks[2], (N, S, EMBED), dtype=jnp.float32)
        fm_w = jnp.eye(HEAD_DIM, dtype=jnp.float32) + 0.02 * jax.random.normal(ks[3], (HEAD_DIM, HEAD_DIM), dtype=jnp.float32)
        fm_b = 0.02 * jax.random.normal(ks[4], (HEAD_DIM,), dtype=jnp.float32)
        fc_w = jax.random.normal(ks[5], (EMBED, HEADS * EXP_DIM), dtype=jnp.float32) * (1.0 / np.sqrt(HEADS * EXP_DIM))
        fc_b = jnp.zeros((EMBED,), dtype=jnp.float32)
        return {'values': values, 'keys': keys_, 'query': query, 'fm_w': fm_w, 'fm_b': fm_b, 'fc_w': fc_w, 'fc_b': fc_b}
    _L1_xattn_all = _L1_xattn_setup()
    _L1_xattn_in = {k: v for k, v in _L1_xattn_all.items() if k in ('fm_w', 'fm_b', 'fc_w', 'fc_b')}
    del _L1_xattn_all

    def _L1_ffn_setup():
        import jax, jax.numpy as jnp
        import numpy as np
        B, S, H = (2, 256, 128)
        E, F, K = (64, 64, 8)
        G, TG = (8, 4)
        SCALE = 2.5
        F_SH = 64

        def _gate(x, gate_w, gate_bias):
            scores = jax.nn.sigmoid(x @ gate_w.T)
            sc = scores + gate_bias[None, :]
            T = x.shape[0]
            group_scores = jax.lax.top_k(sc.reshape(T, G, E // G), 2)[0].sum(-1)
            _, gidx = jax.lax.top_k(group_scores, TG)
            gmask = jnp.zeros((T, G), sc.dtype).at[jnp.arange(T)[:, None], gidx].set(1.0)
            smask = jnp.repeat(gmask, E // G, axis=1)
            masked = jnp.where(smask > 0, sc, -jnp.inf)
            _, tidx = jax.lax.top_k(masked, K)
            tw = jnp.take_along_axis(scores, tidx, axis=1)
            tw = tw / (tw.sum(-1, keepdims=True) + 1e-20)
            return (tidx, tw * SCALE)
        key = jax.random.key(seed)
        ks = jax.random.split(key, 9)

        def w(k, shape, fan_in):
            return jax.random.normal(k, shape, jnp.float32) / np.float32(np.sqrt(fan_in))
        return {'hidden_states': jax.random.normal(ks[0], (B, S, H), jnp.float32), 'gate_w': w(ks[1], (E, H), H), 'gate_bias': jax.random.normal(ks[2], (E,), jnp.float32) * 0.01, 'We_gate': w(ks[3], (E, H, F), H), 'We_up': w(ks[4], (E, H, F), H), 'We_down': w(ks[5], (E, F, H), F), 'Ws_gate': w(ks[6], (H, F_SH), H), 'Ws_up': w(ks[7], (H, F_SH), H), 'Ws_down': w(ks[8], (F_SH, H), F_SH)}
    _L1_ffn_all = _L1_ffn_setup()
    _L1_ffn_in = {k: v for k, v in _L1_ffn_all.items() if k in ('gate_w', 'gate_bias', 'We_gate', 'We_up', 'We_down', 'Ws_gate', 'Ws_up', 'Ws_down')}
    del _L1_ffn_all
    return {'x': x, 'ctx_1024': ctx_1024, 'L0_xattn_Wq': _L0_xattn_in['Wq'], 'L0_xattn_Wk': _L0_xattn_in['Wk'], 'L0_xattn_Wv': _L0_xattn_in['Wv'], 'L0_xattn_Wo': _L0_xattn_in['Wo'], 'L0_ffn_Wq': _L0_ffn_in['Wq'], 'L0_ffn_keys': _L0_ffn_in['keys'], 'L0_ffn_down_embed': _L0_ffn_in['down_embed'], 'L0_ffn_up_embed': _L0_ffn_in['up_embed'], 'L0_ffn_Wg': _L0_ffn_in['Wg'], 'L0_ffn_Wu': _L0_ffn_in['Wu'], 'L0_ffn_Wd': _L0_ffn_in['Wd'], 'L1_xattn_fm_w': _L1_xattn_in['fm_w'], 'L1_xattn_fm_b': _L1_xattn_in['fm_b'], 'L1_xattn_fc_w': _L1_xattn_in['fc_w'], 'L1_xattn_fc_b': _L1_xattn_in['fc_b'], 'L1_ffn_gate_w': _L1_ffn_in['gate_w'], 'L1_ffn_gate_bias': _L1_ffn_in['gate_bias'], 'L1_ffn_We_gate': _L1_ffn_in['We_gate'], 'L1_ffn_We_up': _L1_ffn_in['We_up'], 'L1_ffn_We_down': _L1_ffn_in['We_down'], 'L1_ffn_Ws_gate': _L1_ffn_in['Ws_gate'], 'L1_ffn_Ws_up': _L1_ffn_in['Ws_up'], 'L1_ffn_Ws_down': _L1_ffn_in['Ws_down']}

def reference(x, ctx_1024, L0_xattn_Wq, L0_xattn_Wk, L0_xattn_Wv, L0_xattn_Wo, L0_ffn_Wq, L0_ffn_keys, L0_ffn_down_embed, L0_ffn_up_embed, L0_ffn_Wg, L0_ffn_Wu, L0_ffn_Wd, L1_xattn_fm_w, L1_xattn_fm_b, L1_xattn_fc_w, L1_xattn_fc_b, L1_ffn_gate_w, L1_ffn_gate_bias, L1_ffn_We_gate, L1_ffn_We_up, L1_ffn_We_down, L1_ffn_Ws_gate, L1_ffn_Ws_up, L1_ffn_Ws_down):
    import jax
    import jax.numpy as jnp

    def _L0_xattn_ref(x, context, Wq, Wk, Wv, Wo):
        import jax, jax.numpy as jnp
        import numpy as np
        DIM = 128
        H = 16
        DH = 64
        INNER = H * DH
        SCALE = DH ** (-0.5)
        B, L, _ = x.shape
        R = context.shape[1]
        q = (x @ Wq).reshape(B, L, H, DH).transpose(0, 2, 1, 3)
        k = (context @ Wk).reshape(B, R, H, DH).transpose(0, 2, 1, 3)
        v = (context @ Wv).reshape(B, R, H, DH).transpose(0, 2, 1, 3)
        scores = jnp.einsum('bhld,bhrd->bhlr', q, k) * SCALE
        attn = jax.nn.softmax(scores, axis=-1)
        out = jnp.einsum('bhlr,bhrd->bhld', attn, v)
        out = out.transpose(0, 2, 1, 3).reshape(B, L, INNER)
        return out @ Wo

    def _L0_ffn_ref(hidden_states, Wq, keys, down_embed, up_embed, Wg, Wu, Wd):
        import jax, jax.numpy as jnp
        import numpy as np
        HID = 128
        INTER = 512
        RDIM = 128
        HEADS = 4
        NUM_EXPERTS = 2048
        NUM_KEYS = 128
        TOPK = 8
        B, T = (2, 256)
        b, t, _ = hidden_states.shape
        q = hidden_states @ Wq.T
        q = q.reshape(b, t, 2, HEADS, RDIM // 2)
        q = jnp.transpose(q, (2, 0, 1, 3, 4))
        sim = jnp.einsum('pbthn,hkpn->pbthk', q, keys)
        sx, ix = jax.lax.top_k(sim[0], TOPK)
        sy, iy = jax.lax.top_k(sim[1], TOPK)
        all_scores = (sx[..., :, None] + sy[..., None, :]).reshape(b, t, HEADS, TOPK * TOPK)
        all_indices = (ix[..., :, None] * NUM_KEYS + iy[..., None, :]).reshape(b, t, HEADS, TOPK * TOPK)
        scores, pk = jax.lax.top_k(all_scores, TOPK)
        indices = jnp.take_along_axis(all_indices, pk, axis=-1)
        down = down_embed[indices]
        up = up_embed[indices]
        w = jnp.einsum('btd,bthkd->bthk', hidden_states, down)
        w = jax.nn.silu(w) * jax.nn.softmax(scores, axis=-1)
        experts_states = jnp.einsum('bthk,bthkd->btd', w, up)
        mlp = jax.nn.silu(hidden_states @ Wg.T) * (hidden_states @ Wu.T) @ Wd.T
        return mlp + experts_states

    def _L1_xattn_ref(values, keys, query, fm_w, fm_b, fc_w, fc_b):
        import jax, jax.numpy as jnp
        import numpy as np
        EMBED = 128
        HEADS = 16
        HEAD_DIM = EMBED // HEADS
        EXP_DIM = 2 * HEAD_DIM

        def _feature_map(x, fm_w, fm_b):
            z = jnp.einsum('nshd,ed->nshe', x, fm_w) + fm_b
            return jnp.concatenate([jnp.exp(z), jnp.exp(-z)], axis=-1)
        N, S, _ = query.shape
        v = values.reshape(N, -1, HEADS, HEAD_DIM)
        k = keys.reshape(N, -1, HEADS, HEAD_DIM)
        q = query.reshape(N, -1, HEADS, HEAD_DIM)
        v, k, q = (_feature_map(x, fm_w, fm_b) for x in (v, k, q))
        scores = jnp.einsum('nqhd,nkhd->nhqk', q, k) / jnp.sqrt(jnp.float32(EMBED))
        attn = jax.nn.softmax(scores, axis=-1)
        out = jnp.einsum('nhql,nlhd->nqhd', attn, v)
        out = out.reshape(N, S, HEADS * EXP_DIM)
        return out @ fc_w.T + fc_b

    def _L1_ffn_ref(hidden_states, gate_w, gate_bias, We_gate, We_up, We_down, Ws_gate, Ws_up, Ws_down):
        import jax, jax.numpy as jnp
        import numpy as np
        B, S, H = (2, 256, 128)
        E, F, K = (64, 64, 8)
        G, TG = (8, 4)
        SCALE = 2.5
        F_SH = 64

        def _gate(x, gate_w, gate_bias):
            scores = jax.nn.sigmoid(x @ gate_w.T)
            sc = scores + gate_bias[None, :]
            T = x.shape[0]
            group_scores = jax.lax.top_k(sc.reshape(T, G, E // G), 2)[0].sum(-1)
            _, gidx = jax.lax.top_k(group_scores, TG)
            gmask = jnp.zeros((T, G), sc.dtype).at[jnp.arange(T)[:, None], gidx].set(1.0)
            smask = jnp.repeat(gmask, E // G, axis=1)
            masked = jnp.where(smask > 0, sc, -jnp.inf)
            _, tidx = jax.lax.top_k(masked, K)
            tw = jnp.take_along_axis(scores, tidx, axis=1)
            tw = tw / (tw.sum(-1, keepdims=True) + 1e-20)
            return (tidx, tw * SCALE)
        b, s, h = hidden_states.shape
        x = hidden_states.reshape(-1, h).astype(jnp.float32)
        tidx, tw = _gate(x, gate_w, gate_bias)
        T = x.shape[0]
        w_dense = jnp.zeros((T, E), tw.dtype).at[jnp.arange(T)[:, None], tidx].add(tw)

        def body(acc, ws):
            wg, wu, wdn, cw = ws
            hmid = jax.nn.silu(x @ wg) * (x @ wu)
            return (acc + cw[:, None] * (hmid @ wdn), None)
        y, _ = jax.lax.scan(body, jnp.zeros_like(x), (We_gate, We_up, We_down, w_dense.T))
        y = y.reshape(b, s, h)
        shared = jax.nn.silu(hidden_states @ Ws_gate) * (hidden_states @ Ws_up) @ Ws_down
        return y + shared
    x = x + _L0_xattn_ref(_layernorm(x, axis=-1), ctx_1024, L0_xattn_Wq, L0_xattn_Wk, L0_xattn_Wv, L0_xattn_Wo)
    x = x + _L0_ffn_ref(_layernorm(x, axis=-1), L0_ffn_Wq, L0_ffn_keys, L0_ffn_down_embed, L0_ffn_up_embed, L0_ffn_Wg, L0_ffn_Wu, L0_ffn_Wd)
    x = x + _L1_xattn_ref(ctx_1024, ctx_1024, _layernorm(x, axis=-1), L1_xattn_fm_w, L1_xattn_fm_b, L1_xattn_fc_w, L1_xattn_fc_b)
    x = x + _L1_ffn_ref(_layernorm(x, axis=-1), L1_ffn_gate_w, L1_ffn_gate_bias, L1_ffn_We_gate, L1_ffn_We_up, L1_ffn_We_down, L1_ffn_Ws_gate, L1_ffn_Ws_up, L1_ffn_Ws_down)
    return x

_drawn_inputs = setup_inputs


def setup_inputs(seed=0):
    import zlib

    import numpy as np

    out = dict(_drawn_inputs(seed))
    spreads = {'L1_xattn_fc_b': (0.0, 0.8)}
    factors = {'L0_ffn_Wq': 8.0,
     'L0_ffn_keys': 8.0,
     'L0_ffn_down_embed': 8.0,
     'L0_ffn_up_embed': 8.0,
     'L1_ffn_gate_bias': 15.693}
    for name, (base, spread) in spreads.items():
        noise = np.random.default_rng([zlib.crc32(name.encode()), seed]).standard_normal(out[name].shape)
        drawn = base * np.exp(spread * noise) if base else spread * noise
        out[name] = jnp.asarray(drawn.astype(out[name].dtype))
    for name, factor in factors.items():
        out[name] = (out[name] * factor).astype(out[name].dtype)
    return out
```

```python
import concourse.bass as bass
from concourse import mybir
from contextlib import ExitStack
import numpy as np

F32 = mybir.dt.float32
F32R = mybir.dt.float32r
ALU = mybir.AluOpType
ACT = mybir.ActivationFunctionType
AX = mybir.AxisListType.X

P = 128
BATCH, SEQ, D = 4, 512, 128
TOKENS = BATCH * SEQ
TILES = TOKENS // P
PER_BATCH = SEQ // P
KEYS = 77
CTX = BATCH * KEYS
HEADS = 16
ALL_KEYS = HEADS * KEYS
KEY_CHUNKS = (ALL_KEYS + P - 1) // P
LAST_KEYS = ALL_KEYS - (KEY_CHUNKS - 1) * P
EPS = 1e-5
BANK_HEADS = ((0, 6), (6, 5), (11, 5))
SIM_HEADS, SUBKEYS, TOPK = 4, 128, 8
EXPERTS = 2048
ROWS = EXPERTS // SUBKEYS
E_CHUNKS = EXPERTS // P
INTER = 512
MOE_E, MOE_F = 64, 64
PAIRS = MOE_E // 2
GROUPS, GROUP_E, TOP_GROUPS = 8, 8, 4
TW_SCALE = 2.5
BIG = 1e30


class Memory:

    def __init__(self, nc, stack, name):
        self.nc, self.stack, self.name = nc, stack, name

    def sb(self, name, shape, dt=F32):
        return self.stack.enter_context(self.nc.sbuf_tensor(f"{self.name}_{name}", list(shape), dt))

    def bank(self, name):
        return self.stack.enter_context(self.nc.psum_tensor(f"{self.name}_{name}", [P, 512], F32))

    def sem(self, name):
        return self.stack.enter_context(self.nc.semaphore(f"{self.name}_{name}"))


class Chain:

    def __init__(self, eng, sem, base=0):
        self.eng, self.sem, self.base, self.n = eng, sem, base, 0

    def link(self, instruction):
        self.n += 1
        instruction.then_inc(self.sem, 1)
        self.eng.wait_ge(self.sem, self.base + self.n)


def layer_norm(nc, name, x, xnT, ident, eps):
    with ExitStack() as stack:
        m = Memory(nc, stack, name)
        centred, squares, xn = m.sb("centred", [P, TILES, D]), m.sb("squares", [P, TILES, D]), m.sb("xn", [P, TILES, D])
        total, mean, ss, sd, rstd = (m.sb(n, [P, TILES]) for n in ("total", "mean", "ss", "sd", "rstd"))
        banks = [m.bank(f"turned{i}") for i in range(4)]
        chain, ss_ready, sd_ready, xn_ready, turned = (m.sem(n) for n in ("chain", "ss_ready", "sd_ready", "xn_ready", "turned"))
        block = stack.enter_context(nc.Block())

        @block.vector
        def _(dve):
            c = Chain(dve, chain)
            wide = [P, TILES, D]
            c.link(nc.vector.tensor_reduce(total[:, :], x[:, :, :], AX, ALU.add))
            c.link(nc.vector.tensor_scalar(mean[:, :], total[:, :], 1.0 / D, None, ALU.mult))
            c.link(nc.vector.tensor_tensor(centred[:, :, :], x[:, :, :], mean[:, :].unsqueeze(2).broadcast_to(wide), ALU.subtract))
            c.link(nc.vector.tensor_tensor(squares[:, :, :], centred[:, :, :], centred[:, :, :], ALU.mult))
            nc.vector.tensor_reduce(ss[:, :], squares[:, :, :], AX, ALU.add).then_inc(ss_ready, 1)
            dve.wait_ge(sd_ready, 1)
            c.link(nc.vector.reciprocal(rstd[:, :], sd[:, :]))
            for g in range(4):
                part = slice(4 * g, 4 * g + 4)
                nc.vector.tensor_tensor(xn[:, part, :], centred[:, part, :],
                                        rstd[:, part].unsqueeze(2).broadcast_to([P, 4, D]), ALU.mult).then_inc(xn_ready, 1)

        @block.scalar
        def _(act):
            act.wait_ge(ss_ready, 1)
            nc.scalar.activation(sd[:, :], ss[:, :], ACT.Sqrt, bias=eps[:, 0:1], scale=1.0 / D).then_inc(sd_ready, 1)
            for g in range(4):
                act.wait_ge(turned, g + 1)
                nc.scalar.activation(xnT[:, 512 * g:512 * g + 512], banks[g][:, :], ACT.Copy)

        @block.tensor
        def _(pe):
            for g in range(4):
                pe.wait_ge(xn_ready, g + 1)
                for i in range(4):
                    last = nc.tensor.transpose(banks[g][:, P * i:P * i + P], xn[:, 4 * g + i, :], ident[:, :])
                last.then_inc(turned, 1)


def attention(nc, m, stack, x, xnT, ident, keyT, value, scale, pieces, queries, n_queries,
              query_pe, query_act):
    scores_bank = [[m.bank(f"scores{s}{i}") for i in range(3)] for s in range(2)]
    out_bank = [m.bank(f"out{s}") for s in range(2)]
    top = m.sb("top", [P, 2, HEADS])
    neg_top = m.sb("neg_top", [P, 2, HEADS])
    exps = m.sb("exps", [P, 2, ALL_KEYS])
    sums = m.sb("sums", [P, 2, HEADS])
    inverse = m.sb("inverse", [P, 2, HEADS])
    probsT = m.sb("probsT", [P, 2, KEY_CHUNKS, P])
    query_ready, query_psum = m.sem("query_ready"), m.sem("query_psum")
    scores_ready, neg_top_ready, exps_ready, probs_ready = (m.sem(n) for n in ("scores_ready", "neg_top_ready", "exps_ready", "probs_ready"))
    turned, probsT_ready, out_ready, out_added = (m.sem(n) for n in ("turned", "probsT_ready", "out_ready", "out_added"))
    chain = m.sem("chain")
    CREDIT = 2
    LINKS = 2 * PER_BATCH
    block = stack.enter_context(nc.Block())

    @block.tensor
    def _(pe):
        pe.sem_inc(turned, CREDIT)
        pe.sem_inc(out_ready, CREDIT)
        with pe.Fori(0, BATCH) as b:
            n0 = b * PER_BATCH
            query_pe(pe, b, out_bank, out_added, query_psum)
            pe.wait_ge(query_ready, b + 1)

            def scores(j):
                pe.wait_ge(probsT_ready, n0 + (j + 1))
                for bank, col, n, q, first in pieces:
                    last = nc.tensor.matmul(scores_bank[j % 2][bank][:, col:col + n], queries[:, q, P * j:P * j + P],
                                            keyT[:, bass.ds(b * ALL_KEYS + first, n)], start=True, stop=True)
                last.then_inc(scores_ready, 1)

            def turn(j):
                pe.wait_ge(probs_ready, n0 + (j + 1))
                for c in range(KEY_CHUNKS):
                    rows = LAST_KEYS if c == KEY_CHUNKS - 1 else P
                    last = nc.tensor.transpose(scores_bank[j % 2][c // 4][0:rows, P * (c % 4):P * (c % 4) + P],
                                               exps[:, j % 2, P * c:P * c + rows], ident[:, :])
                last.then_inc(turned, 1)

            def values(j):
                pe.wait_ge(probsT_ready, n0 + (j + 1 + CREDIT))
                pe.wait_ge(out_added, n0 + (j + 1))
                for c in range(KEY_CHUNKS):
                    rows = LAST_KEYS if c == KEY_CHUNKS - 1 else P
                    last = nc.tensor.matmul(out_bank[j % 2][:, 0:D], probsT[0:rows, j % 2, c, :],
                                            value[0:rows, bass.ds((b * KEY_CHUNKS + c) * D, D)],
                                            start=(c == 0), stop=(c == KEY_CHUNKS - 1))
                last.then_inc(out_ready, 1)

            scores(0)
            for j in range(PER_BATCH):
                if j + 1 < PER_BATCH:
                    scores(j + 1)
                if j > 0:
                    values(j - 1)
                turn(j)
            values(PER_BATCH - 1)

    @block.scalar
    def _(act):
        act.sem_inc(probsT_ready, CREDIT)
        with act.Fori(0, BATCH) as b:
            n0 = b * PER_BATCH
            query_act(act, b, turned, out_bank, query_psum, query_ready)

            def exponentials(j):
                act.wait_ge(neg_top_ready, n0 + (j + 1))
                act.wait_ge(turned, n0 + (j + 1))
                for bank, (first, heads) in enumerate(BANK_HEADS):
                    for i in range(heads):
                        h = first + i
                        last = nc.scalar.activation(exps[:, j % 2, KEYS * h:KEYS * h + KEYS],
                                                    scores_bank[j % 2][bank][:, KEYS * i:KEYS * i + KEYS], ACT.Exp,
                                                    bias=neg_top[:, j % 2, h:h + 1], scale=scale,
                                                    accum_out=sums[:, j % 2, h:h + 1])
                last.then_inc(exps_ready, 1)

            def keep_turned(j):
                act.wait_ge(turned, n0 + (j + 1 + CREDIT))
                act.wait_ge(out_ready, n0 + (j + 1))
                for bank in range(3):
                    cs = slice(4 * bank, min(4 * bank + 4, KEY_CHUNKS))
                    full = slice(cs.start, min(cs.stop, KEY_CHUNKS - 1))
                    last = nc.scalar.activation(probsT[:, j % 2, full, :],
                                                scores_bank[j % 2][bank][:, 0:P * (full.stop - full.start)].rearrange("p (c t) -> p c t", t=P),
                                                ACT.Copy)
                last = nc.scalar.activation(probsT[0:LAST_KEYS, j % 2, KEY_CHUNKS - 1, :],
                                            scores_bank[j % 2][2][0:LAST_KEYS, P:2 * P], ACT.Copy)
                last.then_inc(probsT_ready, 1)

            exponentials(0)
            for j in range(PER_BATCH):
                if j + 1 < PER_BATCH:
                    exponentials(j + 1)
                keep_turned(j)

    @block.vector
    def _(dve):
        dve.sem_inc(out_added, CREDIT)
        with dve.Fori(0, BATCH) as b:
            n0 = b * PER_BATCH
            c = Chain(dve, chain, b * LINKS)

            def tops(j):
                dve.wait_ge(scores_ready, n0 + (j + 1))
                for bank, (first, heads) in enumerate(BANK_HEADS):
                    last = nc.vector.tensor_reduce(top[:, j % 2, first:first + heads],
                                                   scores_bank[j % 2][bank][:, 0:KEYS * heads].rearrange("p (h k) -> p h k", k=KEYS),
                                                   AX, ALU.max)
                c.link(last)
                nc.vector.tensor_scalar(neg_top[:, j % 2, :], top[:, j % 2, :], -scale, None, ALU.mult).then_inc(neg_top_ready, 1)

            def normalise(j):
                dve.wait_ge(exps_ready, n0 + (j + 1))
                c.link(nc.vector.reciprocal(inverse[:, j % 2, :], sums[:, j % 2, :]))
                e = exps[:, j % 2, :].rearrange("p (h k) -> p h k", k=KEYS)
                nc.vector.tensor_tensor(e, e, inverse[:, j % 2, :].unsqueeze(2).broadcast_to([P, HEADS, KEYS]), ALU.mult).then_inc(probs_ready, 1)

            def add(j):
                dve.wait_ge(out_ready, n0 + (j + 1 + CREDIT))
                row = x[:, bass.ds(b * PER_BATCH + j, 1), :].rearrange("p o d -> p (o d)")
                nc.vector.tensor_tensor(row, row, out_bank[j % 2][:, 0:D], ALU.add).then_inc(out_added, 1)

            tops(0)
            for j in range(PER_BATCH):
                if j + 1 < PER_BATCH:
                    tops(j + 1)
                normalise(j)
                if j > 0:
                    add(j - 1)
            add(PER_BATCH - 1)
            assert c.n == LINKS


def dense_attention(nc, io, x, xnT, ident, ctxT):
    with ExitStack() as keep:
        mk = Memory(nc, keep, "a0")
        keyT = mk.sb("keyT", [P, BATCH * ALL_KEYS])
        value = mk.sb("value", [P, BATCH * KEY_CHUNKS * D])
        with ExitStack() as stack:
            m = Memory(nc, stack, "a0s")
            wqT, wo = m.sb("wqT", [P, 8, D]), m.sb("wo", [P, 8, D])
            wk, wv = m.sb("wk", [P, 1024]), m.sb("wv", [P, 1024])
            kT, vT = m.sb("kT", [P, 8, CTX]), m.sb("vT", [P, 8, CTX])
            valueT = m.sb("valueT", [P, BATCH, ALL_KEYS])
            banks = [m.bank(f"b{i}") for i in range(8)]
            loaded, proj, kept, folded, folded_kept, turned = (m.sem(n) for n in ("loaded", "proj", "kept", "folded", "folded_kept", "turned"))
            block = stack.enter_context(nc.Block())

            @block.sync
            def _(sp):
                for dst, src in ((wk[:, :], io["Wk"]), (wv[:, :], io["Wv"]), (wqT[:, :, :], io["WqT"]), (wo[:, :, :], io["Wo"])):
                    sp.dma_start(dst, src).then_inc(loaded, 16)

            @block.tensor
            def _(pe):
                pe.wait_ge(loaded, 64)
                for c in range(8):
                    for i, w in enumerate((wk, wv)):
                        n = 2 * c + i
                        if n >= 8:
                            pe.wait_ge(kept, n - 7)
                        nc.tensor.matmul(banks[n % 8][:, 0:CTX], w[:, P * c:P * c + P], ctxT[:, :], start=True, stop=True).then_inc(proj, 1)
                for h in range(HEADS):
                    c, r = h // 2, 64 * (h % 2)
                    for i, (w, kv) in enumerate(((wqT, kT), (wo, vT))):
                        n = 2 * h + i
                        pe.wait_ge(kept, max(2 * c + 2, min(16, 9 + n)))
                        if n >= 8:
                            pe.wait_ge(folded_kept, n - 7)
                        nc.tensor.matmul(banks[n % 8][:, 0:CTX], w[r:r + 64, c, :], kv[r:r + 64, c, :], start=True, stop=True).then_inc(folded, 1)
                pe.wait_ge(folded_kept, 2 * HEADS)
                for b in range(BATCH):
                    for c in range(KEY_CHUNKS):
                        n = b * KEY_CHUNKS + c
                        rows = LAST_KEYS if c == KEY_CHUNKS - 1 else P
                        if n >= 32 and n % 4 == 0:
                            pe.wait_ge(kept, 16 + n // 4 - 7)
                        i = nc.tensor.transpose(banks[n // 4 % 8][0:rows, P * (n % 4):P * (n % 4) + P],
                                                valueT[:, b, P * c:P * c + rows], ident[:, :])
                        if n % 4 == 3:
                            i.then_inc(turned, 1)

            @block.scalar
            def _(act):
                for n in range(16):
                    act.wait_ge(proj, n + 1)
                    dst = (kT, vT)[n % 2]
                    nc.scalar.activation(dst[:, n // 2, :], banks[n % 8][:, 0:CTX], ACT.Copy).then_inc(kept, 1)
                keys = keyT[:, :].rearrange("p (b h k) -> p b h k", b=BATCH, h=HEADS)
                values = valueT[:, :, :].rearrange("p b (h k) -> p b h k", h=HEADS)
                for n in range(2 * HEADS):
                    act.wait_ge(folded, n + 1)
                    dst = (keys, values)[n % 2]
                    nc.scalar.activation(dst[:, :, n // 2, :], banks[n % 8][:, 0:CTX].rearrange("p (b k) -> p b k", b=BATCH),
                                         ACT.Copy).then_inc(folded_kept, 1)
                for g in range(BATCH * KEY_CHUNKS // 4):
                    act.wait_ge(turned, g + 1)
                    keep_chunks(nc, value, banks[g % 8], g).then_inc(kept, 1)

        with ExitStack() as stack:
            m = Memory(nc, stack, "a0t")
            queries = m.sb("queries", [P, 1, SEQ])
            pieces = [(bank, 0, KEYS * heads, 0, KEYS * first) for bank, (first, heads) in enumerate(BANK_HEADS)]

            def query_pe(pe, b, out_bank, out_added, query_psum):
                pass

            def query_act(act, b, turned, out_bank, query_psum, query_ready):
                act.wait_ge(turned, b * PER_BATCH + 2)
                nc.scalar.activation(queries[:, 0, :], xnT[:, bass.ds(b * SEQ, SEQ)], ACT.Copy).then_inc(query_ready, 1)

            attention(nc, m, stack, x, xnT, ident, keyT, value, 64 ** -0.5, pieces, queries, 1, query_pe, query_act)


def keep_chunks(nc, value, bank, g):
    last = None
    for i in range(4):
        n = 4 * g + i
        rows = LAST_KEYS if n % KEY_CHUNKS == KEY_CHUNKS - 1 else P
        last = nc.scalar.activation(value[0:rows, D * n:D * n + D], bank[0:rows, P * i:P * i + P], ACT.Copy)
    return last


def feature_attention(nc, io, x, xnT, ident, ctxT):
    CH = 2
    with ExitStack() as keep:
        mk = Memory(nc, keep, "a1")
        keyT = mk.sb("keyT", [P, BATCH * ALL_KEYS])
        value = mk.sb("value", [P, BATCH * KEY_CHUNKS * D])
        spread = mk.sb("spread", [P, CH * P])
        signed_bias = mk.sb("signed_bias", [P, 1])
        with ExitStack() as stack:
            m = Memory(nc, stack, "a1s")
            fm, fb, fcT = m.sb("fm", [P, 8]), m.sb("fb", [P, 1]), m.sb("fcT", [P, CH, D])
            fcb = m.sb("fcb", [P, D])
            by16, by8, sign = m.sb("by16", [P, 8]), m.sb("by8", [P, 16]), m.sb("sign", [P, 1])
            minus_fm = m.sb("minus_fm", [P, 8])
            features = m.sb("features", [P, CH, CTX])
            valueT = m.sb("valueT", [P, BATCH, ALL_KEYS])
            banks = [m.bank(f"b{i}") for i in range(8)]
            loaded, chain, spread_ready, z_ready, features_ready, keys_ready, folded, folded_kept, turned, kept = (
                m.sem(n) for n in ("loaded", "chain", "spread_ready", "z_ready", "features_ready", "keys_ready", "folded", "folded_kept", "turned", "kept"))
            block = stack.enter_context(nc.Block())

            @block.sync
            def _(sp):
                for dst, src in ((fm, "fm"), (fb, "fb"), (fcT, "fcT"), (fcb, "fcb"), (by16, "by16"), (by8, "by8"), (sign, "sign")):
                    sp.dma_start(dst[:], io[src]).then_inc(loaded, 16)

            @block.vector
            def _(dve):
                c = Chain(dve, chain)
                dve.wait_ge(loaded, 7 * 16)
                c.link(nc.vector.tensor_scalar(minus_fm[:, :], fm[:, :], -1.0, None, ALU.mult))
                s4 = spread[:, :].rearrange("p (h s e) -> p h s e", h=HEADS, s=2)
                for s, w in enumerate((fm, minus_fm)):
                    last = nc.vector.tensor_tensor(s4[:, :, s, :], w[:, :].unsqueeze(1).broadcast_to([P, HEADS, 8]),
                                                   by8[:, :].unsqueeze(2).broadcast_to([P, HEADS, 8]), ALU.mult)
                c.link(last)
                nc.vector.tensor_tensor(signed_bias[:, :], fb[:, :], sign[:, :], ALU.mult).then_inc(spread_ready, 1)
                nc.vector.tensor_tensor(x[:, :, :], x[:, :, :], fcb[:, :].unsqueeze(1).broadcast_to([P, TILES, D]), ALU.add)
                dve.wait_ge(features_ready, CH)
                k4 = keyT[:, :].rearrange("p (b h k) -> p b h k", b=BATCH, h=HEADS)
                f4 = features[:, :, :].rearrange("p c (b k) -> p c b k", b=BATCH)
                for b in range(BATCH):
                    for ch in range(CH):
                        last = nc.vector.tensor_tensor(k4[:, b, 8 * ch:8 * ch + 8, :],
                                                       f4[:, ch, b, :].unsqueeze(1).broadcast_to([P, 8, KEYS]),
                                                       by16[:, :].unsqueeze(2).broadcast_to([P, 8, KEYS]), ALU.mult)
                    last.then_inc(keys_ready, 1)

            @block.tensor
            def _(pe):
                pe.wait_ge(spread_ready, 1)
                for ch in range(CH):
                    nc.tensor.matmul(banks[ch][:, 0:CTX], spread[:, P * ch:P * ch + P], ctxT[:, :], start=True, stop=True).then_inc(z_ready, 1)
                n = 0
                half = 4 * KEYS
                for b in range(BATCH):
                    pe.wait_ge(keys_ready, b + 1)
                    for i in range(4):
                        if n >= 6:
                            pe.wait_ge(folded_kept, n - 5)
                        nc.tensor.matmul(banks[2 + n % 6][:, 0:half], fcT[:, i // 2, :], keyT[:, b * ALL_KEYS + half * i:b * ALL_KEYS + half * i + half],
                                         start=True, stop=True).then_inc(folded, 1)
                        n += 1
                pe.wait_ge(folded_kept, n)
                for b in range(BATCH):
                    for c in range(KEY_CHUNKS):
                        n = b * KEY_CHUNKS + c
                        rows = LAST_KEYS if c == KEY_CHUNKS - 1 else P
                        if n >= 32 and n % 4 == 0:
                            pe.wait_ge(kept, n // 4 - 7)
                        i = nc.tensor.transpose(banks[n // 4 % 8][0:rows, P * (n % 4):P * (n % 4) + P],
                                                valueT[:, b, P * c:P * c + rows], ident[:, :])
                        if n % 4 == 3:
                            i.then_inc(turned, 1)

            @block.scalar
            def _(act):
                for ch in range(CH):
                    act.wait_ge(z_ready, ch + 1)
                    nc.scalar.activation(features[:, ch, :], banks[ch][:, 0:CTX], ACT.Exp, bias=signed_bias[:, 0:1]).then_inc(features_ready, 1)
                for n in range(16):
                    act.wait_ge(folded, n + 1)
                    nc.scalar.activation(valueT[:, n // 4, 4 * KEYS * (n % 4):4 * KEYS * (n % 4) + 4 * KEYS], banks[2 + n % 6][:, 0:4 * KEYS],
                                         ACT.Copy).then_inc(folded_kept, 1)
                for g in range(BATCH * KEY_CHUNKS // 4):
                    act.wait_ge(turned, g + 1)
                    keep_chunks(nc, value, banks[g % 8], g).then_inc(kept, 1)

        with ExitStack() as stack:
            m = Memory(nc, stack, "a1t")
            queries = m.sb("queries", [P, CH, SEQ])
            pieces = [(0, 0, 6 * KEYS, 0, 0), (1, 0, 2 * KEYS, 0, 6 * KEYS), (1, 2 * KEYS, 3 * KEYS, 1, 8 * KEYS), (2, 0, 5 * KEYS, 1, 11 * KEYS)]

            def query_pe(pe, b, out_bank, out_added, query_psum):
                pe.wait_ge(out_added, b * PER_BATCH + 2)
                for ch in range(CH):
                    last = nc.tensor.matmul(out_bank[ch][:, :], spread[:, P * ch:P * ch + P], xnT[:, bass.ds(b * SEQ, SEQ)], start=True, stop=True)
                last.then_inc(query_psum, 1)

            def query_act(act, b, turned, out_bank, query_psum, query_ready):
                act.wait_ge(query_psum, b + 1)
                for ch in range(CH):
                    last = nc.scalar.activation(queries[:, ch, :], out_bank[ch][:, :], ACT.Exp, bias=signed_bias[:, 0:1])
                last.then_inc(query_ready, 1)

            attention(nc, m, stack, x, xnT, ident, keyT, value, float(D) ** -0.5, pieces, queries, CH, query_pe, query_act)


def product_key_ffn(nc, io, x, xnT, ident):
    with ExitStack() as keep:
        mk = Memory(nc, keep, "f0")
        sim_w = mk.sb("sim_w", [P, 2, SIM_HEADS * SUBKEYS])
        downT, up = mk.sb("downT", [P, EXPERTS]), mk.sb("up", [P, E_CHUNKS, D])
        wgT, wuT, wdT = mk.sb("wgT", [P, INTER]), mk.sb("wuT", [P, INTER]), mk.sb("wdT", [P, INTER // P, D])
        loaded = mk.sem("loaded")
        with ExitStack() as stack:
            m = Memory(nc, stack, "f0s")
            wq, keysT = m.sb("wq", [P, SIM_HEADS, D]), m.sb("keysT", [P, SIM_HEADS, SUBKEYS])
            banks = [m.bank(f"b{i}") for i in range(2)]
            keys_loaded, folded = m.sem("keys_loaded"), m.sem("folded")
            block = stack.enter_context(nc.Block())

            @block.sync
            def _(sp):
                sp.dma_start(wq[:, :, :], io["ffn_wq"]).then_inc(keys_loaded, 16)
                sp.dma_start(keysT[:, :, :], io["keysT"]).then_inc(keys_loaded, 16)
                for dst, src in ((wgT, "wgT"), (wuT, "wuT"), (wdT, "wdT"), (downT, "downT"), (up, "up")):
                    sp.dma_start(dst[:], io[src]).then_inc(loaded, 16)

            @block.tensor
            def _(pe):
                pe.wait_ge(keys_loaded, 32)
                for p in range(2):
                    rows = slice(64 * p, 64 * p + 64)
                    for h in range(SIM_HEADS):
                        last = nc.tensor.matmul(banks[p][:, SUBKEYS * h:SUBKEYS * h + SUBKEYS], wq[rows, h, :], keysT[rows, h, :], start=True, stop=True)
                    last.then_inc(folded, 1)

            @block.scalar
            def _(act):
                for p in range(2):
                    act.wait_ge(folded, p + 1)
                    nc.scalar.activation(sim_w[:, p, :], banks[p][:, :], ACT.Copy)

        with ExitStack() as stack:
            m = Memory(nc, stack, "f0t")
            tokens = m.sb("tokens", [P, SEQ])
            gate = m.sb("gate", [P, 2, SEQ])
            hidden = m.sb("hidden", [P, INTER // P, SEQ])
            act_w = m.sb("act_w", [P, E_CHUNKS, SEQ])
            side_top = m.sb("side_top", [P, 2 * SIM_HEADS])
            shifted = m.sb("shifted", [P, 2 * SIM_HEADS, SUBKEYS])
            ex = m.sb("ex", [P, 2, 2 * SIM_HEADS, SUBKEYS])
            top8 = m.sb("top8", [P, 3, SIM_HEADS, TOPK])
            pairs = m.sb("pairs", [P, SIM_HEADS, TOPK * TOPK])
            clip_pairs = m.sb("clip_pairs", [P, SIM_HEADS, TOPK * TOPK])
            picked = m.sb("picked", [P, SIM_HEADS, TOPK])
            total, inverse, clipped, clipped_w = (m.sb(n, [P, SIM_HEADS]) for n in ("total", "inverse", "clipped", "clipped_w"))
            clipped_sum = m.sb("clipped_sum", [P, 1])
            carrier = m.sb("carrier", [P, 1])
            prod = m.sb("prod", [P, 2, EXPERTS])
            weight = m.sb("weight", [P, EXPERTS])
            mixed = m.sb("mixed", [P, E_CHUNKS, P])
            sim_bank = [m.bank(f"sim{i}") for i in range(2)]
            wide_bank = [m.bank(f"wide{i}") for i in range(4)]
            out_bank = [m.bank(f"out{i}") for i in range(2)]
            tokens_ready, mlp_g, mlp_silu, mlp_u, mlp_h, w_ready, act_w_ready = (
                m.sem(n) for n in ("tokens_ready", "mlp_g", "mlp_silu", "mlp_u", "mlp_h", "w_ready", "act_w_ready"))
            sims_ready, shifted_ready, ex_ready, prod_ready, prod_used, weight_ready = (
                m.sem(n) for n in ("sims_ready", "shifted_ready", "ex_ready", "prod_ready", "prod_used", "weight_ready"))
            turned, mixed_ready, out_ready, out_added, chain = (m.sem(n) for n in ("turned", "mixed_ready", "out_ready", "out_added", "chain"))
            T = PER_BATCH
            LINKS = 12 * T
            block = stack.enter_context(nc.Block())

            @block.tensor
            def _(pe):
                pe.wait_ge(loaded, 5 * 16)
                with pe.Fori(0, TILES // T) as b:
                    group = xnT[:, bass.ds(b * SEQ, SEQ)]
                    for c in range(4):
                        if c >= 2:
                            pe.wait_ge(mlp_silu, b * 4 + (c - 1))
                        else:
                            pe.wait_ge(mixed_ready, b * 4 * T + 1)
                        nc.tensor.matmul(wide_bank[c % 2][:, :], wgT[:, P * c:P * c + P], group, start=True, stop=True).then_inc(mlp_g, 1)
                        if c >= 2:
                            pe.wait_ge(mlp_h, b * 4 + (c - 1))
                        nc.tensor.matmul(wide_bank[2 + c % 2][:, :], wuT[:, P * c:P * c + P], group, start=True, stop=True).then_inc(mlp_u, 1)
                    for e in range(E_CHUNKS):
                        if e < 4:
                            (pe.wait_ge(mlp_silu, b * 4 + (3 + e)) if e < 2 else pe.wait_ge(mlp_h, b * 4 + (1 + e)))
                        else:
                            pe.wait_ge(act_w_ready, b * E_CHUNKS + (e - 3))
                        nc.tensor.matmul(wide_bank[e % 4][:, :], downT[:, P * e:P * e + P], group, start=True, stop=True).then_inc(w_ready, 1)
                    pe.wait_ge(tokens_ready, b + 1)

                    def sims(j):
                        pe.wait_ge(shifted_ready, b * T + (j + 1))
                        for p in range(2):
                            last = nc.tensor.matmul(sim_bank[p][:, :], tokens[:, P * j:P * j + P], sim_w[:, p, :], start=True, stop=True)
                        last.then_inc(sims_ready, 1)

                    def turn(j):
                        pe.wait_ge(weight_ready, b * T + (j + 1))
                        for g in range(4):
                            if j == 0 and g == 0:
                                pe.wait_ge(act_w_ready, b * E_CHUNKS + E_CHUNKS)
                            elif 4 * j + g >= 4:
                                pe.wait_ge(mixed_ready, b * 4 * T + (4 * j + g - 4 + 2))
                            for i in range(4):
                                e = 4 * g + i
                                last = nc.tensor.transpose(wide_bank[g][:, P * i:P * i + P], weight[:, P * e:P * e + P], ident[:, :])
                            last.then_inc(turned, 1)

                    def out(j):
                        pe.wait_ge(out_added, b * T + (j + 1))
                        for c in range(4):
                            nc.tensor.matmul(out_bank[j % 2][:, 0:D], hidden[:, c, P * j:P * j + P], wdT[:, c, :], start=(c == 0), stop=False)
                        for g in range(4):
                            pe.wait_ge(mixed_ready, b * 4 * T + (4 * j + g + 2))
                            for i in range(4):
                                e = 4 * g + i
                                last = nc.tensor.matmul(out_bank[j % 2][:, 0:D], mixed[:, e, :], up[:, e, :], start=False, stop=(e == E_CHUNKS - 1))
                        last.then_inc(out_ready, 1)

                    sims(0)
                    for j in range(T):
                        if j + 1 < T:
                            sims(j + 1)
                        if j > 0:
                            out(j - 1)
                        turn(j)
                    out(T - 1)

            @block.scalar
            def _(act):
                with act.Fori(0, TILES // T) as b:
                    act.wait_ge(out_added, b * T + 2)
                    nc.scalar.activation(tokens[:, :], xnT[:, bass.ds(b * SEQ, SEQ)], ACT.Copy).then_inc(tokens_ready, 1)
                    for c in range(4):
                        act.wait_ge(mlp_g, b * 4 + (c + 1))
                        if c >= 2:
                            act.wait_ge(mlp_h, b * 4 + (c - 1))
                        nc.scalar.activation(gate[:, c % 2, :], wide_bank[c % 2][:, :], ACT.Silu).then_inc(mlp_silu, 1)
                    for e in range(E_CHUNKS):
                        act.wait_ge(w_ready, b * E_CHUNKS + (e + 1))
                        nc.scalar.activation(act_w[:, e, :], wide_bank[e % 4][:, :], ACT.Silu).then_inc(act_w_ready, 1)

                    def exponentials(j):
                        act.wait_ge(shifted_ready, b * T + (j + 2))
                        nc.scalar.activation(ex[:, j % 2, :, :], shifted[:, :, :], ACT.Exp).then_inc(ex_ready, 1)

                    exponentials(0)
                    for j in range(T):
                        for h in range(SIM_HEADS):
                            n = SIM_HEADS * j + h
                            act.wait_ge(prod_used, b * SIM_HEADS * T + (n + 1))
                            act.wait_ge(ex_ready, b * T + (j + 1))
                            for a in range(ROWS):
                                last = nc.scalar.activation(prod[:, h % 2, SUBKEYS * a:SUBKEYS * a + SUBKEYS], ex[:, j % 2, SIM_HEADS + h, :], ACT.Copy,
                                                            scale=ex[:, j % 2, h, a:a + 1])
                            last.then_inc(prod_ready, 1)
                            if h == 0 and j + 1 < T:
                                exponentials(j + 1)

            @block.vector
            def _(dve):
                dve.sem_inc(shifted_ready, 1)
                dve.sem_inc(mixed_ready, 1)
                dve.sem_inc(out_added, 2)
                dve.sem_inc(prod_used, 2)
                with dve.Fori(0, TILES // T) as b:
                    k = Chain(dve, chain, b * LINKS)
                    for c in range(4):
                        dve.wait_ge(mlp_silu, b * 4 + (c + 1))
                        dve.wait_ge(mlp_u, b * 4 + (c + 1))
                        nc.vector.tensor_tensor(hidden[:, c, :], gate[:, c % 2, :], wide_bank[2 + c % 2][:, :], ALU.mult).then_inc(mlp_h, 1)

                    def shift(j):
                        dve.wait_ge(sims_ready, b * T + (j + 1))
                        for p in range(2):
                            last = nc.vector.tensor_reduce(side_top[:, SIM_HEADS * p:SIM_HEADS * p + SIM_HEADS],
                                                           sim_bank[p][:, :].rearrange("p (h k) -> p h k", k=SUBKEYS), AX, ALU.max)
                        k.link(last)
                        dve.wait_ge(ex_ready, b * T + j) if j > 0 else None
                        for p in range(2):
                            hs = slice(SIM_HEADS * p, SIM_HEADS * p + SIM_HEADS)
                            last = nc.vector.tensor_tensor(shifted[:, hs, :], sim_bank[p][:, :].rearrange("p (h k) -> p h k", k=SUBKEYS),
                                                           side_top[:, hs].unsqueeze(2).broadcast_to([P, SIM_HEADS, SUBKEYS]), ALU.subtract)
                        last.then_inc(shifted_ready, 1)

                    def before_max():
                        nc.vector.memset(carrier[:, :], 0.0)

                    def select(j):
                        dve.wait_ge(ex_ready, b * T + (j + 1))
                        before_max()
                        for h in range(SIM_HEADS):
                            nc.vector.max(top8[:, 0, h, :], ex[:, j % 2, h, :])
                            nc.vector.max(top8[:, 1, h, :], ex[:, j % 2, SIM_HEADS + h, :])
                            last = nc.vector.max(top8[:, 2, h, :], ex[:, j % 2, h, ROWS:SUBKEYS])
                        k.link(last)
                        shape = [P, SIM_HEADS, TOPK, TOPK]
                        second = top8[:, 1, :, :].unsqueeze(2).broadcast_to(shape)
                        for side, dst in ((0, pairs), (2, clip_pairs)):
                            last = nc.vector.tensor_tensor(dst[:, :, :].rearrange("p h (i j) -> p h i j", i=TOPK),
                                                           top8[:, side, :, :].unsqueeze(3).broadcast_to(shape), second, ALU.mult)
                        k.link(last)
                        before_max()
                        for h in range(SIM_HEADS):
                            last = nc.vector.max(picked[:, h, :], pairs[:, h, :])
                        k.link(last)
                        nc.vector.tensor_reduce(total[:, :], picked[:, :, :], AX, ALU.add)
                        for h in range(SIM_HEADS):
                            last = nc.vector.scalar_tensor_tensor(clip_pairs[:, h, :], clip_pairs[:, h, :], picked[:, h, TOPK - 1:TOPK], clip_pairs[:, h, :],
                                                                  op0=ALU.is_ge, op1=ALU.mult)
                        k.link(last)
                        nc.vector.tensor_reduce(clipped[:, :], clip_pairs[:, :, :], AX, ALU.add)
                        k.link(nc.vector.reciprocal(inverse[:, :], total[:, :]))
                        k.link(nc.vector.tensor_tensor(clipped_w[:, :], clipped[:, :], inverse[:, :], ALU.mult))
                        k.link(nc.vector.tensor_reduce(clipped_sum[:, :], clipped_w[:, :], AX, ALU.add))

                    def mix(j):
                        for g in range(4):
                            dve.wait_ge(turned, b * 4 * T + (4 * j + g + 1))
                            if g == 0:
                                dve.wait_ge(out_ready, b * T + j) if j > 0 else None
                            es = slice(4 * g, 4 * g + 4)
                            nc.vector.tensor_tensor(mixed[:, es, :], act_w[:, es, P * j:P * j + P],
                                                    wide_bank[g][:, :].rearrange("p (e t) -> p e t", t=P), ALU.mult).then_inc(mixed_ready, 1)

                    def weigh(j):
                        for h in range(SIM_HEADS):
                            dve.wait_ge(prod_ready, b * SIM_HEADS * T + (SIM_HEADS * j + h + 1))
                            p = prod[:, h % 2, :]
                            k.link(nc.vector.scalar_tensor_tensor(p, p, picked[:, h, TOPK - 1:TOPK], p, op0=ALU.is_ge, op1=ALU.mult))
                            if h == 0:
                                step = nc.vector.tensor_scalar(weight[:, :], p, inverse[:, h:h + 1], None, ALU.mult)
                            else:
                                step = nc.vector.scalar_tensor_tensor(weight[:, :], p, inverse[:, h:h + 1], weight[:, :], op0=ALU.mult, op1=ALU.add)
                            step.then_inc(prod_used, 1)
                            dve.wait_ge(prod_used, b * SIM_HEADS * T + (SIM_HEADS * j + h + 3))
                        last = weight[:, EXPERTS - 1:EXPERTS]
                        nc.vector.tensor_tensor(last, last, clipped_sum[:, :], ALU.add).then_inc(weight_ready, 1)

                    def add(j):
                        dve.wait_ge(out_ready, b * T + (j + 1))
                        row = x[:, bass.ds(b * T + j, 1), :].rearrange("p o d -> p (o d)")
                        nc.vector.tensor_tensor(row, row, out_bank[j % 2][:, 0:D], ALU.add).then_inc(out_added, 1)

                    shift(0)
                    for j in range(T):
                        select(j)
                        if j + 1 < T:
                            shift(j + 1)
                        if j > 0:
                            mix(j - 1)
                        weigh(j)
                        if j > 0:
                            add(j - 1)
                    mix(T - 1)
                    add(T - 1)
                    assert k.n == LINKS


def expert_ffn(nc, io, x, xnT, ident, out):
    with ExitStack() as keep:
        mk = Memory(nc, keep, "f1")
        combT = mk.sb("combT", [P, TOKENS], F32R)
        gate_w, bias = mk.sb("gate_w", [P, MOE_E]), mk.sb("bias", [P, MOE_E])
        half_id = mk.sb("half_id", [P, MOE_E])
        with ExitStack() as stack:
            m = Memory(nc, stack, "f1g")
            wide = [P, TILES, MOE_E]
            score, biased, masked, sel = (m.sb(n, wide) for n in ("score", "biased", "masked", "sel"))
            hi_lo = m.sb("hi_lo", [P, TILES, 2, MOE_E], F32R)
            tour = [m.sb(f"tour{i}", [P, TILES, GROUPS, 4]) for i in range(6)]
            group_score, group_top, mask = (m.sb(n, [P, TILES, GROUPS]) for n in ("group_score", "group_top", "mask"))
            picked = m.sb("picked", [P, TILES, 8])
            total, inverse = m.sb("total", [P, TILES]), m.sb("inverse", [P, TILES])
            logit_bank = [m.bank(f"logit{i}") for i in range(2)]
            turn_bank = [m.bank(f"turn{i}") for i in range(4)]
            loaded, chain, logits_ready, exp_ready, comb_ready, turned = (m.sem(n) for n in ("loaded", "chain", "logits_ready", "exp_ready", "comb_ready", "turned"))
            block = stack.enter_context(nc.Block())

            @block.sync
            def _(sp):
                for dst, src in ((gate_w, "gate_w"), (bias, "bias"), (half_id, "half_id")):
                    sp.dma_start(dst[:], io[src]).then_inc(loaded, 16)

            @block.tensor
            def _(pe):
                pe.wait_ge(loaded, 48)
                for t in range(TILES):
                    i = nc.tensor.matmul(logit_bank[t // 8][:, MOE_E * (t % 8):MOE_E * (t % 8) + MOE_E], xnT[:, P * t:P * t + P], gate_w[:, :], start=True, stop=True)
                i.then_inc(logits_ready, 1)
                pe.wait_ge(comb_ready, 1)
                for t in range(TILES):
                    i = nc.tensor.transpose(turn_bank[t // 4][:, P * (t % 4):P * (t % 4) + P],
                                            hi_lo[:, t, :, :].rearrange("p s e -> p (s e)").bitcast(F32), ident[:, :])
                i.then_inc(turned, 1)

            @block.scalar
            def _(act):
                act.wait_ge(logits_ready, 1)
                for i in range(2):
                    last = nc.scalar.activation(score[:, 8 * i:8 * i + 8, :], logit_bank[i][:, :].rearrange("p (t e) -> p t e", e=MOE_E), ACT.Exp, scale=-1.0)
                last.then_inc(exp_ready, 1)
                act.wait_ge(turned, 1)
                for i in range(4):
                    nc.scalar.activation(combT[:, 512 * i:512 * i + 512], turn_bank[i][:, :], ACT.Copy)

            @block.vector
            def _(dve):
                k = Chain(dve, chain)
                tt, ts = nc.vector.tensor_tensor, nc.vector.tensor_scalar
                dve.wait_ge(loaded, 48)
                dve.wait_ge(exp_ready, 1)
                k.link(ts(score[:, :, :], score[:, :, :], 1.0, None, ALU.add))
                k.link(nc.vector.reciprocal(score[:, :, :], score[:, :, :]))
                k.link(tt(biased[:, :, :], score[:, :, :], bias[:, :].unsqueeze(1).broadcast_to(wide), ALU.add))
                b4 = biased[:, :, :].rearrange("p t (g e) -> p t g e", e=GROUP_E)
                flat = [t[:, :, :, :].rearrange("p t g e -> p (t g) e") for t in tour]
                b3 = b4.rearrange("p t g e -> p (t g) e")
                best, next_, low, keep_best, keep_next = flat[0], flat[1], flat[2], flat[3], flat[4]
                tt(best, b3[:, :, 0:4], b3[:, :, 4:8], ALU.max)
                k.link(tt(next_, b3[:, :, 0:4], b3[:, :, 4:8], ALU.min))
                for n in (2, 1):
                    a, c = slice(0, n), slice(n, 2 * n)
                    tt(low[:, :, a], best[:, :, a], best[:, :, c], ALU.min)
                    tt(keep_best[:, :, a], best[:, :, a], best[:, :, c], ALU.max)
                    k.link(tt(keep_next[:, :, a], next_[:, :, a], next_[:, :, c], ALU.max))
                    k.link(tt(next_[:, :, a], low[:, :, a], keep_next[:, :, a], ALU.max))
                    best, keep_best = keep_best, best
                k.link(tt(group_score[:, :, :].rearrange("p t g -> p (t g)").unsqueeze(2), best[:, :, 0:1], next_[:, :, 0:1], ALU.add))
                for t in range(TILES):
                    last = nc.vector.max(group_top[:, t, :], group_score[:, t, :])
                k.link(last)
                k.link(tt(mask[:, :, :], group_score[:, :, :], group_top[:, :, TOP_GROUPS - 1:TOP_GROUPS].broadcast_to([P, TILES, GROUPS]), ALU.is_ge))
                k.link(ts(mask[:, :, :], mask[:, :, :], 1.0, BIG, ALU.subtract, ALU.mult))
                k.link(tt(masked[:, :, :].rearrange("p t (g e) -> p (t g) e", e=GROUP_E), b3,
                          mask[:, :, :].rearrange("p t g -> p (t g)").unsqueeze(2).broadcast_to([P, TILES * GROUPS, GROUP_E]), ALU.add))
                for t in range(TILES):
                    last = nc.vector.max(picked[:, t, :], masked[:, t, :])
                k.link(last)
                k.link(tt(sel[:, :, :], masked[:, :, :], picked[:, :, 7:8].broadcast_to(wide), ALU.is_ge))
                k.link(tt(sel[:, :, :], sel[:, :, :], score[:, :, :], ALU.mult))
                k.link(nc.vector.tensor_reduce(total[:, :], sel[:, :, :], AX, ALU.add))
                k.link(ts(total[:, :], total[:, :], 1e-20, None, ALU.add))
                k.link(nc.vector.reciprocal(inverse[:, :], total[:, :]))
                k.link(ts(inverse[:, :], inverse[:, :], TW_SCALE, None, ALU.mult))
                k.link(tt(sel[:, :, :], sel[:, :, :], inverse[:, :].unsqueeze(2).broadcast_to(wide), ALU.mult))
                k.link(nc.vector.tensor_copy(hi_lo[:, :, 0, :], sel[:, :, :]))
                tt(hi_lo[:, :, 1, :], sel[:, :, :], hi_lo[:, :, 0, :].bitcast(F32), ALU.subtract).then_inc(comb_ready, 1)

        with ExitStack() as stack:
            m = Memory(nc, stack, "f1e")
            W = 3 * P
            NG = TOKENS // 512
            slot = m.sb("slot", [P, 2, W])
            shared = m.sb("shared", [P, W])
            spread = m.sb("spread", [P, 2, 2, MOE_F], F32R)
            gate = m.sb("gate", [P, 2, 512])
            gu = m.sb("gu", [P, 2, 512])
            hid = m.sb("hid", [P, 2, 512])
            yT = m.sb("yT", [P, TOKENS])
            g_bank, u_bank, c_bank = m.bank("g"), m.bank("u"), m.bank("c")
            y_bank = [m.bank(f"y{i}") for i in range(NG)]
            t_bank = m.bank("t")
            shared_loaded, slot_loaded, slot_used = m.sem("shared_loaded"), [m.sem(f"slot{i}_loaded") for i in range(2)], m.sem("slot_used")
            spread_ready, g_ready, u_ready, c_ready, silu_ready, gu_ready, hid_ready, hid_used = (
                m.sem(n) for n in ("spread_ready", "g_ready", "u_ready", "c_ready", "silu_ready", "gu_ready", "hid_ready", "hid_used"))
            y_kept, turned, added, stored, y_ready = (m.sem(n) for n in ("y_kept", "turned", "added", "stored", "y_ready"))
            block = stack.enter_context(nc.Block())
            F = MOE_F
            STEP = 2 * NG

            @block.sync
            def _(sp):
                sp.dma_start(shared[:, :], io["shared"]).then_inc(shared_loaded, 16)
                with sp.Fori(0, PAIRS // 2) as i:
                    for s in range(2):
                        sp.wait_ge(hid_used, i * STEP + (NG * (s + 1)) - (NG - 1))
                        sp.dma_start(slot[:, s, :], io["pairs"][:, bass.ds((i * 2 + s) * W, W)]).then_inc(slot_loaded[s], 16)
                for g in range(NG):
                    sp.wait_ge(added, g + 1)
                    sp.dma_start(out[:, 4 * g:4 * g + 4, :], x[:, 4 * g:4 * g + 4, :]).then_inc(stored, 16)
                sp.wait_ge(stored, 16 * NG)

            @block.gpsimd
            def _(pool):
                with pool.Fori(0, PAIRS // 2) as i:
                    for s in range(2):
                        pool.wait_ge(hid_used, i * STEP + (NG * (s + 1)) - (NG - 1))
                        nc.gpsimd.tensor_copy(spread[:, s, :, :], half_id[:, bass.ds((i * 2 + s) * 2, 2)].unsqueeze(2).broadcast_to([P, 2, F])).then_inc(spread_ready, 1)

            @block.tensor
            def _(pe):
                pe.wait_ge(shared_loaded, 16)

                def first(w, k, g, n, spread_w):
                    tok = xnT[:, 512 * g:512 * g + 512]
                    pe.wait_ge(silu_ready, n) if n is not None else None
                    nc.tensor.matmul(g_bank[0:k, :], w[:, 0:k], tok, start=True, stop=True).then_inc(g_ready, 1)

                for g in range(NG):
                    tok = xnT[:, 512 * g:512 * g + 512]
                    if g:
                        pe.wait_ge(silu_ready, g)
                    nc.tensor.matmul(g_bank[0:F, :], shared[:, 0:F], tok, start=True, stop=True).then_inc(g_ready, 1)
                    if g:
                        pe.wait_ge(gu_ready, g)
                    nc.tensor.matmul(u_bank[0:F, :], shared[:, F:2 * F], tok, start=True, stop=True).then_inc(u_ready, 1)
                    pe.wait_ge(hid_ready, g + 1)
                    nc.tensor.matmul(y_bank[g][:, :], shared[0:F, 2 * F:2 * F + D], hid[0:F, g % 2, :], start=True, stop=False).then_inc(hid_used, 1)
                with pe.Fori(0, PAIRS // 2) as i:
                    n0 = i * STEP
                    for s in range(2):
                        pe.wait_ge(slot_loaded[s], i * 16 + 16)
                        for g in range(NG):
                            n = NG * s + g
                            tok = xnT[:, 512 * g:512 * g + 512]
                            pe.wait_ge(silu_ready, n0 + (NG + n))
                            nc.tensor.matmul(g_bank[:, :], slot[:, s, 0:P], tok, start=True, stop=True).then_inc(g_ready, 1)
                            pe.wait_ge(gu_ready, n0 + (NG + n))
                            nc.tensor.matmul(u_bank[:, :], slot[:, s, P:2 * P], tok, start=True, stop=True).then_inc(u_ready, 1)
                            if g == 0:
                                pe.wait_ge(spread_ready, i * 2 + (s + 1))
                            pe.wait_ge(hid_ready, n0 + (NG + n))
                            nc.tensor.matmul(c_bank[:, :], spread[:, s, :, :].rearrange("p a f -> p (a f)"), combT[:, 512 * g:512 * g + 512], start=True, stop=True).then_inc(c_ready, 1)
                            if n > 0:
                                ps, pg = (n - 1) // NG, (n - 1) % NG
                                nc.tensor.matmul(y_bank[pg][:, :], slot[:, ps, 2 * P:3 * P], hid[:, (n - 1) % 2, :], start=False, stop=False).then_inc(hid_used, 1)
                    pe.wait_ge(hid_ready, n0 + (NG + STEP))
                    nc.tensor.matmul(y_bank[NG - 1][:, :], slot[:, 1, 2 * P:3 * P], hid[:, (STEP - 1) % 2, :], start=False, stop=False).then_inc(hid_used, 1)
                for g in range(NG):
                    for i in range(4):
                        last = nc.tensor.matmul(y_bank[g][:, P * i:P * i + P], x[:, 4 * g + i, :], ident[:, :], start=False, stop=(i == 3))
                    last.then_inc(y_ready, 1)
                for g in range(NG):
                    pe.wait_ge(y_kept, g + 1)
                    if g:
                        pe.wait_ge(added, g)
                    for i in range(4):
                        t = 4 * g + i
                        last = nc.tensor.transpose(t_bank[:, P * i:P * i + P], yT[:, P * t:P * t + P], ident[:, :])
                    last.then_inc(turned, 1)

            @block.scalar
            def _(act):
                def silu(n, rows, base):
                    act.wait_ge(g_ready, base + (n + 1))
                    nc.scalar.activation(gate[0:rows, n % 2, :], g_bank[0:rows, :], ACT.Silu).then_inc(silu_ready, 1)

                for g in range(NG):
                    if g >= 2:
                        act.wait_ge(gu_ready, g - 1)
                    silu(g, F, 0)
                with act.Fori(0, PAIRS // 2) as i:
                    for n in range(STEP):
                        act.wait_ge(gu_ready, i * STEP + (NG + n - 1))
                        silu(n, P, i * STEP + NG)
                for g in range(NG):
                    act.wait_ge(y_ready, g + 1)
                    nc.scalar.activation(yT[:, 512 * g:512 * g + 512], y_bank[g][:, :], ACT.Copy).then_inc(y_kept, 1)

            @block.vector
            def _(dve):
                for g in range(NG):
                    dve.wait_ge(silu_ready, g + 1)
                    dve.wait_ge(u_ready, g + 1)
                    nc.vector.tensor_tensor(gu[0:F, g % 2, :], gate[0:F, g % 2, :], u_bank[0:F, :], ALU.mult).then_inc(gu_ready, 1)
                    dve.wait_ge(gu_ready, g + 1)
                    if g >= 2:
                        dve.wait_ge(hid_used, g - 1)
                    nc.vector.tensor_copy(hid[0:F, g % 2, :], gu[0:F, g % 2, :]).then_inc(hid_ready, 1)
                with dve.Fori(0, PAIRS // 2) as i:
                    for n in range(STEP):
                        base = i * STEP
                        dve.wait_ge(silu_ready, base + (NG + n + 1))
                        dve.wait_ge(u_ready, base + (NG + n + 1))
                        nc.vector.tensor_tensor(gu[:, n % 2, :], gate[:, n % 2, :], u_bank[:, :], ALU.mult).then_inc(gu_ready, 1)
                        dve.wait_ge(gu_ready, base + (NG + n + 1))
                        dve.wait_ge(c_ready, base + (n + 1))
                        dve.wait_ge(hid_used, base + (NG + n - 1))
                        nc.vector.tensor_tensor(hid[:, n % 2, :], gu[:, n % 2, :], c_bank[:, :], ALU.mult).then_inc(hid_ready, 1)
                for g in range(NG):
                    dve.wait_ge(turned, g + 1)
                    rows = x[:, 4 * g:4 * g + 4, :]
                    nc.vector.tensor_copy(rows, t_bank[:, :].rearrange("p (t d) -> p t d", t=4)).then_inc(added, 1)


def program(nc, io, out, stop=9):
    with ExitStack() as stack:
        m = Memory(nc, stack, "main")
        x = m.sb("x", [P, TILES, D])
        xnT = m.sb("xnT", [P, TOKENS])
        ctxT = m.sb("ctxT", [P, CTX])
        ident = m.sb("ident", [P, P])
        eps = m.sb("eps", [P, 1])
        with ExitStack() as s:
            block_m = Memory(nc, s, "load")
            loaded = block_m.sem("loaded")
            block = s.enter_context(nc.Block())

            @block.sync
            def _(sp):
                for dst, src in ((x, "x"), (ident, "ident"), (ctxT, "ctxT")):
                    sp.dma_start(dst[:], io[src]).then_inc(loaded, 16)
                sp.wait_ge(loaded, 48)

            @block.vector
            def _(dve):
                nc.vector.memset(eps[:, :], EPS)

        layer_norm(nc, "ln0", x, xnT, ident, eps)
        dense_attention(nc, io, x, xnT, ident, ctxT)
        if stop > 1:
            layer_norm(nc, "ln1", x, xnT, ident, eps)
            product_key_ffn(nc, io, x, xnT, ident)
        if stop > 2:
            layer_norm(nc, "ln2", x, xnT, ident, eps)
            feature_attention(nc, io, x, xnT, ident, ctxT)
        if stop > 3:
            layer_norm(nc, "ln3", x, xnT, ident, eps)
            expert_ffn(nc, io, x, xnT, ident, out)
        else:
            with ExitStack() as s:
                stored = Memory(nc, s, "st").sem("stored")
                block = s.enter_context(nc.Block())

                @block.sync
                def _(sp):
                    sp.dma_start(out, x[:, :, :]).then_inc(stored, 16)
                    sp.wait_ge(stored, 16)


def kernel(**inputs):
    import numpy as np
    import concourse.bacc as bacc
    from concourse.bass_utils import run_bass_kernel_spmd as run

    a = {k: np.asarray(v) for k, v in inputs.items()}
    rows = np.arange(P)
    pairs = np.concatenate([
        a["L1_ffn_We_gate"].reshape(PAIRS, 2, D, MOE_F).transpose(2, 0, 1, 3).reshape(D, PAIRS, P),
        a["L1_ffn_We_up"].reshape(PAIRS, 2, D, MOE_F).transpose(2, 0, 1, 3).reshape(D, PAIRS, P),
        a["L1_ffn_We_down"].reshape(PAIRS, P, D).transpose(1, 0, 2)], axis=2)
    shared = np.zeros((P, 3 * P), np.float32)
    shared[:, 0:MOE_F] = a["L1_ffn_Ws_gate"]
    shared[:, MOE_F:2 * MOE_F] = a["L1_ffn_Ws_up"]
    shared[0:MOE_F, 2 * MOE_F:2 * MOE_F + D] = a["L1_ffn_Ws_down"]
    laid = {
        "x": a["x"].reshape(TILES, P, D).transpose(1, 0, 2),
        "ctxT": a["ctx_1024"].reshape(CTX, D).T,
        "WqT": a["L0_xattn_Wq"].T.reshape(8, P, D).transpose(1, 0, 2),
        "Wk": a["L0_xattn_Wk"],
        "Wv": a["L0_xattn_Wv"],
        "Wo": a["L0_xattn_Wo"].reshape(8, P, D).transpose(1, 0, 2),
        "ffn_wq": a["L0_ffn_Wq"].reshape(2, SIM_HEADS, 64, D).transpose(0, 2, 1, 3).reshape(P, SIM_HEADS, D),
        "keysT": a["L0_ffn_keys"].transpose(2, 3, 0, 1).reshape(P, SIM_HEADS, SUBKEYS),
        "downT": a["L0_ffn_down_embed"].T,
        "up": a["L0_ffn_up_embed"].reshape(E_CHUNKS, P, D).transpose(1, 0, 2),
        "wgT": a["L0_ffn_Wg"].T,
        "wuT": a["L0_ffn_Wu"].T,
        "wdT": a["L0_ffn_Wd"].T.reshape(INTER // P, P, D).transpose(1, 0, 2),
        "fm": np.tile(a["L1_xattn_fm_w"].T, (16, 1)),
        "fb": np.tile(a["L1_xattn_fm_b"], 16).reshape(P, 1),
        "fcT": a["L1_xattn_fc_w"].T.reshape(2, P, D).transpose(1, 0, 2),
        "fcb": np.tile(a["L1_xattn_fc_b"], (P, 1)),
        "gate_w": a["L1_ffn_gate_w"].T,
        "bias": np.tile(a["L1_ffn_gate_bias"], (P, 1)),
        "pairs": pairs.reshape(D, PAIRS * 3 * P),
        "shared": shared,
        "ident": np.eye(P, dtype=np.float32),
        "by16": (rows[:, None] // 16 == np.arange(8)).astype(np.float32),
        "by8": (rows[:, None] // 8 == np.arange(16)).astype(np.float32),
        "sign": (1.0 - 2.0 * (rows[:, None] // 8 % 2)).astype(np.float32),
        "half_id": (rows[:, None] % MOE_E == np.arange(MOE_E)).astype(np.float32),
    }
    laid = {k: np.ascontiguousarray(v) for k, v in laid.items()}
    nc = bacc.Bacc("TRN2", target_bir_lowering=False, num_devices=1)
    io = {k: nc.dram_tensor(f"in_{k}", v.shape, F32, kind="ExternalInput").ap() for k, v in laid.items()}
    out = nc.dram_tensor("out_x", (P, TILES, D), F32, kind="ExternalOutput").ap()
    program(nc, io, out)
    r = run(nc, [{f"in_{k}": v for k, v in laid.items()}], core_ids=[0])
    got = r.results[0]["out_x"]
    return np.ascontiguousarray(got.transpose(1, 0, 2)).reshape(BATCH, SEQ, D)
```

```python
import concourse.bass as bass
from concourse import mybir
from contextlib import ExitStack
import numpy as np

F32 = mybir.dt.float32
F32R = mybir.dt.float32r
ALU = mybir.AluOpType
ACT = mybir.ActivationFunctionType
AX = mybir.AxisListType.X

P = 128
BATCH, SEQ, D = 4, 512, 128
TOKENS = BATCH * SEQ
TILES = TOKENS // P
PER_BATCH = SEQ // P
KEYS = 77
CTX = BATCH * KEYS
HEADS = 16
ALL_KEYS = HEADS * KEYS
KEY_CHUNKS = (ALL_KEYS + P - 1) // P
PADDED_KEYS = KEY_CHUNKS * P
EPS = 1e-5
BANK_HEADS = ((0, 6), (6, 5), (11, 5))
SIM_HEADS, SUBKEYS, TOPK = 4, 128, 8
EXPERTS = 2048
ROWS = EXPERTS // SUBKEYS
E_CHUNKS = EXPERTS // P
INTER = 512
MOE_E, MOE_F = 64, 64
PAIRS = MOE_E // 2
GROUPS, GROUP_E, TOP_GROUPS = 8, 8, 4
TW_SCALE = 2.5
BIG = 1e30


class Memory:

    def __init__(self, nc, stack, name):
        self.nc, self.stack, self.name = nc, stack, name

    def sb(self, name, shape, dt=F32):
        return self.stack.enter_context(self.nc.sbuf_tensor(f"{self.name}_{name}", list(shape), dt))

    def bank(self, name):
        return self.stack.enter_context(self.nc.psum_tensor(f"{self.name}_{name}", [P, 512], F32))

    def sem(self, name):
        return self.stack.enter_context(self.nc.semaphore(f"{self.name}_{name}"))


class Chain:

    def __init__(self, eng, sem, base=0):
        self.eng, self.sem, self.base, self.n = eng, sem, base, 0

    def link(self, instruction):
        self.n += 1
        instruction.then_inc(self.sem, 1)
        self.eng.wait_ge(self.sem, self.base + self.n)


class Norm:

    def __init__(self, nc, m, x, xnT, ident, eps):
        self.nc, self.x, self.xnT, self.ident, self.eps = nc, x, xnT, ident, eps
        self.xn = m.sb("xn", [P, TILES, D])
        self.stats = m.sb("stats", [P, TILES, 6])
        self.moments = m.sb("moments", [P, TILES, 2])
        self.sd, self.rstd = m.sb("sd", [P, TILES]), m.sb("rstd", [P, TILES])
        self.banks = [m.bank(f"xn_turned{i}") for i in range(2)]
        self.stats_ready, self.moments_ready, self.sd_ready, self.rstd_ready, self.xn_ready, self.turned, self.kept = (
            m.sem(n) for n in ("stats_ready", "moments_ready", "sd_ready", "rstd_ready", "xn_ready", "xn_turned", "xn_kept"))

    def vector(self, dve):
        nc = self.nc
        for t in range(TILES):
            last = nc.vector.bn_stats(self.stats[:, t, :], self.x[:, t, :])
        last.then_inc(self.stats_ready, 1)
        dve.wait_ge(self.stats_ready, 1)
        for t in range(TILES):
            last = nc.vector.bn_aggr(self.moments[:, t, :], self.stats[:, t, :])
        last.then_inc(self.moments_ready, 1)
        dve.wait_ge(self.sd_ready, 1)
        nc.vector.reciprocal(self.rstd[:, :], self.sd[:, :]).then_inc(self.rstd_ready, 1)
        dve.wait_ge(self.rstd_ready, 1)
        for t in range(TILES):
            last = nc.vector.tensor_scalar(self.xn[:, t, :], self.x[:, t, :], self.moments[:, t, 0:1], self.rstd[:, t:t + 1], ALU.subtract, ALU.mult)
            if t % 4 == 3:
                last.then_inc(self.xn_ready, 1)

    def scalar_deviation(self, act):
        act.wait_ge(self.moments_ready, 1)
        self.nc.scalar.activation(self.sd[:, :], self.moments[:, :, 1], ACT.Sqrt, bias=self.eps[:, 0:1]).then_inc(self.sd_ready, 1)

    def tensor(self, pe):
        for g in range(4):
            pe.wait_ge(self.xn_ready, g + 1)
            if g >= 2:
                pe.wait_ge(self.kept, g - 1)
            for i in range(4):
                last = self.nc.tensor.transpose(self.banks[g % 2][:, P * i:P * i + P], self.xn[:, 4 * g + i, :], self.ident[:, :])
            last.then_inc(self.turned, 1)

    def scalar_keep(self, act):
        for g in range(4):
            act.wait_ge(self.turned, g + 1)
            self.nc.scalar.activation(self.xnT[:, 512 * g:512 * g + 512], self.banks[g % 2][:, :], ACT.Copy).then_inc(self.kept, 1)


def layer_norm(nc, name, x, xnT, ident, eps):
    with ExitStack() as stack:
        norm = Norm(nc, Memory(nc, stack, name), x, xnT, ident, eps)
        block = stack.enter_context(nc.Block())

        @block.vector
        def _(dve):
            norm.vector(dve)

        @block.scalar
        def _(act):
            norm.scalar_deviation(act)
            norm.scalar_keep(act)

        @block.tensor
        def _(pe):
            norm.tensor(pe)


def attention(nc, m, stack, x, source, ident, keyT, value, scale, pieces):
    CHUNKS = source.shape[1]
    queries = m.sb("queries", [P, CHUNKS, SEQ])
    scores_bank = [[m.bank(f"scores{s}{i}") for i in range(3)] for s in range(2)]
    turn_bank, out_bank = m.bank("turn"), m.bank("out")
    neg_top = m.sb("neg_top", [P, 2, HEADS])
    EXPS = 4
    exps = m.sb("exps", [P, EXPS, PADDED_KEYS])
    sums = m.sb("sums", [P, EXPS, HEADS])
    inverse = m.sb("inverse", [P, 2, HEADS])
    probsT = m.sb("probsT", [P, 2, KEY_CHUNKS, P])
    queries_ready = m.sem("queries_ready")
    CREDIT = 2
    AHEAD = 2
    scores_ready, neg_top_ready, exps_ready, inverse_ready, probs_ready = (
        m.sem(n) for n in ("scores_ready", "neg_top_ready", "exps_ready", "inverse_ready", "probs_ready"))
    ROUNDS = [range(4 * r, min(4 * r + 4, KEY_CHUNKS)) for r in range(3)]
    R = len(ROUNDS)
    turned, kept, out_ready, out_added, padded = (m.sem(n) for n in ("turned", "kept", "out_ready", "out_added", "padded"))
    block = stack.enter_context(nc.Block())

    def tile(b, k):
        return b + k // PER_BATCH, k % PER_BATCH, b * PER_BATCH + k

    def steps(eng, step):
        step(0, 0, True, False)
        with eng.Fori(0, BATCH - 1) as b:
            for k in range(1, PER_BATCH + 1):
                step(b, k, True, True)
        for k in range(1, PER_BATCH):
            step(BATCH - 1, k, k + AHEAD < PER_BATCH, True)

    @block.gpsimd
    def _(pool):
        nc.gpsimd.memset(exps[:, :, ALL_KEYS:PADDED_KEYS], 0.0).then_inc(padded, 1)

    @block.tensor
    def _(pe):
        pe.sem_inc(turned, R * EXPS)
        pe.sem_inc(out_ready, CREDIT)
        pe.wait_ge(padded, 1)

        def scores(b, k):
            batch, j, n = tile(b, k)
            if j == 0:
                pe.wait_ge(queries_ready, batch + 1)
            pe.wait_ge(exps_ready, n + 1)
            for bank, col, cols, q, first in pieces:
                last = nc.tensor.matmul(scores_bank[k % 2][bank][:, col:col + cols], queries[:, q, P * j:P * j + P],
                                        keyT[:, bass.ds(batch * ALL_KEYS + first, cols)], start=True, stop=True)
            last.then_inc(scores_ready, 1)

        def turn(b, k, r):
            batch, j, n = tile(b, k)
            if r == 0:
                pe.wait_ge(probs_ready, n + 1)
            pe.wait_ge(kept, n * R + (r + CREDIT))
            for i, c in enumerate(ROUNDS[r]):
                last = nc.tensor.transpose(turn_bank[:, P * i:P * i + P], exps[:, k % EXPS, P * c:P * c + P], ident[:, :])
            last.then_inc(turned, 1)

        def values(b, k, r):
            batch, j, n = tile(b, k)
            if r == 0:
                pe.wait_ge(kept, n * R + (R + CREDIT))
                pe.wait_ge(out_added, n + 1)
            for c in ROUNDS[r]:
                last = nc.tensor.matmul(out_bank[:, 0:D], probsT[:, k % 2, c, :], value[:, bass.ds((batch * KEY_CHUNKS + c) * D, D)],
                                        start=(c == 0), stop=(c == KEY_CHUNKS - 1))
            if r == R - 1:
                last.then_inc(out_ready, 1)

        def step(b, k, ahead, before):
            if ahead:
                scores(b, k + AHEAD)
            for r in range(R):
                turn(b, k, r)
                if before:
                    values(b, k - 1, r)

        for k in range(AHEAD):
            scores(0, k)
        steps(pe, step)
        for r in range(R):
            values(BATCH - 1, PER_BATCH - 1, r)

    @block.scalar
    def _(act):
        act.sem_inc(exps_ready, CREDIT)

        def fetch(batch):
            for q in range(CHUNKS):
                last = nc.scalar.activation(queries[:, q, :], source[:, q, bass.ds(batch * SEQ, SEQ)], ACT.Copy, scale=scale)
            last.then_inc(queries_ready, 1)

        def exponentials(b, k, more):
            batch, j, n = tile(b, k)
            act.wait_ge(neg_top_ready, n + 1)
            act.wait_ge(turned, n * R + R)
            for bank, (first, heads) in enumerate(BANK_HEADS):
                for i in range(heads):
                    h = first + i
                    last = nc.scalar.activation(exps[:, k % EXPS, KEYS * h:KEYS * h + KEYS],
                                                scores_bank[k % 2][bank][:, KEYS * i:KEYS * i + KEYS], ACT.Exp,
                                                bias=neg_top[:, k % 2, h:h + 1], accum_out=sums[:, k % EXPS, h:h + 1])
                if bank == 0 and j == PER_BATCH - AHEAD and more:
                    act.wait_ge(scores_ready, batch * PER_BATCH + PER_BATCH)
                    fetch(batch + 1)
            last.then_inc(exps_ready, 1)

        def step(b, k, ahead, before):
            exponentials(b, k, not (isinstance(b, int) and b == BATCH - 1))

        fetch(0)
        steps(act, step)

    @block.vector
    def _(dve):
        dve.sem_inc(out_added, 1)
        dve.sem_inc(kept, CREDIT)

        def tops(b, k):
            batch, j, n = tile(b, k)
            dve.wait_ge(scores_ready, n + 1)
            for bank, (first, heads) in enumerate(BANK_HEADS):
                last = nc.vector.tensor_reduce(neg_top[:, k % 2, first:first + heads],
                                               scores_bank[k % 2][bank][:, 0:KEYS * heads].rearrange("p (h k) -> p h k", k=KEYS),
                                               AX, ALU.max, negate=True)
            last.then_inc(neg_top_ready, 1)

        def normalise(b, k):
            batch, j, n = tile(b, k)
            dve.wait_ge(exps_ready, n + 1 + CREDIT)
            nc.vector.reciprocal(inverse[:, k % 2, :], sums[:, k % EXPS, :]).then_inc(inverse_ready, 1)
            dve.wait_ge(inverse_ready, n + 1)
            e = exps[:, k % EXPS, 0:ALL_KEYS].rearrange("p (h k) -> p h k", k=KEYS)
            nc.vector.tensor_tensor(e, e, inverse[:, k % 2, :].unsqueeze(2).broadcast_to([P, HEADS, KEYS]), ALU.mult).then_inc(probs_ready, 1)

        def keep(b, k, r):
            batch, j, n = tile(b, k)
            dve.wait_ge(turned, n * R + (r + 1 + R * EXPS))
            if r == 0:
                dve.wait_ge(out_ready, n + 1)
            chunks = len(ROUNDS[r])
            nc.vector.tensor_copy(probsT[:, k % 2, 4 * r:4 * r + chunks, :],
                                  turn_bank[:, 0:P * chunks].rearrange("p (c t) -> p c t", t=P)).then_inc(kept, 1)

        def add(b, k):
            batch, j, n = tile(b, k)
            dve.wait_ge(out_ready, n + 1 + CREDIT)
            row = x[:, bass.ds(n, 1), :].rearrange("p o d -> p (o d)")
            nc.vector.tensor_tensor(row, row, out_bank[:, 0:D], ALU.add).then_inc(out_added, 1)

        def step(b, k, ahead, before):
            normalise(b, k)
            keep(b, k, 0)
            if ahead:
                tops(b, k + AHEAD)
            for r in range(1, R):
                keep(b, k, r)
            if before:
                add(b, k - 1)

        for k in range(AHEAD):
            tops(0, k)
        steps(dve, step)
        add(BATCH - 1, PER_BATCH - 1)


def dense_setup(nc, mk, io, x, xnT, ident, eps, ctxT, keyT, value):
    with ExitStack() as stack:
        m = Memory(nc, stack, "a0s")
        norm = Norm(nc, m, x, xnT, ident, eps)
        NB = 6
        wqT, wo = m.sb("wqT", [P, 8, D]), m.sb("wo", [P, 8, D])
        wk, wv = m.sb("wk", [P, 1024]), m.sb("wv", [P, 1024])
        kT, vT = m.sb("kT", [P, 8, CTX]), m.sb("vT", [P, 8, CTX])
        valueT = m.sb("valueT", [P, BATCH, PADDED_KEYS])
        banks = [m.bank(f"b{i}") for i in range(NB)]
        x_loaded, kv_loaded, fold_loaded, eps_ready, padded = (m.sem(n) for n in ("x_loaded", "kv_loaded", "fold_loaded", "eps_ready", "padded"))
        proj, k_kept, v_kept, folded, keys_kept, values_kept, turned, turned_kept = (
            m.sem(n) for n in ("proj", "k_kept", "v_kept", "folded", "keys_kept", "values_kept", "turned", "turned_kept"))
        TURNS = BATCH * KEY_CHUNKS // 4
        block = stack.enter_context(nc.Block())

        @block.sync
        def _(sp):
            sp.dma_start(x[:, :, :], io["x"]).then_inc(x_loaded, 16)
            sp.dma_start(wk[:, :], io["Wk"]).then_inc(kv_loaded, 16)
            sp.dma_start(wqT[:, :, :], io["WqT"]).then_inc(fold_loaded, 16)
            sp.dma_start(ident[:, :], io["ident"]).then_inc(fold_loaded, 16)

        @block.gpsimd
        def _(pool):
            nc.gpsimd.memset(eps[:, :], EPS).then_inc(eps_ready, 1)
            nc.gpsimd.memset(valueT[:, :, ALL_KEYS:PADDED_KEYS], 0.0).then_inc(padded, 1)

        @block.tensor
        def _(pe):
            pe.wait_ge(kv_loaded, 48)
            for c in range(8):
                for i, w in enumerate((wk, wv)):
                    n = 2 * c + i
                    if n >= NB:
                        pe.wait_ge((k_kept, v_kept)[i], (n - NB) // 2 + 1)
                    nc.tensor.matmul(banks[n % NB][:, 0:CTX], w[:, P * c:P * c + P], ctxT[:, :], start=True, stop=True).then_inc(proj, 1)
            pe.wait_ge(fold_loaded, 48)
            for h in range(HEADS):
                c, r = h // 2, 64 * (h % 2)
                for i, (w, kv) in enumerate(((wqT, kT), (wo, vT))):
                    n = 2 * h + i
                    pe.wait_ge((k_kept, v_kept)[i], max(c + 1, min(8, 7 + h)))
                    if n >= NB:
                        pe.wait_ge((keys_kept, values_kept)[i], (n - NB) // 2 + 1)
                    nc.tensor.matmul(banks[n % NB][:, 0:CTX], w[r:r + 64, c, :], kv[r:r + 64, c, :], start=True, stop=True).then_inc(folded, 1)
            norm.tensor(pe)
            pe.wait_ge(padded, 1)
            pe.wait_ge(values_kept, HEADS)
            pe.wait_ge(keys_kept, HEADS)
            for t in range(TURNS):
                if t >= NB:
                    pe.wait_ge(turned_kept, t - NB + 1)
                for i in range(4):
                    b, c = (4 * t + i) // KEY_CHUNKS, (4 * t + i) % KEY_CHUNKS
                    last = nc.tensor.transpose(banks[t % NB][:, P * i:P * i + P], valueT[:, b, P * c:P * c + P], ident[:, :])
                last.then_inc(turned, 1)

        @block.scalar
        def _(act):
            act.dma_start(ctxT[:, :], io["ctxT"]).then_inc(kv_loaded, 16)
            act.dma_start(wv[:, :], io["Wv"]).then_inc(kv_loaded, 16)
            act.dma_start(wo[:, :, :], io["Wo"]).then_inc(fold_loaded, 16)
            for n in range(0, 16, 2):
                act.wait_ge(proj, n + 1)
                nc.scalar.activation(kT[:, n // 2, :], banks[n % NB][:, 0:CTX], ACT.Copy).then_inc(k_kept, 1)
            act.wait_ge(eps_ready, 1)
            norm.scalar_deviation(act)
            keys = keyT[:, :].rearrange("p (b h k) -> p b h k", b=BATCH, h=HEADS)
            for n in range(0, 2 * HEADS, 2):
                act.wait_ge(folded, n + 1)
                nc.scalar.activation(keys[:, :, n // 2, :], banks[n % NB][:, 0:CTX].rearrange("p (b k) -> p b k", b=BATCH), ACT.Copy).then_inc(keys_kept, 1)
            norm.scalar_keep(act)
            keep_turned(nc, act, value, banks, turned, turned_kept, TURNS)

        @block.vector
        def _(dve):
            for n in range(1, 16, 2):
                dve.wait_ge(proj, n + 1)
                nc.vector.tensor_copy(vT[:, n // 2, :], banks[n % NB][:, 0:CTX]).then_inc(v_kept, 1)
            dve.wait_ge(x_loaded, 16)
            norm.vector(dve)
            values = valueT[:, :, 0:ALL_KEYS].rearrange("p b (h k) -> p b h k", h=HEADS)
            for n in range(1, 2 * HEADS, 2):
                dve.wait_ge(folded, n + 1)
                nc.vector.tensor_copy(values[:, :, n // 2, :], banks[n % NB][:, 0:CTX].rearrange("p (b k) -> p b k", b=BATCH)).then_inc(values_kept, 1)


def keep_turned(nc, act, value, banks, turned, turned_kept, turns):
    for t in range(turns):
        act.wait_ge(turned, t + 1)
        nc.scalar.activation(value[:, 4 * D * t:4 * D * t + 4 * D], banks[t % len(banks)][:, :], ACT.Copy).then_inc(turned_kept, 1)


def dense_attention(nc, io, x, xnT, ident, eps, ctxT):
    with ExitStack() as keep:
        mk = Memory(nc, keep, "a0")
        keyT = mk.sb("keyT", [P, BATCH * ALL_KEYS])
        value = mk.sb("value", [P, BATCH * KEY_CHUNKS * D])
        dense_setup(nc, mk, io, x, xnT, ident, eps, ctxT, keyT, value)
        with ExitStack() as stack:
            m = Memory(nc, stack, "a0t")
            pieces = [(bank, 0, KEYS * heads, 0, KEYS * first) for bank, (first, heads) in enumerate(BANK_HEADS)]
            attention(nc, m, stack, x, xnT[:, :].unsqueeze(1), ident, keyT, value, 64 ** -0.5, pieces)


FEATURE_CHUNKS = 2


def feature_setup(nc, io, x, xnT, ident, eps, ctxT, keyT, value, spread, signed_bias):
    CH = FEATURE_CHUNKS
    with ExitStack() as stack:
        m = Memory(nc, stack, "a1s")
        norm = Norm(nc, m, x, xnT, ident, eps)
        NB = 6
        fm, fb, fcT = m.sb("fm", [P, 8]), m.sb("fb", [P, 1]), m.sb("fcT", [P, CH, D])
        by16, by8, sign = m.sb("by16", [P, 8]), m.sb("by8", [P, 16]), m.sb("sign", [P, 1])
        minus_fm = m.sb("minus_fm", [P, 8])
        features = m.sb("features", [P, CH, CTX])
        valueT = m.sb("valueT", [P, BATCH, PADDED_KEYS])
        banks = [m.bank(f"b{i}") for i in range(NB)]
        loaded, minus_ready, halves_ready, spread_ready, z_ready, features_ready, keys_ready, folded, folded_kept, turned, turned_kept, padded = (
            m.sem(n) for n in ("loaded", "minus_ready", "halves_ready", "spread_ready", "z_ready", "features_ready", "keys_ready", "folded",
                               "folded_kept", "turned", "turned_kept", "padded"))
        TURNS = BATCH * KEY_CHUNKS // 4
        half = 4 * KEYS
        block = stack.enter_context(nc.Block())

        @block.sync
        def _(sp):
            for dst, src in ((fm, "fm"), (fb, "fb"), (fcT, "fcT"), (by16, "by16"), (by8, "by8"), (sign, "sign")):
                sp.dma_start(dst[:], io[src]).then_inc(loaded, 16)

        @block.gpsimd
        def _(pool):
            nc.gpsimd.memset(valueT[:, :, ALL_KEYS:PADDED_KEYS], 0.0).then_inc(padded, 1)

        @block.vector
        def _(dve):
            norm.vector(dve)
            dve.wait_ge(loaded, 6 * 16)
            nc.vector.tensor_scalar(minus_fm[:, :], fm[:, :], -1.0, None, ALU.mult).then_inc(minus_ready, 1)
            dve.wait_ge(minus_ready, 1)
            s4 = spread[:, :].rearrange("p (h s e) -> p h s e", h=HEADS, s=2)
            for s, w in enumerate((fm, minus_fm)):
                nc.vector.tensor_tensor(s4[:, :, s, :], w[:, :].unsqueeze(1).broadcast_to([P, HEADS, 8]),
                                        by8[:, :].unsqueeze(2).broadcast_to([P, HEADS, 8]), ALU.mult)
            nc.vector.tensor_tensor(signed_bias[:, :], fb[:, :], sign[:, :], ALU.mult).then_inc(spread_ready, 1)
            dve.wait_ge(features_ready, CH)
            k4 = keyT[:, :].rearrange("p (b h k) -> p b h k", b=BATCH, h=HEADS)
            f4 = features[:, :, :].rearrange("p c (b k) -> p c b k", b=BATCH)
            for b in range(BATCH):
                for ch in range(CH):
                    last = nc.vector.tensor_tensor(k4[:, b, 8 * ch:8 * ch + 8, :],
                                                   f4[:, ch, b, :].unsqueeze(1).broadcast_to([P, 8, KEYS]),
                                                   by16[:, :].unsqueeze(2).broadcast_to([P, 8, KEYS]), ALU.mult)
                last.then_inc(keys_ready, 1)

        @block.tensor
        def _(pe):
            norm.tensor(pe)
            pe.wait_ge(spread_ready, 1)
            for ch in range(CH):
                nc.tensor.matmul(banks[ch][:, 0:CTX], spread[:, P * ch:P * ch + P], ctxT[:, :], start=True, stop=True).then_inc(z_ready, 1)
            pe.wait_ge(features_ready, CH)
            for n in range(4 * BATCH):
                b, i = n // 4, n % 4
                pe.wait_ge(keys_ready, b + 1)
                if n >= NB:
                    pe.wait_ge(folded_kept, n - NB + 1)
                nc.tensor.matmul(banks[n % NB][:, 0:half], fcT[:, i // 2, :], keyT[:, b * ALL_KEYS + half * i:b * ALL_KEYS + half * i + half],
                                 start=True, stop=True).then_inc(folded, 1)
            pe.wait_ge(folded_kept, 4 * BATCH)
            pe.wait_ge(padded, 1)
            for t in range(TURNS):
                if t >= NB:
                    pe.wait_ge(turned_kept, t - NB + 1)
                for i in range(4):
                    b, c = (4 * t + i) // KEY_CHUNKS, (4 * t + i) % KEY_CHUNKS
                    last = nc.tensor.transpose(banks[t % NB][:, P * i:P * i + P], valueT[:, b, P * c:P * c + P], ident[:, :])
                last.then_inc(turned, 1)

        @block.scalar
        def _(act):
            norm.scalar_deviation(act)
            norm.scalar_keep(act)
            for ch in range(CH):
                act.wait_ge(z_ready, ch + 1)
                nc.scalar.activation(features[:, ch, :], banks[ch][:, 0:CTX], ACT.Exp, bias=signed_bias[:, 0:1]).then_inc(features_ready, 1)
            for n in range(4 * BATCH):
                act.wait_ge(folded, n + 1)
                nc.scalar.activation(valueT[:, n // 4, half * (n % 4):half * (n % 4) + half], banks[n % NB][:, 0:half], ACT.Copy).then_inc(folded_kept, 1)
            keep_turned(nc, act, value, banks, turned, turned_kept, TURNS)


def feature_attention(nc, io, x, xnT, ident, keyT, value, spread, signed_bias):
    CH = FEATURE_CHUNKS
    with ExitStack() as keep:
        mk = Memory(nc, keep, "a1")
        features = mk.sb("features", [P, CH, TOKENS])
        with ExitStack() as stack:
            m = Memory(nc, stack, "a1q")
            fcb = m.sb("fcb", [P, D])
            banks = [m.bank(f"z{i}") for i in range(8)]
            loaded, z_ready = m.sem("loaded"), m.sem("z_ready")
            block = stack.enter_context(nc.Block())

            @block.sync
            def _(sp):
                sp.dma_start(fcb[:, :], io["fcb"]).then_inc(loaded, 16)

            @block.vector
            def _(dve):
                dve.wait_ge(loaded, 16)
                nc.vector.tensor_tensor(x[:, :, :], x[:, :, :], fcb[:, :].unsqueeze(1).broadcast_to([P, TILES, D]), ALU.add)

            @block.tensor
            def _(pe):
                for n in range(8):
                    nc.tensor.matmul(banks[n][:, :], spread[:, P * (n % CH):P * (n % CH) + P], xnT[:, SEQ * (n // CH):SEQ * (n // CH) + SEQ],
                                     start=True, stop=True).then_inc(z_ready, 1)

            @block.scalar
            def _(act):
                for n in range(8):
                    act.wait_ge(z_ready, n + 1)
                    nc.scalar.activation(features[:, n % CH, SEQ * (n // CH):SEQ * (n // CH) + SEQ], banks[n][:, :], ACT.Exp, bias=signed_bias[:, 0:1])

        with ExitStack() as stack:
            m = Memory(nc, stack, "a1t")
            pieces = [(0, 0, 6 * KEYS, 0, 0), (1, 0, 2 * KEYS, 0, 6 * KEYS), (1, 2 * KEYS, 3 * KEYS, 1, 8 * KEYS), (2, 0, 5 * KEYS, 1, 11 * KEYS)]
            attention(nc, m, stack, x, features[:, :, :], ident, keyT, value, float(D) ** -0.5, pieces)


def product_key_ffn(nc, io, x, xnT, ident):
    with ExitStack() as keep:
        mk = Memory(nc, keep, "f0")
        sim_w = mk.sb("sim_w", [P, 2, SIM_HEADS * SUBKEYS])
        downT, up = mk.sb("downT", [P, EXPERTS]), mk.sb("up", [P, E_CHUNKS, D])
        wgT, wuT, wdT = mk.sb("wgT", [P, INTER]), mk.sb("wuT", [P, INTER]), mk.sb("wdT", [P, INTER // P, D])
        loaded = mk.sem("loaded")
        with ExitStack() as stack:
            m = Memory(nc, stack, "f0s")
            wq, keysT = m.sb("wq", [P, SIM_HEADS, D]), m.sb("keysT", [P, SIM_HEADS, SUBKEYS])
            banks = [m.bank(f"b{i}") for i in range(2)]
            keys_loaded, folded = m.sem("keys_loaded"), m.sem("folded")
            block = stack.enter_context(nc.Block())

            @block.sync
            def _(sp):
                sp.dma_start(wq[:, :, :], io["ffn_wq"]).then_inc(keys_loaded, 16)
                sp.dma_start(keysT[:, :, :], io["keysT"]).then_inc(keys_loaded, 16)
                for dst, src in ((wgT, "wgT"), (wuT, "wuT"), (wdT, "wdT"), (downT, "downT"), (up, "up")):
                    sp.dma_start(dst[:], io[src]).then_inc(loaded, 16)

            @block.tensor
            def _(pe):
                pe.wait_ge(keys_loaded, 32)
                for p in range(2):
                    rows = slice(64 * p, 64 * p + 64)
                    for h in range(SIM_HEADS):
                        last = nc.tensor.matmul(banks[p][:, SUBKEYS * h:SUBKEYS * h + SUBKEYS], wq[rows, h, :], keysT[rows, h, :], start=True, stop=True)
                    last.then_inc(folded, 1)

            @block.scalar
            def _(act):
                for p in range(2):
                    act.wait_ge(folded, p + 1)
                    nc.scalar.activation(sim_w[:, p, :], banks[p][:, :], ACT.Copy)

        with ExitStack() as stack:
            m = Memory(nc, stack, "f0t")
            tokens = m.sb("tokens", [P, SEQ])
            gate = m.sb("gate", [P, 2, SEQ])
            hidden = m.sb("hidden", [P, INTER // P, SEQ])
            act_w = m.sb("act_w", [P, E_CHUNKS, SEQ])
            side_top = m.sb("side_top", [P, 2 * SIM_HEADS])
            shifted = m.sb("shifted", [P, 2 * SIM_HEADS, SUBKEYS])
            ex = m.sb("ex", [P, 2, 2 * SIM_HEADS, SUBKEYS])
            top8 = m.sb("top8", [P, 3, SIM_HEADS, TOPK])
            pairs = m.sb("pairs", [P, SIM_HEADS, TOPK * TOPK])
            clip_pairs = m.sb("clip_pairs", [P, SIM_HEADS, TOPK * TOPK])
            picked = m.sb("picked", [P, SIM_HEADS, TOPK])
            total, inverse, clipped, clipped_w = (m.sb(n, [P, SIM_HEADS]) for n in ("total", "inverse", "clipped", "clipped_w"))
            clipped_sum = m.sb("clipped_sum", [P, 1])
            carrier = m.sb("carrier", [P, 1])
            prod = m.sb("prod", [P, 2, EXPERTS])
            weight = m.sb("weight", [P, EXPERTS])
            mixed = m.sb("mixed", [P, E_CHUNKS, P])
            sim_bank = [m.bank(f"sim{i}") for i in range(2)]
            wide_bank = [m.bank(f"wide{i}") for i in range(4)]
            out_bank = [m.bank(f"out{i}") for i in range(2)]
            tokens_ready, mlp_g, mlp_silu, mlp_u, mlp_h, w_ready, act_w_ready = (
                m.sem(n) for n in ("tokens_ready", "mlp_g", "mlp_silu", "mlp_u", "mlp_h", "w_ready", "act_w_ready"))
            sims_ready, shifted_ready, ex_ready, prod_ready, prod_used, weight_ready = (
                m.sem(n) for n in ("sims_ready", "shifted_ready", "ex_ready", "prod_ready", "prod_used", "weight_ready"))
            turned, mixed_ready, out_ready, out_added, chain = (m.sem(n) for n in ("turned", "mixed_ready", "out_ready", "out_added", "chain"))
            T = PER_BATCH
            LINKS = 12 * T
            block = stack.enter_context(nc.Block())

            @block.tensor
            def _(pe):
                pe.wait_ge(loaded, 5 * 16)
                with pe.Fori(0, TILES // T) as b:
                    group = xnT[:, bass.ds(b * SEQ, SEQ)]
                    for c in range(4):
                        if c >= 2:
                            pe.wait_ge(mlp_silu, b * 4 + (c - 1))
                        else:
                            pe.wait_ge(mixed_ready, b * 4 * T + 1)
                        nc.tensor.matmul(wide_bank[c % 2][:, :], wgT[:, P * c:P * c + P], group, start=True, stop=True).then_inc(mlp_g, 1)
                        if c >= 2:
                            pe.wait_ge(mlp_h, b * 4 + (c - 1))
                        nc.tensor.matmul(wide_bank[2 + c % 2][:, :], wuT[:, P * c:P * c + P], group, start=True, stop=True).then_inc(mlp_u, 1)
                    for e in range(E_CHUNKS):
                        if e < 4:
                            (pe.wait_ge(mlp_silu, b * 4 + (3 + e)) if e < 2 else pe.wait_ge(mlp_h, b * 4 + (1 + e)))
                        else:
                            pe.wait_ge(act_w_ready, b * E_CHUNKS + (e - 3))
                        nc.tensor.matmul(wide_bank[e % 4][:, :], downT[:, P * e:P * e + P], group, start=True, stop=True).then_inc(w_ready, 1)
                    pe.wait_ge(tokens_ready, b + 1)

                    def sims(j):
                        pe.wait_ge(shifted_ready, b * T + (j + 1))
                        for p in range(2):
                            last = nc.tensor.matmul(sim_bank[p][:, :], tokens[:, P * j:P * j + P], sim_w[:, p, :], start=True, stop=True)
                        last.then_inc(sims_ready, 1)

                    def turn(j):
                        pe.wait_ge(weight_ready, b * T + (j + 1))
                        for g in range(4):
                            if j == 0 and g == 0:
                                pe.wait_ge(act_w_ready, b * E_CHUNKS + E_CHUNKS)
                            elif 4 * j + g >= 4:
                                pe.wait_ge(mixed_ready, b * 4 * T + (4 * j + g - 4 + 2))
                            for i in range(4):
                                e = 4 * g + i
                                last = nc.tensor.transpose(wide_bank[g][:, P * i:P * i + P], weight[:, P * e:P * e + P], ident[:, :])
                            last.then_inc(turned, 1)

                    def out(j):
                        pe.wait_ge(out_added, b * T + (j + 1))
                        for c in range(4):
                            nc.tensor.matmul(out_bank[j % 2][:, 0:D], hidden[:, c, P * j:P * j + P], wdT[:, c, :], start=(c == 0), stop=False)
                        for g in range(4):
                            pe.wait_ge(mixed_ready, b * 4 * T + (4 * j + g + 2))
                            for i in range(4):
                                e = 4 * g + i
                                last = nc.tensor.matmul(out_bank[j % 2][:, 0:D], mixed[:, e, :], up[:, e, :], start=False, stop=(e == E_CHUNKS - 1))
                        last.then_inc(out_ready, 1)

                    sims(0)
                    for j in range(T):
                        if j + 1 < T:
                            sims(j + 1)
                        if j > 0:
                            out(j - 1)
                        turn(j)
                    out(T - 1)

            @block.scalar
            def _(act):
                with act.Fori(0, TILES // T) as b:
                    act.wait_ge(out_added, b * T + 2)
                    nc.scalar.activation(tokens[:, :], xnT[:, bass.ds(b * SEQ, SEQ)], ACT.Copy).then_inc(tokens_ready, 1)
                    for c in range(4):
                        act.wait_ge(mlp_g, b * 4 + (c + 1))
                        if c >= 2:
                            act.wait_ge(mlp_h, b * 4 + (c - 1))
                        nc.scalar.activation(gate[:, c % 2, :], wide_bank[c % 2][:, :], ACT.Silu).then_inc(mlp_silu, 1)
                    for e in range(E_CHUNKS):
                        act.wait_ge(w_ready, b * E_CHUNKS + (e + 1))
                        nc.scalar.activation(act_w[:, e, :], wide_bank[e % 4][:, :], ACT.Silu).then_inc(act_w_ready, 1)

                    def exponentials(j):
                        act.wait_ge(shifted_ready, b * T + (j + 2))
                        nc.scalar.activation(ex[:, j % 2, :, :], shifted[:, :, :], ACT.Exp).then_inc(ex_ready, 1)

                    exponentials(0)
                    for j in range(T):
                        for h in range(SIM_HEADS):
                            n = SIM_HEADS * j + h
                            act.wait_ge(prod_used, b * SIM_HEADS * T + (n + 1))
                            act.wait_ge(ex_ready, b * T + (j + 1))
                            for a in range(ROWS):
                                last = nc.scalar.activation(prod[:, h % 2, SUBKEYS * a:SUBKEYS * a + SUBKEYS], ex[:, j % 2, SIM_HEADS + h, :], ACT.Copy,
                                                            scale=ex[:, j % 2, h, a:a + 1])
                            last.then_inc(prod_ready, 1)
                            if h == 0 and j + 1 < T:
                                exponentials(j + 1)

            @block.vector
            def _(dve):
                dve.sem_inc(shifted_ready, 1)
                dve.sem_inc(mixed_ready, 1)
                dve.sem_inc(out_added, 2)
                dve.sem_inc(prod_used, 2)
                with dve.Fori(0, TILES // T) as b:
                    k = Chain(dve, chain, b * LINKS)
                    for c in range(4):
                        dve.wait_ge(mlp_silu, b * 4 + (c + 1))
                        dve.wait_ge(mlp_u, b * 4 + (c + 1))
                        nc.vector.tensor_tensor(hidden[:, c, :], gate[:, c % 2, :], wide_bank[2 + c % 2][:, :], ALU.mult).then_inc(mlp_h, 1)

                    def shift(j):
                        dve.wait_ge(sims_ready, b * T + (j + 1))
                        for p in range(2):
                            last = nc.vector.tensor_reduce(side_top[:, SIM_HEADS * p:SIM_HEADS * p + SIM_HEADS],
                                                           sim_bank[p][:, :].rearrange("p (h k) -> p h k", k=SUBKEYS), AX, ALU.max)
                        k.link(last)
                        dve.wait_ge(ex_ready, b * T + j) if j > 0 else None
                        for p in range(2):
                            hs = slice(SIM_HEADS * p, SIM_HEADS * p + SIM_HEADS)
                            last = nc.vector.tensor_tensor(shifted[:, hs, :], sim_bank[p][:, :].rearrange("p (h k) -> p h k", k=SUBKEYS),
                                                           side_top[:, hs].unsqueeze(2).broadcast_to([P, SIM_HEADS, SUBKEYS]), ALU.subtract)
                        last.then_inc(shifted_ready, 1)

                    def before_max():
                        nc.vector.memset(carrier[:, :], 0.0)

                    def select(j):
                        dve.wait_ge(ex_ready, b * T + (j + 1))
                        before_max()
                        for h in range(SIM_HEADS):
                            nc.vector.max(top8[:, 0, h, :], ex[:, j % 2, h, :])
                            nc.vector.max(top8[:, 1, h, :], ex[:, j % 2, SIM_HEADS + h, :])
                            last = nc.vector.max(top8[:, 2, h, :], ex[:, j % 2, h, ROWS:SUBKEYS])
                        k.link(last)
                        shape = [P, SIM_HEADS, TOPK, TOPK]
                        second = top8[:, 1, :, :].unsqueeze(2).broadcast_to(shape)
                        for side, dst in ((0, pairs), (2, clip_pairs)):
                            last = nc.vector.tensor_tensor(dst[:, :, :].rearrange("p h (i j) -> p h i j", i=TOPK),
                                                           top8[:, side, :, :].unsqueeze(3).broadcast_to(shape), second, ALU.mult)
                        k.link(last)
                        before_max()
                        for h in range(SIM_HEADS):
                            last = nc.vector.max(picked[:, h, :], pairs[:, h, :])
                        k.link(last)
                        nc.vector.tensor_reduce(total[:, :], picked[:, :, :], AX, ALU.add)
                        for h in range(SIM_HEADS):
                            last = nc.vector.scalar_tensor_tensor(clip_pairs[:, h, :], clip_pairs[:, h, :], picked[:, h, TOPK - 1:TOPK], clip_pairs[:, h, :],
                                                                  op0=ALU.is_ge, op1=ALU.mult)
                        k.link(last)
                        nc.vector.tensor_reduce(clipped[:, :], clip_pairs[:, :, :], AX, ALU.add)
                        k.link(nc.vector.reciprocal(inverse[:, :], total[:, :]))
                        k.link(nc.vector.tensor_tensor(clipped_w[:, :], clipped[:, :], inverse[:, :], ALU.mult))
                        k.link(nc.vector.tensor_reduce(clipped_sum[:, :], clipped_w[:, :], AX, ALU.add))

                    def mix(j):
                        for g in range(4):
                            dve.wait_ge(turned, b * 4 * T + (4 * j + g + 1))
                            if g == 0:
                                dve.wait_ge(out_ready, b * T + j) if j > 0 else None
                            es = slice(4 * g, 4 * g + 4)
                            nc.vector.tensor_tensor(mixed[:, es, :], act_w[:, es, P * j:P * j + P],
                                                    wide_bank[g][:, :].rearrange("p (e t) -> p e t", t=P), ALU.mult).then_inc(mixed_ready, 1)

                    def weigh(j):
                        for h in range(SIM_HEADS):
                            dve.wait_ge(prod_ready, b * SIM_HEADS * T + (SIM_HEADS * j + h + 1))
                            p = prod[:, h % 2, :]
                            k.link(nc.vector.scalar_tensor_tensor(p, p, picked[:, h, TOPK - 1:TOPK], p, op0=ALU.is_ge, op1=ALU.mult))
                            if h == 0:
                                step = nc.vector.tensor_scalar(weight[:, :], p, inverse[:, h:h + 1], None, ALU.mult)
                            else:
                                step = nc.vector.scalar_tensor_tensor(weight[:, :], p, inverse[:, h:h + 1], weight[:, :], op0=ALU.mult, op1=ALU.add)
                            step.then_inc(prod_used, 1)
                            dve.wait_ge(prod_used, b * SIM_HEADS * T + (SIM_HEADS * j + h + 3))
                        last = weight[:, EXPERTS - 1:EXPERTS]
                        nc.vector.tensor_tensor(last, last, clipped_sum[:, :], ALU.add).then_inc(weight_ready, 1)

                    def add(j):
                        dve.wait_ge(out_ready, b * T + (j + 1))
                        row = x[:, bass.ds(b * T + j, 1), :].rearrange("p o d -> p (o d)")
                        nc.vector.tensor_tensor(row, row, out_bank[j % 2][:, 0:D], ALU.add).then_inc(out_added, 1)

                    shift(0)
                    for j in range(T):
                        select(j)
                        if j + 1 < T:
                            shift(j + 1)
                        if j > 0:
                            mix(j - 1)
                        weigh(j)
                        if j > 0:
                            add(j - 1)
                    mix(T - 1)
                    add(T - 1)
                    assert k.n == LINKS


def expert_ffn(nc, io, x, xnT, ident, out):
    with ExitStack() as keep:
        mk = Memory(nc, keep, "f1")
        combT = mk.sb("combT", [P, TOKENS], F32R)
        gate_w, bias = mk.sb("gate_w", [P, MOE_E]), mk.sb("bias", [P, MOE_E])
        half_id = mk.sb("half_id", [P, MOE_E])
        with ExitStack() as stack:
            m = Memory(nc, stack, "f1g")
            wide = [P, TILES, MOE_E]
            score, biased, masked, sel = (m.sb(n, wide) for n in ("score", "biased", "masked", "sel"))
            hi_lo = m.sb("hi_lo", [P, TILES, 2, MOE_E], F32R)
            tour = [m.sb(f"tour{i}", [P, TILES, GROUPS, 4]) for i in range(6)]
            group_score, group_top, mask = (m.sb(n, [P, TILES, GROUPS]) for n in ("group_score", "group_top", "mask"))
            picked = m.sb("picked", [P, TILES, 8])
            total, inverse = m.sb("total", [P, TILES]), m.sb("inverse", [P, TILES])
            logit_bank = [m.bank(f"logit{i}") for i in range(2)]
            turn_bank = [m.bank(f"turn{i}") for i in range(4)]
            loaded, chain, logits_ready, exp_ready, comb_ready, turned = (m.sem(n) for n in ("loaded", "chain", "logits_ready", "exp_ready", "comb_ready", "turned"))
            block = stack.enter_context(nc.Block())

            @block.sync
            def _(sp):
                for dst, src in ((gate_w, "gate_w"), (bias, "bias"), (half_id, "half_id")):
                    sp.dma_start(dst[:], io[src]).then_inc(loaded, 16)

            @block.tensor
            def _(pe):
                pe.wait_ge(loaded, 48)
                for t in range(TILES):
                    i = nc.tensor.matmul(logit_bank[t // 8][:, MOE_E * (t % 8):MOE_E * (t % 8) + MOE_E], xnT[:, P * t:P * t + P], gate_w[:, :], start=True, stop=True)
                i.then_inc(logits_ready, 1)
                pe.wait_ge(comb_ready, 1)
                for t in range(TILES):
                    i = nc.tensor.transpose(turn_bank[t // 4][:, P * (t % 4):P * (t % 4) + P],
                                            hi_lo[:, t, :, :].rearrange("p s e -> p (s e)").bitcast(F32), ident[:, :])
                i.then_inc(turned, 1)

            @block.scalar
            def _(act):
                act.wait_ge(logits_ready, 1)
                for i in range(2):
                    last = nc.scalar.activation(score[:, 8 * i:8 * i + 8, :], logit_bank[i][:, :].rearrange("p (t e) -> p t e", e=MOE_E), ACT.Exp, scale=-1.0)
                last.then_inc(exp_ready, 1)
                act.wait_ge(turned, 1)
                for i in range(4):
                    nc.scalar.activation(combT[:, 512 * i:512 * i + 512], turn_bank[i][:, :], ACT.Copy)

            @block.vector
            def _(dve):
                k = Chain(dve, chain)
                tt, ts = nc.vector.tensor_tensor, nc.vector.tensor_scalar
                dve.wait_ge(loaded, 48)
                dve.wait_ge(exp_ready, 1)
                k.link(ts(score[:, :, :], score[:, :, :], 1.0, None, ALU.add))
                k.link(nc.vector.reciprocal(score[:, :, :], score[:, :, :]))
                k.link(tt(biased[:, :, :], score[:, :, :], bias[:, :].unsqueeze(1).broadcast_to(wide), ALU.add))
                b4 = biased[:, :, :].rearrange("p t (g e) -> p t g e", e=GROUP_E)
                flat = [t[:, :, :, :].rearrange("p t g e -> p (t g) e") for t in tour]
                b3 = b4.rearrange("p t g e -> p (t g) e")
                best, next_, low, keep_best, keep_next = flat[0], flat[1], flat[2], flat[3], flat[4]
                tt(best, b3[:, :, 0:4], b3[:, :, 4:8], ALU.max)
                k.link(tt(next_, b3[:, :, 0:4], b3[:, :, 4:8], ALU.min))
                for n in (2, 1):
                    a, c = slice(0, n), slice(n, 2 * n)
                    tt(low[:, :, a], best[:, :, a], best[:, :, c], ALU.min)
                    tt(keep_best[:, :, a], best[:, :, a], best[:, :, c], ALU.max)
                    k.link(tt(keep_next[:, :, a], next_[:, :, a], next_[:, :, c], ALU.max))
                    k.link(tt(next_[:, :, a], low[:, :, a], keep_next[:, :, a], ALU.max))
                    best, keep_best = keep_best, best
                k.link(tt(group_score[:, :, :].rearrange("p t g -> p (t g)").unsqueeze(2), best[:, :, 0:1], next_[:, :, 0:1], ALU.add))
                for t in range(TILES):
                    last = nc.vector.max(group_top[:, t, :], group_score[:, t, :])
                k.link(last)
                k.link(tt(mask[:, :, :], group_score[:, :, :], group_top[:, :, TOP_GROUPS - 1:TOP_GROUPS].broadcast_to([P, TILES, GROUPS]), ALU.is_ge))
                k.link(ts(mask[:, :, :], mask[:, :, :], 1.0, BIG, ALU.subtract, ALU.mult))
                k.link(tt(masked[:, :, :].rearrange("p t (g e) -> p (t g) e", e=GROUP_E), b3,
                          mask[:, :, :].rearrange("p t g -> p (t g)").unsqueeze(2).broadcast_to([P, TILES * GROUPS, GROUP_E]), ALU.add))
                for t in range(TILES):
                    last = nc.vector.max(picked[:, t, :], masked[:, t, :])
                k.link(last)
                k.link(tt(sel[:, :, :], masked[:, :, :], picked[:, :, 7:8].broadcast_to(wide), ALU.is_ge))
                k.link(tt(sel[:, :, :], sel[:, :, :], score[:, :, :], ALU.mult))
                k.link(nc.vector.tensor_reduce(total[:, :], sel[:, :, :], AX, ALU.add))
                k.link(ts(total[:, :], total[:, :], 1e-20, None, ALU.add))
                k.link(nc.vector.reciprocal(inverse[:, :], total[:, :]))
                k.link(ts(inverse[:, :], inverse[:, :], TW_SCALE, None, ALU.mult))
                k.link(tt(sel[:, :, :], sel[:, :, :], inverse[:, :].unsqueeze(2).broadcast_to(wide), ALU.mult))
                k.link(nc.vector.tensor_copy(hi_lo[:, :, 0, :], sel[:, :, :]))
                tt(hi_lo[:, :, 1, :], sel[:, :, :], hi_lo[:, :, 0, :].bitcast(F32), ALU.subtract).then_inc(comb_ready, 1)

        with ExitStack() as stack:
            m = Memory(nc, stack, "f1e")
            W = 3 * P
            NG = TOKENS // 512
            STEP = 2 * NG
            LOOPS = PAIRS // 2
            LAG = 2
            RING = 4
            tok_hi, tok_lo = m.sb("tok_hi", [P, TOKENS], F32R), m.sb("tok_lo", [P, TOKENS], F32R)
            raw = m.sb("raw", [P, 2, W])
            one, one_ready = m.sb("one", [P, 1]), m.sem("one_ready")
            w_hi, w_lo = m.sb("w_hi", [P, 2, W], F32R), m.sb("w_lo", [P, 2, W], F32R)
            spread = m.sb("spread", [P, 2, 2, MOE_F], F32R)
            gate, gu, hid = m.sb("gate", [P, 2, 512]), m.sb("gu", [P, 2, 512]), m.sb("hid", [P, 2, 512])
            hid_hi, hid_lo = m.sb("hid_hi", [P, RING, 512], F32R), m.sb("hid_lo", [P, RING, 512], F32R)
            yT = m.sb("yT", [P, TOKENS])
            g_bank, u_bank, c_bank = m.bank("g"), m.bank("u"), m.bank("c")
            y_bank = [m.bank(f"y{i}") for i in range(NG)]
            t_bank = m.bank("t")
            raw_loaded = [m.sem(f"raw{i}_loaded") for i in range(2)]
            tok_hi_ready, tok_lo_ready, w_hi_ready, w_ready = (m.sem(n) for n in ("tok_hi_ready", "tok_lo_ready", "w_hi_ready", "w_ready"))
            g_ready, u_ready, c_ready, silu_ready, gu_ready, hid_ready, hi_ready, lo_ready, hid_used = (
                m.sem(n) for n in ("g_ready", "u_ready", "c_ready", "silu_ready", "gu_ready", "hid_ready", "hi_ready", "lo_ready", "hid_used"))
            y_ready, y_kept, turned, x_ready, stored = (m.sem(n) for n in ("y_ready", "y_kept", "turned", "x_ready", "stored"))
            block = stack.enter_context(nc.Block())

            def steps(eng, first_step, step, last_step):
                first_step()
                with eng.Fori(0, LOOPS - 1) as i:
                    step(i * STEP + NG, i * 2 + 1)
                last_step((LOOPS - 1) * STEP + NG, (LOOPS - 1) * 2 + 1)

            @block.sync
            def _(sp):
                def load(pair, slot, src):
                    sp.dma_start(raw[:, slot, :], src).then_inc(raw_loaded[slot], 16)

                load(0, 0, io["shared"])
                load(1, 1, io["pairs"][:, 0:W])
                def reload(turn, slot, pair):
                    sp.wait_ge(w_ready, turn - 1)
                    load(turn, slot, io["pairs"][:, bass.ds(pair * W, W)])

                with sp.Fori(0, LOOPS - 1) as i:
                    for slot in range(2):
                        reload(i * 2 + (2 + slot), slot, i * 2 + (1 + slot))
                reload(PAIRS, 0, PAIRS - 1)
                for g in range(NG):
                    sp.wait_ge(x_ready, g + 1)
                    sp.dma_start(out[:, 4 * g:4 * g + 4, :], x[:, 4 * g:4 * g + 4, :]).then_inc(stored, 16)
                sp.wait_ge(stored, 16 * NG)

            @block.gpsimd
            def _(pool):
                def split(pair, slot, loads, free):
                    pool.wait_ge(raw_loaded[slot], loads)
                    if free is not None:
                        pool.wait_ge(hid_used, free)
                    nc.gpsimd.tensor_tensor(w_hi[:, slot, :], raw[:, slot, :], one[:, :].broadcast_to([P, W]), ALU.mult).then_inc(w_hi_ready, 1)
                    pool.wait_ge(w_hi_ready, pair + 1)
                    return nc.gpsimd.tensor_tensor(w_lo[:, slot, :], raw[:, slot, :], w_hi[:, slot, :].bitcast(F32), ALU.subtract)

                nc.gpsimd.memset(one[:, :], 1.0).then_inc(one_ready, 1)
                pool.wait_ge(one_ready, 1)
                split(0, 0, 16, None).then_inc(w_ready, 1)
                with pool.Fori(0, LOOPS) as i:
                    for s in range(2):
                        slot = (1 + s) % 2
                        pair = i * 2 + (1 + s)
                        free = i * STEP + (NG if s else 1)
                        split(pair, slot, (i + 1 + s) * 16, free)
                        nc.gpsimd.tensor_copy(spread[:, slot, :, :], half_id[:, bass.ds((i * 2 + s) * 2, 2)].unsqueeze(2).broadcast_to([P, 2, MOE_F])).then_inc(w_ready, 1)

            @block.tensor
            def _(pe):
                def split_product(bank, w_slice, hi, lo, start, stop):
                    slot, cols = w_slice
                    nc.tensor.matmul(bank, w_hi[:, slot, cols], hi, start=start, stop=False)
                    nc.tensor.matmul(bank, w_hi[:, slot, cols], lo, start=False, stop=False)
                    return nc.tensor.matmul(bank, w_lo[:, slot, cols], hi, start=False, stop=stop)

                def up(base, n, pair, shared=False):
                    g, slot = n % NG, (n // NG + (0 if shared else 1)) % 2
                    hi, lo = (t[:, 512 * g:512 * g + 512] for t in (tok_hi, tok_lo))
                    if g == 0 or (shared and g == 0):
                        pe.wait_ge(w_ready, pair + 1)
                    if not (shared and n == 0):
                        pe.wait_ge(silu_ready, base + n)
                    split_product(g_bank[:, :], (slot, slice(0, P)), hi, lo, True, True).then_inc(g_ready, 1)
                    if not (shared and n == 0):
                        pe.wait_ge(gu_ready, base + n)
                    split_product(u_bank[:, :], (slot, slice(P, 2 * P)), hi, lo, True, True).then_inc(u_ready, 1)
                    if not shared:
                        pe.wait_ge(hid_ready, base + n)
                        nc.tensor.matmul(c_bank[:, :], spread[:, slot, :, :].rearrange("p a f -> p (a f)"),
                                         combT[:, 512 * g:512 * g + 512], start=True, stop=True).then_inc(c_ready, 1)

                def down(base, n, shared=False, stop=False):
                    g, slot = n % NG, (n // NG + (0 if shared else 1)) % 2
                    pe.wait_ge(lo_ready, base + (n + 1))
                    split_product(y_bank[g][:, :], (slot, slice(2 * P, 3 * P)), hid_hi[:, n % RING, :], hid_lo[:, n % RING, :],
                                  shared, stop).then_inc(hid_used, 1)

                def first_step():
                    pe.wait_ge(tok_lo_ready, 1)
                    for n in range(NG + LAG):
                        if n < NG:
                            up(0, n, 0, shared=True)
                        else:
                            up(NG, n - NG, 1)
                        if n >= LAG:
                            down(0, n - LAG, shared=True)

                def step(base, pair):
                    for n in range(STEP):
                        k = n + LAG
                        up(base, k, pair + k // NG)
                        down(base, n)

                def last_step(base, pair):
                    for n in range(STEP):
                        k = n + LAG
                        if k < STEP:
                            up(base, k, pair + k // NG)
                        down(base, n)

                steps(pe, first_step, step, last_step)
                for g in range(NG):
                    for i in range(4):
                        last = nc.tensor.matmul(y_bank[g][:, P * i:P * i + P], x[:, 4 * g + i, :], ident[:, :], start=False, stop=(i == 3))
                    last.then_inc(y_ready, 1)
                for g in range(NG):
                    pe.wait_ge(y_kept, g + 1)
                    if g:
                        pe.wait_ge(x_ready, g)
                    for i in range(4):
                        t = 4 * g + i
                        last = nc.tensor.transpose(t_bank[:, P * i:P * i + P], yT[:, P * t:P * t + P], ident[:, :])
                    last.then_inc(turned, 1)

            @block.scalar
            def _(act):
                def silu(base, n, first=False):
                    act.wait_ge(g_ready, base + (n + 1))
                    if not first:
                        act.wait_ge(gu_ready, base + (n - 1))
                    nc.scalar.activation(gate[:, n % 2, :], g_bank[:, :], ACT.Silu).then_inc(silu_ready, 1)

                def high(base, n, first=False):
                    act.wait_ge(hid_ready, base + (n + 1))
                    if not first:
                        act.wait_ge(hid_used, base + (n + 2 - RING))
                    nc.scalar.activation(hid_hi[:, n % RING, :], hid[:, n % 2, :], ACT.Copy).then_inc(hi_ready, 1)

                def first_step():
                    for i in range(NG):
                        last = nc.scalar.activation(tok_hi[:, 512 * i:512 * i + 512], xnT[:, 512 * i:512 * i + 512], ACT.Copy)
                    last.then_inc(tok_hi_ready, 1)
                    for n in range(NG):
                        silu(0, n, first=(n < 2))
                        if n:
                            high(0, n - 1, first=True)

                def step(base, pair):
                    for n in range(STEP):
                        silu(base, n)
                        high(base, n - 1)

                def last_step(base, pair):
                    step(base, pair)
                    high(base, STEP - 1)

                steps(act, first_step, step, last_step)
                for g in range(NG):
                    act.wait_ge(y_ready, g + 1)
                    nc.scalar.activation(yT[:, 512 * g:512 * g + 512], y_bank[g][:, :], ACT.Copy).then_inc(y_kept, 1)

            @block.vector
            def _(dve):
                def hidden(base, n, shared=False):
                    dve.wait_ge(silu_ready, base + (n + 1))
                    dve.wait_ge(u_ready, base + (n + 1))
                    nc.vector.tensor_tensor(gu[:, n % 2, :], gate[:, n % 2, :], u_bank[:, :], ALU.mult).then_inc(gu_ready, 1)
                    dve.wait_ge(gu_ready, base + (n + 1))
                    if shared:
                        nc.vector.tensor_copy(hid[:, n % 2, :], gu[:, n % 2, :]).then_inc(hid_ready, 1)
                    else:
                        dve.wait_ge(c_ready, base + (n + 1 - NG))
                        nc.vector.tensor_tensor(hid[:, n % 2, :], gu[:, n % 2, :], c_bank[:, :], ALU.mult).then_inc(hid_ready, 1)

                def low(base, n):
                    dve.wait_ge(hi_ready, base + (n + 1))
                    nc.vector.tensor_tensor(hid_lo[:, n % RING, :], hid[:, n % 2, :], hid_hi[:, n % RING, :].bitcast(F32), ALU.subtract).then_inc(lo_ready, 1)

                def first_step():
                    dve.wait_ge(tok_hi_ready, 1)
                    nc.vector.tensor_tensor(tok_lo[:, :], xnT[:, :], tok_hi[:, :].bitcast(F32), ALU.subtract).then_inc(tok_lo_ready, 1)
                    for n in range(NG):
                        hidden(0, n, shared=True)
                        if n:
                            low(0, n - 1)

                def step(base, pair):
                    for n in range(STEP):
                        hidden(base, n)
                        low(base, n - 1)

                def last_step(base, pair):
                    step(base, pair)
                    low(base, STEP - 1)

                steps(dve, first_step, step, last_step)
                for g in range(NG):
                    dve.wait_ge(turned, g + 1)
                    nc.vector.tensor_copy(x[:, 4 * g:4 * g + 4, :], t_bank[:, :].rearrange("p (t d) -> p t d", t=4)).then_inc(x_ready, 1)


def program(nc, io, out, stop=9):
    with ExitStack() as stack:
        m = Memory(nc, stack, "main")
        x = m.sb("x", [P, TILES, D])
        xnT = m.sb("xnT", [P, TOKENS])
        ctxT = m.sb("ctxT", [P, CTX])
        ident = m.sb("ident", [P, P])
        eps = m.sb("eps", [P, 1])
        dense_attention(nc, io, x, xnT, ident, eps, ctxT)
        with ExitStack() as layer1:
            m1 = Memory(nc, layer1, "layer1")
            keyT, value = m1.sb("keyT", [P, BATCH * ALL_KEYS]), m1.sb("value", [P, BATCH * KEY_CHUNKS * D])
            spread, signed_bias = m1.sb("spread", [P, FEATURE_CHUNKS * P]), m1.sb("signed_bias", [P, 1])
            if stop > 1:
                feature_setup(nc, io, x, xnT, ident, eps, ctxT, keyT, value, spread, signed_bias)
                product_key_ffn(nc, io, x, xnT, ident)
            if stop > 2:
                layer_norm(nc, "ln2", x, xnT, ident, eps)
                feature_attention(nc, io, x, xnT, ident, keyT, value, spread, signed_bias)
        if stop > 3:
            layer_norm(nc, "ln3", x, xnT, ident, eps)
            expert_ffn(nc, io, x, xnT, ident, out)
        else:
            with ExitStack() as s:
                stored = Memory(nc, s, "st").sem("stored")
                block = s.enter_context(nc.Block())

                @block.sync
                def _(sp):
                    sp.dma_start(out, x[:, :, :]).then_inc(stored, 16)
                    sp.wait_ge(stored, 16)


def kernel(**inputs):
    import numpy as np
    import concourse.bacc as bacc
    from concourse.bass_utils import run_bass_kernel_spmd as run

    a = {k: np.asarray(v) for k, v in inputs.items()}
    rows = np.arange(P)
    pairs = np.concatenate([
        a["L1_ffn_We_gate"].reshape(PAIRS, 2, D, MOE_F).transpose(2, 0, 1, 3).reshape(D, PAIRS, P),
        a["L1_ffn_We_up"].reshape(PAIRS, 2, D, MOE_F).transpose(2, 0, 1, 3).reshape(D, PAIRS, P),
        a["L1_ffn_We_down"].reshape(PAIRS, P, D).transpose(1, 0, 2)], axis=2)
    shared = np.zeros((P, 3 * P), np.float32)
    shared[:, 0:MOE_F] = a["L1_ffn_Ws_gate"]
    shared[:, P:P + MOE_F] = a["L1_ffn_Ws_up"]
    shared[0:MOE_F, 2 * P:2 * P + D] = a["L1_ffn_Ws_down"]
    laid = {
        "x": a["x"].reshape(TILES, P, D).transpose(1, 0, 2),
        "ctxT": a["ctx_1024"].reshape(CTX, D).T,
        "WqT": a["L0_xattn_Wq"].T.reshape(8, P, D).transpose(1, 0, 2),
        "Wk": a["L0_xattn_Wk"],
        "Wv": a["L0_xattn_Wv"],
        "Wo": a["L0_xattn_Wo"].reshape(8, P, D).transpose(1, 0, 2),
        "ffn_wq": a["L0_ffn_Wq"].reshape(2, SIM_HEADS, 64, D).transpose(0, 2, 1, 3).reshape(P, SIM_HEADS, D),
        "keysT": a["L0_ffn_keys"].transpose(2, 3, 0, 1).reshape(P, SIM_HEADS, SUBKEYS),
        "downT": a["L0_ffn_down_embed"].T,
        "up": a["L0_ffn_up_embed"].reshape(E_CHUNKS, P, D).transpose(1, 0, 2),
        "wgT": a["L0_ffn_Wg"].T,
        "wuT": a["L0_ffn_Wu"].T,
        "wdT": a["L0_ffn_Wd"].T.reshape(INTER // P, P, D).transpose(1, 0, 2),
        "fm": np.tile(a["L1_xattn_fm_w"].T, (16, 1)),
        "fb": np.tile(a["L1_xattn_fm_b"], 16).reshape(P, 1),
        "fcT": a["L1_xattn_fc_w"].T.reshape(2, P, D).transpose(1, 0, 2),
        "fcb": np.tile(a["L1_xattn_fc_b"], (P, 1)),
        "gate_w": a["L1_ffn_gate_w"].T,
        "bias": np.tile(a["L1_ffn_gate_bias"], (P, 1)),
        "pairs": pairs.reshape(D, PAIRS * 3 * P),
        "shared": shared,
        "ident": np.eye(P, dtype=np.float32),
        "by16": (rows[:, None] // 16 == np.arange(8)).astype(np.float32),
        "by8": (rows[:, None] // 8 == np.arange(16)).astype(np.float32),
        "sign": (1.0 - 2.0 * (rows[:, None] // 8 % 2)).astype(np.float32),
        "half_id": (rows[:, None] % MOE_E == np.arange(MOE_E)).astype(np.float32),
    }
    laid = {k: np.ascontiguousarray(v) for k, v in laid.items()}
    nc = bacc.Bacc("TRN2", target_bir_lowering=False, num_devices=1)
    io = {k: nc.dram_tensor(f"in_{k}", v.shape, F32, kind="ExternalInput").ap() for k, v in laid.items()}
    out = nc.dram_tensor("out_x", (P, TILES, D), F32, kind="ExternalOutput").ap()
    program(nc, io, out)
    r = run(nc, [{f"in_{k}": v for k, v in laid.items()}], core_ids=[0])
    got = r.results[0]["out_x"]
    return np.ascontiguousarray(got.transpose(1, 0, 2)).reshape(BATCH, SEQ, D)
```

```python
import concourse.bass as bass
from concourse import mybir
from contextlib import ExitStack
import numpy as np

F32 = mybir.dt.float32
F32R = mybir.dt.float32r
ALU = mybir.AluOpType
ACT = mybir.ActivationFunctionType
AX = mybir.AxisListType.X

P = 128
BATCH, SEQ, D = 4, 512, 128
TOKENS = BATCH * SEQ
TILES = TOKENS // P
PER_BATCH = SEQ // P
KEYS = 77
CTX = BATCH * KEYS
HEADS = 16
ALL_KEYS = HEADS * KEYS
KEY_CHUNKS = (ALL_KEYS + P - 1) // P
PADDED_KEYS = KEY_CHUNKS * P
EPS = 1e-5
BANK_HEADS = ((0, 6), (6, 5), (11, 5))
SIM_HEADS, SUBKEYS, TOPK = 4, 128, 8
EXPERTS = 2048
ROWS = EXPERTS // SUBKEYS
E_CHUNKS = EXPERTS // P
INTER = 512
MOE_E, MOE_F = 64, 64
PAIRS = MOE_E // 2
GROUPS, GROUP_E, TOP_GROUPS = 8, 8, 4
TW_SCALE = 2.5
BIG = 1e30


class Memory:

    def __init__(self, nc, stack, name):
        self.nc, self.stack, self.name = nc, stack, name

    def sb(self, name, shape, dt=F32):
        return self.stack.enter_context(self.nc.sbuf_tensor(f"{self.name}_{name}", list(shape), dt))

    def bank(self, name):
        return self.stack.enter_context(self.nc.psum_tensor(f"{self.name}_{name}", [P, 512], F32))

    def sem(self, name):
        return self.stack.enter_context(self.nc.semaphore(f"{self.name}_{name}"))


class Chain:

    def __init__(self, eng, sem, base=0):
        self.eng, self.sem, self.base, self.n = eng, sem, base, 0

    def link(self, instruction):
        self.n += 1
        instruction.then_inc(self.sem, 1)
        self.eng.wait_ge(self.sem, self.base + self.n)


class Norm:

    def __init__(self, nc, m, x, xnT, ident, eps, stats, stats_made=True, banks=None):
        self.nc, self.x, self.xnT, self.ident, self.eps, self.stats, self.stats_made = nc, x, xnT, ident, eps, stats, stats_made
        self.xn = m.sb("xn", [P, TILES, D])
        self.moments = m.sb("moments", [P, TILES, 2])
        self.sd, self.rstd = m.sb("sd", [P, TILES]), m.sb("rstd", [P, TILES])
        self.banks = banks or [m.bank(f"xn_turned{i}") for i in range(2)]
        self.stats_ready, self.moments_ready, self.sd_ready, self.rstd_ready, self.xn_ready, self.turned, self.kept = (
            m.sem(n) for n in ("stats_ready", "moments_ready", "sd_ready", "rstd_ready", "xn_ready", "xn_turned", "xn_kept"))

    def vector(self, dve):
        self.vector_moments(dve)
        for t in range(TILES):
            self.vector_scale(t)

    def vector_moments(self, dve, meanwhile=None):
        nc = self.nc
        if not self.stats_made:
            for t in range(TILES):
                last = nc.vector.bn_stats(self.stats[:, t, :], self.x[:, t, :])
            last.then_inc(self.stats_ready, 1)
            dve.wait_ge(self.stats_ready, 1)
        for t in range(TILES):
            last = nc.vector.bn_aggr(self.moments[:, t, :], self.stats[:, t, :])
        last.then_inc(self.moments_ready, 1)
        if meanwhile:
            meanwhile()
        dve.wait_ge(self.sd_ready, 1)
        nc.vector.reciprocal(self.rstd[:, :], self.sd[:, :]).then_inc(self.rstd_ready, 1)
        dve.wait_ge(self.rstd_ready, 1)

    def vector_scale(self, t):
        scaled = self.nc.vector.tensor_scalar(self.xn[:, t, :], self.x[:, t, :], self.moments[:, t, 0:1], self.rstd[:, t:t + 1], ALU.subtract, ALU.mult)
        if t % 4 == 3:
            scaled.then_inc(self.xn_ready, 1)

    def scalar_deviation(self, act):
        act.wait_ge(self.moments_ready, 1)
        self.nc.scalar.activation(self.sd[:, :], self.moments[:, :, 1], ACT.Sqrt, bias=self.eps[:, 0:1]).then_inc(self.sd_ready, 1)

    def tensor(self, pe):
        for g in range(4):
            self.tensor_group(pe, g)

    def tensor_group(self, pe, g):
        pe.wait_ge(self.xn_ready, g + 1)
        if g >= 2:
            pe.wait_ge(self.kept, g - 1)
        for i in range(4):
            last = self.nc.tensor.transpose(self.banks[g % 2][:, P * i:P * i + P], self.xn[:, 4 * g + i, :], self.ident[:, :])
        last.then_inc(self.turned, 1)

    def scalar_keep(self, act):
        for g in range(4):
            self.scalar_keep_group(act, g)

    def scalar_keep_group(self, act, g):
        act.wait_ge(self.turned, g + 1)
        self.nc.scalar.activation(self.xnT[:, 512 * g:512 * g + 512], self.banks[g % 2][:, :], ACT.Copy).then_inc(self.kept, 1)


def attention(nc, m, stack, x, stats, source, ident, keyT, value, scale, pieces):
    CHUNKS = source.shape[1]
    queries = m.sb("queries", [P, CHUNKS, SEQ])
    scores_bank = [[m.bank(f"scores{s}{i}") for i in range(3)] for s in range(2)]
    turn_bank, out_bank = m.bank("turn"), m.bank("out")
    neg_top = m.sb("neg_top", [P, 2, HEADS])
    EXPS = 4
    exps = m.sb("exps", [P, EXPS, PADDED_KEYS])
    sums = m.sb("sums", [P, EXPS, HEADS])
    inverse = m.sb("inverse", [P, 2, HEADS])
    probsT = m.sb("probsT", [P, 2, KEY_CHUNKS, P])
    queries_ready = m.sem("queries_ready")
    CREDIT = 2
    AHEAD = 2
    scores_ready, neg_top_ready, exps_ready, inverse_ready, probs_ready = (
        m.sem(n) for n in ("scores_ready", "neg_top_ready", "exps_ready", "inverse_ready", "probs_ready"))
    ROUNDS = [range(4 * r, min(4 * r + 4, KEY_CHUNKS)) for r in range(3)]
    R = len(ROUNDS)
    turned, kept, out_ready, out_added, padded = (m.sem(n) for n in ("turned", "kept", "out_ready", "out_added", "padded"))
    block = stack.enter_context(nc.Block())

    def tile(b, k):
        return b + k // PER_BATCH, k % PER_BATCH, b * PER_BATCH + k

    def steps(eng, step):
        step(0, 0, True, False)
        with eng.Fori(0, BATCH - 1) as b:
            for k in range(1, PER_BATCH + 1):
                step(b, k, True, True)
        for k in range(1, PER_BATCH):
            step(BATCH - 1, k, k + AHEAD < PER_BATCH, True)

    @block.gpsimd
    def _(pool):
        nc.gpsimd.memset(exps[:, :, ALL_KEYS:PADDED_KEYS], 0.0).then_inc(padded, 1)

    @block.tensor
    def _(pe):
        pe.sem_inc(turned, R * EXPS)
        pe.sem_inc(out_ready, CREDIT)
        pe.wait_ge(padded, 1)

        def scores(b, k):
            batch, j, n = tile(b, k)
            if j == 0:
                pe.wait_ge(queries_ready, batch + 1)
            pe.wait_ge(exps_ready, n + 1)
            for bank, col, cols, q, first in pieces:
                last = nc.tensor.matmul(scores_bank[k % 2][bank][:, col:col + cols], queries[:, q, P * j:P * j + P],
                                        keyT[:, bass.ds(batch * ALL_KEYS + first, cols)], start=True, stop=True)
            last.then_inc(scores_ready, 1)

        def turn(b, k, r):
            batch, j, n = tile(b, k)
            if r == 0:
                pe.wait_ge(probs_ready, n + 1)
            pe.wait_ge(kept, n * R + (r + CREDIT))
            for i, c in enumerate(ROUNDS[r]):
                last = nc.tensor.transpose(turn_bank[:, P * i:P * i + P], exps[:, k % EXPS, P * c:P * c + P], ident[:, :])
            last.then_inc(turned, 1)

        def values(b, k, r):
            batch, j, n = tile(b, k)
            if r == 0:
                pe.wait_ge(kept, n * R + (R + CREDIT))
                pe.wait_ge(out_added, n + 1)
            for c in ROUNDS[r]:
                last = nc.tensor.matmul(out_bank[:, 0:D], probsT[:, k % 2, c, :], value[:, bass.ds((batch * KEY_CHUNKS + c) * D, D)],
                                        start=(c == 0), stop=(c == KEY_CHUNKS - 1))
            if r == R - 1:
                last.then_inc(out_ready, 1)

        def step(b, k, ahead, before):
            if ahead:
                scores(b, k + AHEAD)
            for r in range(R):
                turn(b, k, r)
                if before:
                    values(b, k - 1, r)

        for k in range(AHEAD):
            scores(0, k)
        steps(pe, step)
        for r in range(R):
            values(BATCH - 1, PER_BATCH - 1, r)

    @block.scalar
    def _(act):
        act.sem_inc(exps_ready, CREDIT)

        def fetch(batch):
            for q in range(CHUNKS):
                last = nc.scalar.activation(queries[:, q, :], source[:, q, bass.ds(batch * SEQ, SEQ)], ACT.Copy, scale=scale)
            last.then_inc(queries_ready, 1)

        def exponentials(b, k, more):
            batch, j, n = tile(b, k)
            act.wait_ge(neg_top_ready, n + 1)
            act.wait_ge(turned, n * R + R)
            for bank, (first, heads) in enumerate(BANK_HEADS):
                for i in range(heads):
                    h = first + i
                    last = nc.scalar.activation(exps[:, k % EXPS, KEYS * h:KEYS * h + KEYS],
                                                scores_bank[k % 2][bank][:, KEYS * i:KEYS * i + KEYS], ACT.Exp,
                                                bias=neg_top[:, k % 2, h:h + 1], accum_out=sums[:, k % EXPS, h:h + 1])
                if bank == 0 and j == PER_BATCH - AHEAD and more:
                    act.wait_ge(scores_ready, batch * PER_BATCH + PER_BATCH)
                    fetch(batch + 1)
            last.then_inc(exps_ready, 1)

        def step(b, k, ahead, before):
            exponentials(b, k, not (isinstance(b, int) and b == BATCH - 1))

        fetch(0)
        steps(act, step)

    @block.vector
    def _(dve):
        dve.sem_inc(out_added, 1)
        dve.sem_inc(kept, CREDIT)

        def tops(b, k, banks=range(len(BANK_HEADS))):
            batch, j, n = tile(b, k)
            if 0 in banks:
                dve.wait_ge(scores_ready, n + 1)
            for bank in banks:
                first, heads = BANK_HEADS[bank]
                last = nc.vector.tensor_reduce(neg_top[:, k % 2, first:first + heads],
                                               scores_bank[k % 2][bank][:, 0:KEYS * heads].rearrange("p (h k) -> p h k", k=KEYS),
                                               AX, ALU.max, negate=True)
            if len(BANK_HEADS) - 1 in banks:
                last.then_inc(neg_top_ready, 1)

        def normalise(b, k):
            batch, j, n = tile(b, k)
            dve.wait_ge(exps_ready, n + 1 + CREDIT)
            nc.vector.reciprocal(inverse[:, k % 2, :], sums[:, k % EXPS, :]).then_inc(inverse_ready, 1)
            dve.wait_ge(inverse_ready, n + 1)
            e = exps[:, k % EXPS, 0:ALL_KEYS].rearrange("p (h k) -> p h k", k=KEYS)
            nc.vector.tensor_tensor(e, e, inverse[:, k % 2, :].unsqueeze(2).broadcast_to([P, HEADS, KEYS]), ALU.mult).then_inc(probs_ready, 1)

        def keep(b, k, r):
            batch, j, n = tile(b, k)
            dve.wait_ge(turned, n * R + (r + 1 + R * EXPS))
            if r == 0:
                dve.wait_ge(out_ready, n + 1)
            chunks = len(ROUNDS[r])
            nc.vector.tensor_copy(probsT[:, k % 2, 4 * r:4 * r + chunks, :],
                                  turn_bank[:, 0:P * chunks].rearrange("p (c t) -> p c t", t=P)).then_inc(kept, 1)

        def add(b, k):
            batch, j, n = tile(b, k)
            dve.wait_ge(out_ready, n + 1 + CREDIT)
            row = x[:, bass.ds(n, 1), :].rearrange("p o d -> p (o d)")
            nc.vector.tensor_tensor(row, row, out_bank[:, 0:D], ALU.add).then_inc(out_added, 1)
            dve.wait_ge(out_added, n + 2)
            nc.vector.bn_stats(stats[:, bass.ds(n, 1), :].rearrange("p o s -> p (o s)"), row)

        def step(b, k, ahead, before):
            for r in range(R):
                keep(b, k, r)
                if ahead:
                    tops(b, k + AHEAD, [r])
            if not (isinstance(b, int) and b == BATCH - 1 and k == PER_BATCH - 1):
                normalise(b, k + 1)
            if before:
                add(b, k - 1)

        for k in range(AHEAD):
            tops(0, k)
        normalise(0, 0)
        steps(dve, step)
        add(BATCH - 1, PER_BATCH - 1)


class Early:

    SHAPES = dict(
        features=dict(fm=[P, 8], fb=[P, 1], fcT=[P, 2, D], by16=[P, 8], by8=[P, 16], sign=[P, 1], fcb=[P, D]),
        ffn=dict(wgT=[P, INTER], wuT=[P, INTER], wdT=[P, INTER // P, D], downT=[P, EXPERTS], up=[P, E_CHUNKS, D]),
        gating=dict(gate_w=[P, MOE_E], bias=[P, MOE_E], half_id=[P, MOE_E]))

    def __init__(self, m, io):
        self.io, self.tensors, self.loaded, self.needed = io, {}, {}, {}
        for stage, shapes in self.SHAPES.items():
            self.tensors[stage] = {name: m.sb(name, shape) for name, shape in shapes.items()}
            self.loaded[stage], self.needed[stage] = m.sem(f"{stage}_loaded"), 16 * len(shapes)

    def load(self, sp):
        for stage, tensors in self.tensors.items():
            for name, t in tensors.items():
                sp.dma_start(t[:], self.io[name]).then_inc(self.loaded[stage], 16)

    def wait(self, eng, stage):
        eng.wait_ge(self.loaded[stage], self.needed[stage])


def dense_setup(nc, mk, io, x, stats, xnT, ident, eps, ctxT, keyT, value, early):
    with ExitStack() as stack:
        m = Memory(nc, stack, "a0s")
        norm = Norm(nc, m, x, xnT, ident, eps, stats, stats_made=False)
        NB = 6
        wqT, wo = m.sb("wqT", [P, HEADS, D]), m.sb("wo", [P, HEADS, D])
        wk, wv = m.sb("wk", [P, 1024]), m.sb("wv", [P, 1024])
        kT, vT = m.sb("kT", [P, 8, CTX]), m.sb("vT", [P, 8, CTX])
        valueT = m.sb("valueT", [P, BATCH, PADDED_KEYS])
        banks = [m.bank(f"b{i}") for i in range(NB)]
        x_loaded, k_loaded, v_loaded, fold_loaded, ident_loaded, eps_ready, padded, zeroed = (
            m.sem(n) for n in ("x_loaded", "k_loaded", "v_loaded", "fold_loaded", "ident_loaded", "eps_ready", "padded", "zeroed"))
        proj, kv_kept, folded, keys_kept, values_kept, turned, turned_kept = (
            m.sem(n) for n in ("proj", "kv_kept", "folded", "keys_kept", "values_kept", "turned", "turned_kept"))
        TURNS = BATCH * KEY_CHUNKS // 4
        block = stack.enter_context(nc.Block())

        @block.sync
        def _(sp):
            sp.dma_start(wk[:, :], io["Wk"]).then_inc(k_loaded, 16)
            for w, name in ((wqT, "WqT"), (wo, "Wo")):
                for half in range(2):
                    rows = slice(64 * half, 64 * half + 64)
                    sp.dma_start(w[rows, half:HEADS:2, :], io[name][rows]).then_inc(fold_loaded, 16)
            sp.dma_start(x[:, :, :], io["x"]).then_inc(x_loaded, 16)
            sp.dma_start(ident[:, :], io["ident"]).then_inc(ident_loaded, 16)
            early.load(sp)

        @block.gpsimd
        def _(pool):
            nc.gpsimd.memset(eps[:, :], EPS).then_inc(eps_ready, 1)
            nc.gpsimd.memset(valueT[:, :, ALL_KEYS:PADDED_KEYS], 0.0).then_inc(padded, 1)

        @block.tensor
        def _(pe):
            for c in range(8):
                for i, w in enumerate((wk, wv)):
                    n = 2 * c + i
                    if c == 0:
                        pe.wait_ge((k_loaded, v_loaded)[i], 32 - 16 * i)
                    if n >= NB:
                        pe.wait_ge(kv_kept, n - NB + 1)
                    nc.tensor.matmul(banks[n % NB][:, 0:CTX], w[:, P * c:P * c + P], ctxT[:, :], start=True, stop=True).then_inc(proj, 1)
            pe.wait_ge(fold_loaded, 64)
            pe.wait_ge(zeroed, 1)
            for h in range(HEADS):
                c = h // 2
                for i, (w, kv) in enumerate(((wqT, kT), (wo, vT))):
                    n = 2 * h + i
                    if n < 4:
                        pe.wait_ge(kv_kept, 16 - 4 + n + 1)
                    if n >= NB:
                        pe.wait_ge((keys_kept, values_kept)[i], (n - NB) // 2 + 1)
                    nc.tensor.matmul(banks[n % NB][:, 0:CTX], w[:, h, :], kv[:, c, :], start=True, stop=True).then_inc(folded, 1)
            pe.wait_ge(ident_loaded, 16)
            norm.tensor(pe)
            pe.wait_ge(padded, 1)
            pe.wait_ge(values_kept, HEADS)
            pe.wait_ge(keys_kept, HEADS)
            for t in range(TURNS):
                if t >= NB:
                    pe.wait_ge(turned_kept, t - NB + 1)
                for i in range(4):
                    b, c = (4 * t + i) // KEY_CHUNKS, (4 * t + i) % KEY_CHUNKS
                    last = nc.tensor.transpose(banks[t % NB][:, P * i:P * i + P], valueT[:, b, P * c:P * c + P], ident[:, :])
                last.then_inc(turned, 1)

        @block.scalar
        def _(act):
            act.dma_start(ctxT[:, :], io["ctxT"]).then_inc(k_loaded, 16)
            act.dma_start(wv[:, :], io["Wv"]).then_inc(v_loaded, 16)
            for n in range(16):
                act.wait_ge(proj, n + 1)
                nc.scalar.activation((kT, vT)[n % 2][:, n // 2, :], banks[n % NB][:, 0:CTX], ACT.Copy).then_inc(kv_kept, 1)
            act.wait_ge(eps_ready, 1)
            norm.scalar_deviation(act)
            keys = keyT[:, :].rearrange("p (b h k) -> p b h k", b=BATCH, h=HEADS)
            for n in range(0, 2 * HEADS, 2):
                act.wait_ge(folded, n + 1)
                nc.scalar.activation(keys[:, :, n // 2, :], banks[n % NB][:, 0:CTX].rearrange("p (b k) -> p b k", b=BATCH), ACT.Copy).then_inc(keys_kept, 1)
            norm.scalar_keep(act)
            keep_turned(nc, act, value, banks, turned, turned_kept, TURNS)

        @block.vector
        def _(dve):
            for w in (wqT, wo):
                nc.vector.memset(w[0:64, 1:HEADS:2, :], 0.0)
                last = nc.vector.memset(w[64:P, 0:HEADS:2, :], 0.0)
            last.then_inc(zeroed, 1)
            dve.wait_ge(x_loaded, 16)
            norm.vector_moments(dve)
            values = valueT[:, :, 0:ALL_KEYS].rearrange("p b (h k) -> p b h k", h=HEADS)
            for n in range(1, 2 * HEADS, 2):
                dve.wait_ge(folded, n + 1)
                nc.vector.tensor_copy(values[:, :, n // 2, :], banks[n % NB][:, 0:CTX].rearrange("p (b k) -> p b k", b=BATCH)).then_inc(values_kept, 1)
                norm.vector_scale(n // 2)


def keep_turned(nc, act, value, banks, turned, turned_kept, turns):
    for t in range(turns):
        act.wait_ge(turned, t + 1)
        nc.scalar.activation(value[:, 4 * D * t:4 * D * t + 4 * D], banks[t % len(banks)][:, :], ACT.Copy).then_inc(turned_kept, 1)


def dense_attention(nc, io, x, stats, xnT, ident, eps, ctxT, early):
    with ExitStack() as keep:
        mk = Memory(nc, keep, "a0")
        keyT = mk.sb("keyT", [P, BATCH * ALL_KEYS])
        value = mk.sb("value", [P, BATCH * KEY_CHUNKS * D])
        dense_setup(nc, mk, io, x, stats, xnT, ident, eps, ctxT, keyT, value, early)
        with ExitStack() as stack:
            m = Memory(nc, stack, "a0t")
            pieces = [(bank, 0, KEYS * heads, 0, KEYS * first) for bank, (first, heads) in enumerate(BANK_HEADS)]
            attention(nc, m, stack, x, stats, xnT[:, :].unsqueeze(1), ident, keyT, value, 64 ** -0.5, pieces)


FEATURE_CHUNKS = 2


def feature_setup(nc, io, x, stats, xnT, ident, eps, ctxT, keyT, value, spread, signed_bias, early, sim_w):
    CH = FEATURE_CHUNKS
    with ExitStack() as stack:
        m = Memory(nc, stack, "a1s")
        norm = Norm(nc, m, x, xnT, ident, eps, stats)
        NB = 6
        fm, fb, fcT, by16, by8, sign = (early.tensors["features"][n] for n in ("fm", "fb", "fcT", "by16", "by8", "sign"))
        wq, keysT = m.sb("wq", [P, SIM_HEADS, D]), m.sb("keysT", [P, SIM_HEADS, SUBKEYS])
        minus_fm = m.sb("minus_fm", [P, 8])
        features = m.sb("features", [P, CH, CTX])
        valueT = m.sb("valueT", [P, BATCH, PADDED_KEYS])
        banks = [m.bank(f"b{i}") for i in range(NB)]
        loaded, sims_folded, sims_kept, minus_ready, spread_ready, z_ready, features_ready, keys_ready, folded, folded_kept, turned, turned_kept, padded = (
            m.sem(n) for n in ("loaded", "sims_folded", "sims_kept", "minus_ready", "spread_ready", "z_ready", "features_ready", "keys_ready", "folded",
                               "folded_kept", "turned", "turned_kept", "padded"))
        TURNS = BATCH * KEY_CHUNKS // 4
        half = 4 * KEYS
        block = stack.enter_context(nc.Block())

        @block.sync
        def _(sp):
            sp.dma_start(wq[:, :, :], io["ffn_wq"]).then_inc(loaded, 16)
            sp.dma_start(keysT[:, :, :], io["keysT"]).then_inc(loaded, 16)

        @block.gpsimd
        def _(pool):
            nc.gpsimd.memset(valueT[:, :, ALL_KEYS:PADDED_KEYS], 0.0).then_inc(padded, 1)

        @block.vector
        def _(dve):
            def spread_out():
                nc.vector.tensor_scalar(minus_fm[:, :], fm[:, :], -1.0, None, ALU.mult).then_inc(minus_ready, 1)
                dve.wait_ge(minus_ready, 1)
                s4 = spread[:, :].rearrange("p (h s e) -> p h s e", h=HEADS, s=2)
                for s, w in enumerate((fm, minus_fm)):
                    nc.vector.tensor_tensor(s4[:, :, s, :], w[:, :].unsqueeze(1).broadcast_to([P, HEADS, 8]),
                                            by8[:, :].unsqueeze(2).broadcast_to([P, HEADS, 8]), ALU.mult)
                nc.vector.tensor_tensor(signed_bias[:, :], fb[:, :], sign[:, :], ALU.mult).then_inc(spread_ready, 1)

            early.wait(dve, "features")
            spread_out()
            def spread_keys():
                dve.wait_ge(features_ready, CH)
                k4 = keyT[:, :].rearrange("p (b h k) -> p b h k", b=BATCH, h=HEADS)
                f4 = features[:, :, :].rearrange("p c (b k) -> p c b k", b=BATCH)
                for b in range(BATCH):
                    for ch in range(CH):
                        last = nc.vector.tensor_tensor(k4[:, b, 8 * ch:8 * ch + 8, :],
                                                       f4[:, ch, b, :].unsqueeze(1).broadcast_to([P, 8, KEYS]),
                                                       by16[:, :].unsqueeze(2).broadcast_to([P, 8, KEYS]), ALU.mult)
                    last.then_inc(keys_ready, 1)

            norm.vector_moments(dve, spread_keys)
            for t in range(TILES):
                norm.vector_scale(t)

        @block.tensor
        def _(pe):
            early.wait(pe, "features")
            pe.wait_ge(spread_ready, 1)
            for ch in range(CH):
                nc.tensor.matmul(banks[ch][:, 0:CTX], spread[:, P * ch:P * ch + P], ctxT[:, :], start=True, stop=True).then_inc(z_ready, 1)
            pe.wait_ge(loaded, 32)
            for p in range(2):
                rows = slice(64 * p, 64 * p + 64)
                for h in range(SIM_HEADS):
                    last = nc.tensor.matmul(banks[2 + p][:, SUBKEYS * h:SUBKEYS * h + SUBKEYS], wq[rows, h, :], keysT[rows, h, :], start=True, stop=True)
                last.then_inc(sims_folded, 1)
            pe.wait_ge(sims_kept, 2)
            pe.wait_ge(features_ready, CH)
            for n in range(4 * BATCH):
                b, i = n // 4, n % 4
                pe.wait_ge(keys_ready, b + 1)
                if n >= NB:
                    pe.wait_ge(folded_kept, n - NB + 1)
                nc.tensor.matmul(banks[n % NB][:, 0:half], fcT[:, i // 2, :], keyT[:, b * ALL_KEYS + half * i:b * ALL_KEYS + half * i + half],
                                 start=True, stop=True).then_inc(folded, 1)
            norm.tensor(pe)
            pe.wait_ge(folded_kept, 4 * BATCH)
            pe.wait_ge(padded, 1)
            for t in range(TURNS):
                if t >= NB:
                    pe.wait_ge(turned_kept, t - NB + 1)
                for i in range(4):
                    b, c = (4 * t + i) // KEY_CHUNKS, (4 * t + i) % KEY_CHUNKS
                    last = nc.tensor.transpose(banks[t % NB][:, P * i:P * i + P], valueT[:, b, P * c:P * c + P], ident[:, :])
                last.then_inc(turned, 1)

        @block.scalar
        def _(act):
            for ch in range(CH):
                act.wait_ge(z_ready, ch + 1)
                nc.scalar.activation(features[:, ch, :], banks[ch][:, 0:CTX], ACT.Exp, bias=signed_bias[:, 0:1]).then_inc(features_ready, 1)
            for p in range(2):
                act.wait_ge(sims_folded, p + 1)
                nc.scalar.activation(sim_w[:, p, :], banks[2 + p][:, :], ACT.Copy).then_inc(sims_kept, 1)
            norm.scalar_deviation(act)
            for n in range(4 * BATCH):
                act.wait_ge(folded, n + 1)
                nc.scalar.activation(valueT[:, n // 4, half * (n % 4):half * (n % 4) + half], banks[n % NB][:, 0:half], ACT.Copy).then_inc(folded_kept, 1)
            norm.scalar_keep(act)
            keep_turned(nc, act, value, banks, turned, turned_kept, TURNS)


def feature_attention(nc, x, stats, xnT, ident, eps, keyT, value, spread, signed_bias, early):
    CH = FEATURE_CHUNKS
    with ExitStack() as keep:
        mk = Memory(nc, keep, "a1")
        features = mk.sb("features", [P, CH, TOKENS])
        with ExitStack() as stack:
            m = Memory(nc, stack, "a1q")
            norm = Norm(nc, m, x, xnT, ident, eps, stats)
            fcb = early.tensors["features"]["fcb"]
            banks = [m.bank(f"z{i}") for i in range(4)]
            z_ready, features_ready = m.sem("z_ready"), m.sem("features_ready")
            block = stack.enter_context(nc.Block())

            @block.vector
            def _(dve):
                norm.vector(dve)
                early.wait(dve, "features")
                dve.wait_ge(norm.xn_ready, 4)
                nc.vector.tensor_tensor(x[:, :, :], x[:, :, :], fcb[:, :].unsqueeze(1).broadcast_to([P, TILES, D]), ALU.add)

            @block.tensor
            def _(pe):
                def products(g):
                    pe.wait_ge(norm.kept, g + 1)
                    if g >= 2:
                        pe.wait_ge(features_ready, CH * (g - 1))
                    for ch in range(CH):
                        nc.tensor.matmul(banks[2 * (g % 2) + ch][:, :], spread[:, P * ch:P * ch + P], xnT[:, SEQ * g:SEQ * g + SEQ],
                                         start=True, stop=True).then_inc(z_ready, 1)

                for g in range(BATCH):
                    norm.tensor_group(pe, g)
                    if g:
                        products(g - 1)
                products(BATCH - 1)

            @block.scalar
            def _(act):
                def exponentials(g):
                    for ch in range(CH):
                        act.wait_ge(z_ready, CH * g + ch + 1)
                        nc.scalar.activation(features[:, ch, SEQ * g:SEQ * g + SEQ], banks[2 * (g % 2) + ch][:, :], ACT.Exp,
                                             bias=signed_bias[:, 0:1]).then_inc(features_ready, 1)

                norm.scalar_deviation(act)
                for g in range(BATCH):
                    norm.scalar_keep_group(act, g)
                    if g:
                        exponentials(g - 1)
                exponentials(BATCH - 1)

        with ExitStack() as stack:
            m = Memory(nc, stack, "a1t")
            pieces = [(0, 0, 6 * KEYS, 0, 0), (1, 0, 2 * KEYS, 0, 6 * KEYS), (1, 2 * KEYS, 3 * KEYS, 1, 8 * KEYS), (2, 0, 5 * KEYS, 1, 11 * KEYS)]
            attention(nc, m, stack, x, stats, features[:, :, :], ident, keyT, value, float(D) ** -0.5, pieces)


def product_key_ffn(nc, x, stats, xnT, ident, early, sim_w):
    wgT, wuT, wdT, downT, up = (early.tensors["ffn"][n] for n in ("wgT", "wuT", "wdT", "downT", "up"))
    with ExitStack() as stack:
        m = Memory(nc, stack, "f0t")
        HALF = EXPERTS // 2
        HALF_ROWS, HALF_CHUNKS = ROWS // 2, E_CHUNKS // 2
        PAIR_T = 2 * P
        STREAMS = 3
        Y, X, TOPS = 0, SIM_HEADS * SUBKEYS, SIM_HEADS * (SUBKEYS + ROWS)
        WIDTH = TOPS + 2 * SIM_HEADS * TOPK
        tokens = m.sb("tokens", [P, 2, P])
        hidden = m.sb("hidden", [P, 2, INTER // P, PAIR_T])
        act_w = m.sb("act_w", [P, 2, E_CHUNKS, PAIR_T])
        best = m.sb("best", [P, 2, SIM_HEADS, TOPK])
        shifted, ex = m.sb("shifted", [P, 2, WIDTH]), m.sb("ex", [P, 2, WIDTH])
        pairs = m.sb("pairs", [P, SIM_HEADS, TOPK * TOPK])
        picked = m.sb("picked", [P, SIM_HEADS, TOPK])
        bar = m.sb("bar", [P, SIM_HEADS])
        total, inverse = m.sb("total", [P, SIM_HEADS]), m.sb("inverse", [P, SIM_HEADS])
        unclipped, unclipped_w = m.sb("unclipped", [P, 2, SIM_HEADS]), m.sb("unclipped_w", [P, 2, SIM_HEADS])
        ratio = m.sb("ratio", [P, 2])
        minus_sum, clip_add, carrier = (m.sb(n, [P, 1]) for n in ("minus_sum", "clip_add", "carrier"))
        diag = m.sb("diag", [P, 2, STREAMS, P])
        prod = m.sb("prod", [P, 2, SIM_HEADS, HALF])
        kept = m.sb("kept", [P, 2, STREAMS, HALF])
        mixed = m.sb("mixed", [P, 2, HALF_CHUNKS, P])
        feed_bank = [m.bank(f"feed{i}") for i in range(3)]
        weight_bank = [[m.bank(f"weight{h}{i}") for i in range(2)] for h in range(2)]
        out_bank = m.bank("out")
        tokens_ready, sims_ready, shifted_ready, ex_ready, selected, diag_ready = (
            m.sem(n) for n in ("tokens_ready", "sims_ready", "shifted_ready", "ex_ready", "selected", "diag_ready"))
        FEEDS, SILUS = 12, 10
        feed_ready, silu_ready, hidden_ready = (m.sem(n) for n in ("feed_ready", "silu_ready", "hidden_ready"))
        prod_ready, prod_used, kept_ready, weight_ready, mixed_ready = (
            m.sem(n) for n in ("prod_ready", "prod_used", "kept_ready", "weight_ready", "mixed_ready"))
        out_ready, out_added, best_ready, own_ready, select_chain, keep_chain = (
            m.sem(n) for n in ("out_ready", "out_added", "best_ready", "own_ready", "select_chain", "keep_chain"))
        T = PER_BATCH
        OWN = (1,)
        MADE = [SIM_HEADS - (half in OWN) for half in range(2)]
        UNITS = sum(MADE)
        MIXED_CREDIT = 5
        SELECT_LINKS = 4
        KEEP_LINKS = 4 + (1 in OWN)

        def joined(k, half):
            return k % 2 == 1 and half == 0

        block = stack.enter_context(nc.Block())

        @block.tensor
        def _(pe):
            def sims(q, k):
                n = q * T + k
                pe.wait_ge(tokens_ready, n + 1)
                if k % 2:
                    pe.wait_ge(silu_ready, (q * 2 + k // 2) * SILUS + SILUS)
                    pe.wait_ge(hidden_ready, (q * 2 + k // 2) * 2 + 2)
                elif not (isinstance(n, int) and n == 0):
                    pe.wait_ge(shifted_ready, n)
                for bank in range(2):
                    last = nc.tensor.matmul(feed_bank[bank][:, :], tokens[:, k % 2, :], sim_w[:, bank, :], start=True, stop=True)
                last.then_inc(sims_ready, 1)

            def feed(q, i, steps=range(FEEDS)):
                pair = q * 2 + i
                group = xnT[:, bass.ds(pair * PAIR_T, PAIR_T)]
                for s in steps:
                    if s < 2:
                        pe.wait_ge(shifted_ready, pair * 2 + 1)
                    elif s == 2:
                        pe.wait_ge(hidden_ready, pair * 2 + 1)
                    else:
                        pe.wait_ge(silu_ready, pair * SILUS + (s - 2))
                    w, first = (wgT, 2 * s) if s < 2 else (downT, 2 * (s - 2)) if s < SILUS else (wuT, 2 * (s - SILUS))
                    for j in range(2):
                        c = first + j
                        last = nc.tensor.matmul(feed_bank[s % 3][:, PAIR_T * j:PAIR_T * j + PAIR_T], w[:, P * c:P * c + P], group, start=True, stop=True)
                    last.then_inc(feed_ready, 1)

            def weigh(q, k, half, bank):
                n = q * T + k
                if bank == 0:
                    pe.wait_ge(kept_ready, n * 2 + (half + 1))
                    pe.wait_ge(mixed_ready, n * 2 + (half - 1 + MIXED_CREDIT))
                    if half == 0:
                        pe.wait_ge(diag_ready, n + 1)
                streams = STREAMS - joined(k, half)
                for c in range(4 * bank, 4 * bank + 4):
                    for s in range(streams):
                        last = nc.tensor.matmul(weight_bank[half][c // 4][:, P * (c % 4):P * (c % 4) + P], kept[:, half, s, P * c:P * c + P],
                                                diag[:, k % 2, s, :], start=(s == 0), stop=(s == streams - 1))
                if bank == 1:
                    last.then_inc(weight_ready, 1)

            def mix_out(q, k, half):
                n = q * T + k
                if half == 0:
                    pe.wait_ge(out_added, n + 1)
                    pe.wait_ge(hidden_ready, (q * 2 + k // 2) * 2 + 3)
                    for c in range(INTER // P):
                        nc.tensor.matmul(out_bank[:, 0:D], hidden[:, k // 2 % 2, c, P * (k % 2):P * (k % 2) + P], wdT[:, c, :], start=(c == 0), stop=False)
                pe.wait_ge(mixed_ready, n * 2 + (half + 1 + MIXED_CREDIT))
                for c in range(HALF_CHUNKS):
                    last = nc.tensor.matmul(out_bank[:, 0:D], mixed[:, half, c, :], up[:, HALF_CHUNKS * half + c, :],
                                            start=False, stop=(half == 1 and c == HALF_CHUNKS - 1))
                if half == 1:
                    last.then_inc(out_ready, 1)

            def step(q, k, before=True, ahead=True):
                weigh(q, k, 0, 0)
                weigh(q, k, 0, 1)
                if ahead:
                    sims(q, k + 2)
                if before:
                    mix_out(q, k - 1, 1)
                weigh(q, k, 1, 0)
                if ahead and k % 2 == 0:
                    feed(q, k // 2 + 1, range(0, 3))
                weigh(q, k, 1, 1)
                if ahead and k % 2 == 0:
                    feed(q, k // 2 + 1, range(3, FEEDS))
                mix_out(q, k, 0)

            early.wait(pe, "ffn")
            sims(0, 0)
            feed(0, 0)
            sims(0, 1)
            step(0, 0, before=False)
            with pe.Fori(0, TILES // T - 1) as q:
                for k in range(1, T + 1):
                    step(q, k)
            for k in range(1, T):
                step(TILES // T - 1, k, ahead=k < T - 2)
            mix_out(TILES // T - 1, T - 1, 1)

        @block.scalar
        def _(act):
            def fetch(q, k):
                n = q * T + k
                if k >= 2:
                    act.wait_ge(sims_ready, n - 1)
                nc.scalar.activation(tokens[:, k % 2, :], xnT[:, bass.ds(n * P, P)], ACT.Copy).then_inc(tokens_ready, 1)

            def exponentials(q, k):
                n = q * T + k
                act.wait_ge(shifted_ready, n + 1)
                if k >= 2:
                    act.wait_ge(selected, n - 1)
                nc.scalar.activation(ex[:, k % 2, :], shifted[:, k % 2, :], ACT.Exp).then_inc(ex_ready, 1)

            def silus(q, i):
                pair = q * 2 + i
                for s in range(SILUS):
                    act.wait_ge(feed_ready, pair * FEEDS + (s + 1))
                    if s == 0 and not (isinstance(pair, int) and pair == 0):
                        act.wait_ge(out_added, pair * 2 - 1)
                    if s == 2:
                        act.wait_ge(mixed_ready, pair * 4 + (MIXED_CREDIT - 4))
                    bank = feed_bank[s % 3][:, :].rearrange("p (c t) -> p c t", t=PAIR_T)
                    dst = hidden[:, i % 2, 2 * s:2 * s + 2, :] if s < 2 else act_w[:, i % 2, 2 * (s - 2):2 * (s - 2) + 2, :]
                    nc.scalar.activation(dst, bank, ACT.Silu).then_inc(silu_ready, 1)

            def products(q, k):
                n = q * T + k
                act.wait_ge(ex_ready, n + 1)
                for half in range(2):
                    for h in range(MADE[half]):
                        act.wait_ge(prod_used, n * UNITS + (MADE[0] * half + (1, 3, 2, 4)[h]))
                        for a in range(HALF_ROWS):
                            row = X + ROWS * h + HALF_ROWS * half + a
                            last = nc.scalar.activation(prod[:, half, h, SUBKEYS * a:SUBKEYS * a + SUBKEYS],
                                                        ex[:, k % 2, Y + SUBKEYS * h:Y + SUBKEYS * h + SUBKEYS], ACT.Copy,
                                                        scale=ex[:, k % 2, row:row + 1])
                        last.then_inc(prod_ready, 1)

            def step(q, k, ahead=True):
                if ahead:
                    fetch(q, k + 2)
                if k % 2 == 0:
                    silus(q, k // 2)
                products(q, k)
                if ahead or k < T - 1:
                    exponentials(q, k + 1)

            fetch(0, 0)
            fetch(0, 1)
            exponentials(0, 0)
            step(0, 0)
            with act.Fori(0, TILES // T - 1) as q:
                for k in range(1, T + 1):
                    step(q, k)
            for k in range(1, T):
                step(TILES // T - 1, k, ahead=k < T - 2)

        @block.gpsimd
        def _(pool):
            def diagonals(q, k):
                n = q * T + k
                pool.wait_ge(selected, n + 1)
                if k >= 2:
                    pool.wait_ge(weight_ready, (n - 1) * 2)
                r = inverse[:, 0:SIM_HEADS]
                streams = [P, 1, P]
                nc.gpsimd.tensor_tensor(diag[:, k % 2, 0:1, :], ident[:, :].unsqueeze(1), r[:, 0:1].unsqueeze(2).broadcast_to(streams), ALU.mult)
                nc.gpsimd.tensor_tensor(diag[:, k % 2, 1:STREAMS, :], ident[:, :].unsqueeze(1).broadcast_to([P, 2, P]),
                                        r[:, 2:4].unsqueeze(2).broadcast_to([P, 2, P]), ALU.mult).then_inc(diag_ready, 1)

            diagonals(0, 0)
            diagonals(0, 1)
            diagonals(0, 2)
            diagonals(0, 3)
            with pool.Fori(1, TILES // T) as q:
                for k in range(T):
                    diagonals(q, k)

        @block.vector
        def _(dve):
            tt = nc.vector.tensor_tensor

            def before_max():
                nc.vector.memset(carrier[:, :], 0.0)

            def tops(q, k):
                n = q * T + k
                dve.wait_ge(sims_ready, n + 1)
                before_max()
                for h in range(SIM_HEADS):
                    first, end = SUBKEYS * h, SUBKEYS * h + SUBKEYS
                    nc.vector.max(best[:, 0, h, :], feed_bank[0][:, first:end])
                    last = nc.vector.max(best[:, 1, h, :], feed_bank[1][:, first:end])
                last.then_inc(best_ready, 1)
                dve.wait_ge(best_ready, n + 1)
                if k >= 2:
                    dve.wait_ge(ex_ready, n - 1)
                top = [best[:, side, :, 0:1] for side in range(2)]
                s = shifted[:, k % 2, :]
                sims = [feed_bank[i][:, :].rearrange("p (h k) -> p h k", k=SUBKEYS) for i in range(2)]
                tt(s[:, Y:X].rearrange("p (h k) -> p h k", k=SUBKEYS), sims[1], top[1].broadcast_to([P, SIM_HEADS, SUBKEYS]), ALU.subtract)
                tt(s[:, X:TOPS].rearrange("p (h k) -> p h k", k=ROWS), sims[0][:, :, 0:ROWS], top[0].broadcast_to([P, SIM_HEADS, ROWS]), ALU.subtract)
                s8 = s[:, TOPS:WIDTH].rearrange("p (s h k) -> p s h k", s=2, k=TOPK)
                for i in range(2):
                    last = tt(s8[:, i, :, :], best[:, i, :, :], top[i].broadcast_to([P, SIM_HEADS, TOPK]), ALU.subtract)
                last.then_inc(shifted_ready, 1)

            def select(q, k):
                n = q * T + k
                chain = Chain(dve, select_chain, n * SELECT_LINKS)
                dve.wait_ge(ex_ready, n + 1)
                top8 = ex[:, k % 2, TOPS:WIDTH].rearrange("p (s h k) -> p s h k", s=2, k=TOPK)
                shape = [P, SIM_HEADS, TOPK, TOPK]
                chain.link(tt(pairs[:, :, :].rearrange("p h (i j) -> p h i j", i=TOPK), top8[:, 0, :, :].unsqueeze(3).broadcast_to(shape),
                              top8[:, 1, :, :].unsqueeze(2).broadcast_to(shape), ALU.mult))
                before_max()
                for h in range(SIM_HEADS):
                    last = nc.vector.max(picked[:, h, :], pairs[:, h, :])
                chain.link(last)
                nc.vector.tensor_scalar(bar[:, :], picked[:, :, TOPK - 1], 1.0 - 2.0 ** -22, None, ALU.mult)
                chain.link(nc.vector.tensor_reduce(total[:, :], picked[:, :, :], AX, ALU.add))
                if not (isinstance(n, int) and n == 0):
                    dve.wait_ge(diag_ready, n)
                chain.link(nc.vector.reciprocal(inverse[:, :], total[:, :]))
                tt(ratio[:, :], inverse[:, 1:4:2], total[:, 0:3:2], ALU.mult).then_inc(selected, 1)
                assert chain.n == SELECT_LINKS

            def keep_picked(q, k, half):
                n = q * T + k
                linked = n * KEEP_LINKS + half + (q * (T // 2) + (k + 0) // 2) + (half if joined(k, 0) else 0)
                used = n * UNITS + MADE[0] * half + UNITS
                if not (isinstance(n, int) and n == 0):
                    dve.wait_ge(weight_ready, n * 2 + (half - 1))

                def threshold(dst, h):
                    if h < MADE[half]:
                        dve.wait_ge(prod_ready, n * UNITS + (MADE[0] * half + h + 1))
                    src = prod[:, half, h, :]
                    return nc.vector.scalar_tensor_tensor(dst, src, bar[:, h:h + 1], src, op0=ALU.is_ge, op1=ALU.mult,
                                                          accum_out=unclipped[:, half, h:h + 1])

                own = half in OWN
                if own:
                    h, shape = SIM_HEADS - 1, [P, HALF_ROWS, SUBKEYS]
                    rows = X + ROWS * h + HALF_ROWS * half
                    tt(prod[:, half, h, :].rearrange("p (a k) -> p a k", k=SUBKEYS), ex[:, k % 2, rows:rows + HALF_ROWS].unsqueeze(2).broadcast_to(shape),
                       ex[:, k % 2, Y + SUBKEYS * h:Y + SUBKEYS * h + SUBKEYS].unsqueeze(1).broadcast_to(shape), ALU.mult).then_inc(own_ready, 1)
                both = kept[:, half, 0, :]
                threshold(both, 0).then_inc(prod_used, 1)
                threshold(prod[:, half, 1, :], 1).then_inc(keep_chain, 1)
                threshold(kept[:, half, 1, :], 2).then_inc(prod_used, 1)
                if joined(k, half):
                    threshold(prod[:, half, 3, :], 3).then_inc(keep_chain, 1)
                dve.wait_ge(keep_chain, linked + 1)
                dve.wait_ge(prod_used, used + 1)
                nc.vector.scalar_tensor_tensor(both, prod[:, half, 1, :], ratio[:, 0:1], both, op0=ALU.mult, op1=ALU.add).then_inc(prod_used, 1)
                if own:
                    dve.wait_ge(own_ready, n * len(OWN) + (OWN.index(half) + 1))
                if joined(k, half):
                    dve.wait_ge(keep_chain, linked + 2)
                    dve.wait_ge(prod_used, used + 2)
                    second = kept[:, half, 1, :]
                    last = nc.vector.scalar_tensor_tensor(second, prod[:, half, 3, :], ratio[:, 1:2], second, op0=ALU.mult, op1=ALU.add)
                else:
                    last = threshold(kept[:, half, 2, :], 3)
                if not own:
                    last.then_inc(prod_used, 1)
                if half == 0:
                    nc.vector.memset(carrier[:, :], 0.0).then_inc(kept_ready, 1)
                    return
                if own:
                    last.then_inc(keep_chain, 1)
                    dve.wait_ge(keep_chain, linked + 2)
                else:
                    dve.wait_ge(prod_used, used + 4)
                extra = 1 if own else 0
                nc.vector.scalar_tensor_tensor(unclipped_w[:, :, :], unclipped[:, :, :], -1.0, inverse[:, :].unsqueeze(1).broadcast_to([P, 2, SIM_HEADS]),
                                               op0=ALU.mult, op1=ALU.mult, accum_out=minus_sum[:, :]).then_inc(keep_chain, 1)
                dve.wait_ge(keep_chain, linked + (2 + extra))
                nc.vector.tensor_scalar(clip_add[:, :], minus_sum[:, :], float(SIM_HEADS), total[:, 0:1], ALU.add, ALU.mult).then_inc(keep_chain, 1)
                dve.wait_ge(keep_chain, linked + (3 + extra))
                tt(both[:, HALF - 1:HALF], both[:, HALF - 1:HALF], clip_add[:, :], ALU.add).then_inc(kept_ready, 1)

            def mix(q, k, half):
                n = q * T + k
                dve.wait_ge(weight_ready, n * 2 + (half + 1))
                if not (isinstance(n, int) and n == 0):
                    dve.wait_ge(out_ready, n)
                for i in range(2):
                    cs = slice(4 * i, 4 * i + 4)
                    last = tt(mixed[:, half, cs, :], act_w[:, k // 2 % 2, HALF_CHUNKS * half + 4 * i:HALF_CHUNKS * half + 4 * i + 4, P * (k % 2):P * (k % 2) + P],
                              weight_bank[half][i][:, :].rearrange("p (c t) -> p c t", t=P), ALU.mult)
                last.then_inc(mixed_ready, 1)

            def join(q, i):
                pair = q * 2 + i
                for s in range(2):
                    dve.wait_ge(feed_ready, pair * FEEDS + (SILUS + s + 1))
                    gates = hidden[:, i % 2, 2 * s:2 * s + 2, :]
                    tt(gates, gates,
                       feed_bank[(SILUS + s) % 3][:, :].rearrange("p (c t) -> p c t", t=PAIR_T), ALU.mult).then_inc(hidden_ready, 1)

            def add(q, k):
                n = q * T + k
                dve.wait_ge(out_ready, n + 1)
                row = x[:, bass.ds(n, 1), :].rearrange("p o d -> p (o d)")
                tt(row, row, out_bank[:, 0:D], ALU.add).then_inc(out_added, 1)

            def statistics(q, k):
                n = q * T + k
                dve.wait_ge(out_added, n + 2)
                nc.vector.bn_stats(stats[:, bass.ds(n, 1), :].rearrange("p o s -> p (o s)"), x[:, bass.ds(n, 1), :].rearrange("p o d -> p (o d)"))

            def step(q, k, before=True, ahead=True):
                select(q, k)
                keep_picked(q, k, 0)
                if before:
                    mix(q, k - 1, 1)
                if ahead and k % 2:
                    join(q, (k + 1) // 2)
                keep_picked(q, k, 1)
                if ahead:
                    tops(q, k + 2)
                if before:
                    add(q, k - 1)
                mix(q, k, 0)
                if before:
                    statistics(q, k - 1)

            dve.sem_inc(mixed_ready, MIXED_CREDIT)
            dve.sem_inc(hidden_ready, 1)
            dve.sem_inc(out_added, 1)
            dve.sem_inc(prod_used, UNITS)
            tops(0, 0)
            join(0, 0)
            tops(0, 1)
            step(0, 0, before=False)
            with dve.Fori(0, TILES // T - 1) as q:
                for k in range(1, T + 1):
                    step(q, k)
            for k in range(1, T):
                step(TILES // T - 1, k, ahead=k < T - 2)
            mix(TILES // T - 1, T - 1, 1)
            add(TILES // T - 1, T - 1)
            statistics(TILES // T - 1, T - 1)


def expert_ffn(nc, io, x, stats, xnT, ident, eps, out, early):
    with ExitStack() as keep:
        mk = Memory(nc, keep, "f1")
        combT = mk.sb("combT", [P, TOKENS], F32R)
        gate_w, bias, half_id = (early.tensors["gating"][n] for n in ("gate_w", "bias", "half_id"))
        m = Memory(nc, keep, "f1g")
        wide = [P, TILES, MOE_E]
        score, biased, masked, sel = (m.sb(n, wide) for n in ("score", "biased", "masked", "sel"))
        hi_lo = m.sb("hi_lo", [P, TILES, 2, MOE_E], F32R)
        tour = [m.sb(f"tour{i}", [P, TILES, GROUPS, 4]) for i in range(6)]
        group_score, group_top, mask = (m.sb(n, [P, TILES, GROUPS]) for n in ("group_score", "group_top", "mask"))
        picked = m.sb("picked", [P, TILES, 8])
        total, inverse = m.sb("total", [P, TILES]), m.sb("inverse", [P, TILES])
        chain, logits_ready, score_ready, comb_ready, gates_turned, comb_kept = (m.sem(n) for n in ("chain", "logits_ready", "score_ready", "comb_ready", "gates_turned", "comb_kept"))

        def gate_tensor(pe, norm, logit_bank, turn_bank, meanwhile):
            early.wait(pe, "gating")

            def logits(g):
                pe.wait_ge(norm.kept, g + 1)
                for t in range(4 * g, 4 * g + 4):
                    i = nc.tensor.matmul(logit_bank[t // 8][:, MOE_E * (t % 8):MOE_E * (t % 8) + MOE_E], xnT[:, P * t:P * t + P], gate_w[:, :], start=True, stop=True)
                i.then_inc(logits_ready, 1)

            for g in range(TILES // 4):
                norm.tensor_group(pe, g)
                if g:
                    logits(g - 1)
            logits(TILES // 4 - 1)
            meanwhile()
            pe.wait_ge(comb_ready, 1)
            for t in range(TILES):
                i = nc.tensor.transpose(turn_bank[t // 4][:, P * (t % 4):P * (t % 4) + P],
                                        hi_lo[:, t, :, :].rearrange("p s e -> p (s e)").bitcast(F32), ident[:, :])
            i.then_inc(gates_turned, 1)

        def gate_scalar(act, logit_bank, turn_bank, meanwhile):
            for i in range(2):
                act.wait_ge(logits_ready, 2 * i + 2)
                last = nc.scalar.activation(score[:, 8 * i:8 * i + 8, :], logit_bank[i][:, :].rearrange("p (t e) -> p t e", e=MOE_E), ACT.Sigmoid)
            last.then_inc(score_ready, 1)
            meanwhile()
            act.wait_ge(gates_turned, 1)
            for i in range(4):
                last = nc.scalar.activation(combT[:, 512 * i:512 * i + 512], turn_bank[i][:, :], ACT.Copy)
            last.then_inc(comb_kept, 1)

        def gate_vector(dve):
            k = Chain(dve, chain)
            tt, ts = nc.vector.tensor_tensor, nc.vector.tensor_scalar
            early.wait(dve, "gating")
            dve.wait_ge(score_ready, 1)
            k.link(tt(biased[:, :, :], score[:, :, :], bias[:, :].unsqueeze(1).broadcast_to(wide), ALU.add))
            b4 = biased[:, :, :].rearrange("p t (g e) -> p t g e", e=GROUP_E)
            flat = [t[:, :, :, :].rearrange("p t g e -> p (t g) e") for t in tour]
            b3 = b4.rearrange("p t g e -> p (t g) e")
            best, next_, low, keep_best, keep_next = flat[0], flat[1], flat[2], flat[3], flat[4]
            tt(best, b3[:, :, 0:4], b3[:, :, 4:8], ALU.max)
            k.link(tt(next_, b3[:, :, 0:4], b3[:, :, 4:8], ALU.min))
            for n in (2, 1):
                a, c = slice(0, n), slice(n, 2 * n)
                tt(low[:, :, a], best[:, :, a], best[:, :, c], ALU.min)
                tt(keep_best[:, :, a], best[:, :, a], best[:, :, c], ALU.max)
                k.link(tt(keep_next[:, :, a], next_[:, :, a], next_[:, :, c], ALU.max))
                k.link(tt(next_[:, :, a], low[:, :, a], keep_next[:, :, a], ALU.max))
                best, keep_best = keep_best, best
            k.link(tt(group_score[:, :, :].rearrange("p t g -> p (t g)").unsqueeze(2), best[:, :, 0:1], next_[:, :, 0:1], ALU.add))
            for t in range(TILES):
                last = nc.vector.max(group_top[:, t, :], group_score[:, t, :])
            k.link(last)
            k.link(tt(mask[:, :, :], group_score[:, :, :], group_top[:, :, TOP_GROUPS - 1:TOP_GROUPS].broadcast_to([P, TILES, GROUPS]), ALU.is_ge))
            k.link(ts(mask[:, :, :], mask[:, :, :], 1.0, BIG, ALU.subtract, ALU.mult))
            k.link(tt(masked[:, :, :].rearrange("p t (g e) -> p (t g) e", e=GROUP_E), b3,
                      mask[:, :, :].rearrange("p t g -> p (t g)").unsqueeze(2).broadcast_to([P, TILES * GROUPS, GROUP_E]), ALU.add))
            for t in range(TILES):
                last = nc.vector.max(picked[:, t, :], masked[:, t, :])
            k.link(last)
            k.link(tt(sel[:, :, :], masked[:, :, :], picked[:, :, 7:8].broadcast_to(wide), ALU.is_ge))
            k.link(tt(sel[:, :, :], sel[:, :, :], score[:, :, :], ALU.mult))
            k.link(nc.vector.tensor_reduce(total[:, :], sel[:, :, :], AX, ALU.add))
            k.link(ts(total[:, :], total[:, :], 1e-20, None, ALU.add))
            k.link(nc.vector.reciprocal(inverse[:, :], total[:, :]))
            k.link(ts(inverse[:, :], inverse[:, :], TW_SCALE, None, ALU.mult))
            k.link(tt(sel[:, :, :], sel[:, :, :], inverse[:, :].unsqueeze(2).broadcast_to(wide), ALU.mult))
            k.link(nc.vector.tensor_copy(hi_lo[:, :, 0, :], sel[:, :, :]))
            tt(hi_lo[:, :, 1, :], sel[:, :, :], hi_lo[:, :, 0, :].bitcast(F32), ALU.subtract).then_inc(comb_ready, 1)

        with ExitStack() as stack:
            m = Memory(nc, stack, "f1e")
            W = 3 * P
            NG = TOKENS // 512
            STEP = 2 * NG
            LOOPS = PAIRS // 2
            LAG = 2
            RING = 4
            g_bank, u_bank, c_bank = m.bank("g"), m.bank("u"), m.bank("c")
            norm = Norm(nc, m, x, xnT, ident, eps, stats, banks=[g_bank, u_bank])
            tok_hi, tok_lo = m.sb("tok_hi", [P, TOKENS], F32R), m.sb("tok_lo", [P, TOKENS], F32R)
            raw = m.sb("raw", [P, 2, W])
            one, one_ready = m.sb("one", [P, 1]), m.sem("one_ready")
            w_hi, w_lo = m.sb("w_hi", [P, 2, W], F32R), m.sb("w_lo", [P, 2, W], F32R)
            spread = m.sb("spread", [P, 2, 2, MOE_F], F32R)
            gate, gu, hid = m.sb("gate", [P, 2, 512]), m.sb("gu", [P, 2, 512]), m.sb("hid", [P, 2, 512])
            hid_hi, hid_lo = m.sb("hid_hi", [P, RING, 512], F32R), m.sb("hid_lo", [P, RING, 512], F32R)
            yT = m.sb("yT", [P, TOKENS])
            y_bank = [m.bank(f"y{i}") for i in range(NG)]
            t_bank = m.bank("t")
            raw_loaded = [m.sem(f"raw{i}_loaded") for i in range(2)]
            tok_hi_ready, tok_lo_ready, w_hi_ready, w_ready = (m.sem(n) for n in ("tok_hi_ready", "tok_lo_ready", "w_hi_ready", "w_ready"))
            g_ready, u_ready, c_ready, silu_ready, gu_ready, hid_ready, hi_ready, lo_ready, hid_used = (
                m.sem(n) for n in ("g_ready", "u_ready", "c_ready", "silu_ready", "gu_ready", "hid_ready", "hi_ready", "lo_ready", "hid_used"))
            y_kept, turned, x_ready, stored = (m.sem(n) for n in ("y_kept", "turned", "x_ready", "stored"))
            block = stack.enter_context(nc.Block())

            def steps(eng, first_step, step, last_step):
                first_step()
                with eng.Fori(0, LOOPS - 1) as i:
                    step(i * STEP + NG, i * 2 + 1)
                last_step((LOOPS - 1) * STEP + NG, (LOOPS - 1) * 2 + 1)

            @block.sync
            def _(sp):
                def load(pair, slot, src):
                    sp.dma_start(raw[:, slot, :], src).then_inc(raw_loaded[slot], 16)

                load(0, 0, io["shared"])
                load(1, 1, io["pairs"][:, 0:W])

                def reload(turn, slot, pair):
                    sp.wait_ge(w_ready, turn - 1)
                    load(turn, slot, io["pairs"][:, bass.ds(pair * W, W)])

                with sp.Fori(0, LOOPS - 1) as i:
                    for slot in range(2):
                        reload(i * 2 + (2 + slot), slot, i * 2 + (1 + slot))
                reload(PAIRS, 0, PAIRS - 1)
                for g in range(NG):
                    sp.wait_ge(x_ready, g + 1)
                    sp.dma_start(out[:, 4 * g:4 * g + 4, :], x[:, 4 * g:4 * g + 4, :]).then_inc(stored, 16)
                sp.wait_ge(stored, 16 * NG)

            @block.gpsimd
            def _(pool):
                def split(pair, slot, loads, free):
                    pool.wait_ge(raw_loaded[slot], loads)
                    if free is not None:
                        pool.wait_ge(hid_used, free)
                    nc.gpsimd.tensor_tensor(w_hi[:, slot, :], raw[:, slot, :], one[:, :].broadcast_to([P, W]), ALU.mult).then_inc(w_hi_ready, 1)
                    pool.wait_ge(w_hi_ready, pair + 1)
                    return nc.gpsimd.tensor_tensor(w_lo[:, slot, :], raw[:, slot, :], w_hi[:, slot, :].bitcast(F32), ALU.subtract)

                nc.gpsimd.memset(one[:, :], 1.0).then_inc(one_ready, 1)
                pool.wait_ge(one_ready, 1)
                split(0, 0, 16, None).then_inc(w_ready, 1)
                with pool.Fori(0, LOOPS) as i:
                    for s in range(2):
                        slot = (1 + s) % 2
                        pair = i * 2 + (1 + s)
                        free = i * STEP + (NG if s else 1)
                        split(pair, slot, (i + 1 + s) * 16, free)
                        nc.gpsimd.tensor_copy(spread[:, slot, :, :], half_id[:, bass.ds((i * 2 + s) * 2, 2)].unsqueeze(2).broadcast_to([P, 2, MOE_F])).then_inc(w_ready, 1)

            @block.tensor
            def _(pe):
                def split_product(bank, w_slice, hi, lo, start, stop):
                    slot, cols = w_slice
                    nc.tensor.matmul(bank, w_hi[:, slot, cols], hi, start=start, stop=False)
                    nc.tensor.matmul(bank, w_hi[:, slot, cols], lo, start=False, stop=False)
                    return nc.tensor.matmul(bank, w_lo[:, slot, cols], hi, start=False, stop=stop)

                def up(base, n, pair, shared=False):
                    g, slot = n % NG, (n // NG + (0 if shared else 1)) % 2
                    hi, lo = (t[:, 512 * g:512 * g + 512] for t in (tok_hi, tok_lo))
                    if g == 0:
                        pe.wait_ge(w_ready, pair + 1)
                    if not (shared and n == 0):
                        pe.wait_ge(silu_ready, base + n)
                    split_product(g_bank[:, :], (slot, slice(0, P)), hi, lo, True, True).then_inc(g_ready, 1)
                    if not (shared and n == 0):
                        pe.wait_ge(gu_ready, base + n)
                    split_product(u_bank[:, :], (slot, slice(P, 2 * P)), hi, lo, True, True).then_inc(u_ready, 1)
                    if not shared:
                        pe.wait_ge(hid_ready, base + n)
                        nc.tensor.matmul(c_bank[:, :], spread[:, slot, :, :].rearrange("p a f -> p (a f)"),
                                         combT[:, 512 * g:512 * g + 512], start=True, stop=True).then_inc(c_ready, 1)

                def down(base, n, shared=False, stop=False):
                    g, slot = n % NG, (n // NG + (0 if shared else 1)) % 2
                    pe.wait_ge(lo_ready, base + (n + 1))
                    split_product(y_bank[g][:, :], (slot, slice(2 * P, 3 * P)), hid_hi[:, n % RING, :], hid_lo[:, n % RING, :],
                                  shared, stop).then_inc(hid_used, 1)

                def residual(g):
                    for i in range(4):
                        nc.tensor.matmul(y_bank[g][:, P * i:P * i + P], x[:, 4 * g + i, :], ident[:, :], start=False, stop=False)

                def first_step():
                    for n in range(NG + LAG):
                        if n == LAG:
                            pe.wait_ge(comb_kept, 1)
                        if 0 < n < NG:
                            up(0, n, 0, shared=True)
                        elif n:
                            up(NG, n - NG, 1)
                        if n >= LAG:
                            down(0, n - LAG, shared=True)
                            residual(n - LAG)

                def step(base, pair):
                    for n in range(STEP):
                        k = n + LAG
                        up(base, k, pair + k // NG)
                        down(base, n)

                def last_step(base, pair):
                    for n in range(STEP):
                        k = n + LAG
                        if k < STEP:
                            up(base, k, pair + k // NG)
                        down(base, n, stop=(n >= STEP - NG))

                def first_up():
                    pe.wait_ge(tok_lo_ready, 1)
                    up(0, 0, 0, shared=True)

                gate_tensor(pe, norm, [c_bank, t_bank], y_bank, first_up)
                steps(pe, first_step, step, last_step)
                turn_bank = (t_bank, g_bank, u_bank, c_bank)
                for g in range(NG):
                    pe.wait_ge(y_kept, g + 1)
                    for i in range(4):
                        t = 4 * g + i
                        last = nc.tensor.transpose(turn_bank[g][:, P * i:P * i + P], yT[:, P * t:P * t + P], ident[:, :])
                    last.then_inc(turned, 1)

            @block.scalar
            def _(act):
                def silu(base, n, first=False):
                    act.wait_ge(g_ready, base + (n + 1))
                    if not first:
                        act.wait_ge(gu_ready, base + (n - 1))
                    nc.scalar.activation(gate[:, n % 2, :], g_bank[:, :], ACT.Silu).then_inc(silu_ready, 1)

                def high(base, n, first=False):
                    act.wait_ge(hid_ready, base + (n + 1))
                    if not first:
                        act.wait_ge(hid_used, base + (n + 2 - RING))
                    nc.scalar.activation(hid_hi[:, n % RING, :], hid[:, n % 2, :], ACT.Copy).then_inc(hi_ready, 1)

                def token_split():
                    norm.scalar_deviation(act)
                    for i in range(NG):
                        norm.scalar_keep_group(act, i)
                        act.wait_ge(norm.kept, i + 1)
                        last = nc.scalar.activation(tok_hi[:, 512 * i:512 * i + 512], xnT[:, 512 * i:512 * i + 512], ACT.Copy)
                        last.then_inc(tok_hi_ready, 1)

                def first_step():
                    for n in range(NG):
                        if n:
                            silu(0, n, first=(n < 2))
                            high(0, n - 1, first=True)

                def step(base, pair):
                    for n in range(STEP):
                        silu(base, n)
                        high(base, n - 1)

                def last_step(base, pair):
                    step(base, pair)
                    high(base, STEP - 1)

                token_split()
                gate_scalar(act, [c_bank, t_bank], y_bank, lambda: silu(0, 0, first=True))
                steps(act, first_step, step, last_step)
                for g in range(NG):
                    act.wait_ge(hid_used, PAIRS * NG + g + 1)
                    nc.scalar.activation(yT[:, 512 * g:512 * g + 512], y_bank[g][:, :], ACT.Copy).then_inc(y_kept, 1)

            @block.vector
            def _(dve):
                def hidden(base, n, shared=False):
                    dve.wait_ge(silu_ready, base + (n + 1))
                    dve.wait_ge(u_ready, base + (n + 1))
                    nc.vector.tensor_tensor(gu[:, n % 2, :], gate[:, n % 2, :], u_bank[:, :], ALU.mult).then_inc(gu_ready, 1)
                    dve.wait_ge(gu_ready, base + (n + 1))
                    if shared:
                        nc.vector.tensor_copy(hid[:, n % 2, :], gu[:, n % 2, :]).then_inc(hid_ready, 1)
                    else:
                        dve.wait_ge(c_ready, base + (n + 1 - NG))
                        nc.vector.tensor_tensor(hid[:, n % 2, :], gu[:, n % 2, :], c_bank[:, :], ALU.mult).then_inc(hid_ready, 1)

                def low(base, n):
                    dve.wait_ge(hi_ready, base + (n + 1))
                    nc.vector.tensor_tensor(hid_lo[:, n % RING, :], hid[:, n % 2, :], hid_hi[:, n % RING, :].bitcast(F32), ALU.subtract).then_inc(lo_ready, 1)

                def token_split():
                    norm.vector(dve)
                    for i in range(NG):
                        dve.wait_ge(tok_hi_ready, i + 1)
                        group = slice(512 * i, 512 * i + 512)
                        last = nc.vector.tensor_tensor(tok_lo[:, group], xnT[:, group], tok_hi[:, group].bitcast(F32), ALU.subtract)
                    last.then_inc(tok_lo_ready, 1)

                def first_step():
                    for n in range(NG):
                        hidden(0, n, shared=True)
                        if n:
                            low(0, n - 1)

                def step(base, pair):
                    for n in range(STEP):
                        hidden(base, n)
                        low(base, n - 1)

                def last_step(base, pair):
                    step(base, pair)
                    low(base, STEP - 1)

                token_split()
                gate_vector(dve)
                steps(dve, first_step, step, last_step)
                for g in range(NG):
                    dve.wait_ge(turned, g + 1)
                    nc.vector.tensor_copy(x[:, 4 * g:4 * g + 4, :], (t_bank, g_bank, u_bank, c_bank)[g][:, :].rearrange("p (t d) -> p t d", t=4)).then_inc(x_ready, 1)


def program(nc, io, out):
    with ExitStack() as stack:
        m = Memory(nc, stack, "main")
        x = m.sb("x", [P, TILES, D])
        xnT = m.sb("xnT", [P, TOKENS])
        ctxT = m.sb("ctxT", [P, CTX])
        ident = m.sb("ident", [P, P])
        stats = m.sb("stats", [P, TILES, 6])
        eps = m.sb("eps", [P, 1])
        early = Early(Memory(nc, stack, "early"), io)
        sim_w = m.sb("sim_w", [P, 2, SIM_HEADS * SUBKEYS])
        dense_attention(nc, io, x, stats, xnT, ident, eps, ctxT, early)
        with ExitStack() as layer1:
            m1 = Memory(nc, layer1, "layer1")
            keyT, value = m1.sb("keyT", [P, BATCH * ALL_KEYS]), m1.sb("value", [P, BATCH * KEY_CHUNKS * D])
            spread, signed_bias = m1.sb("spread", [P, FEATURE_CHUNKS * P]), m1.sb("signed_bias", [P, 1])
            feature_setup(nc, io, x, stats, xnT, ident, eps, ctxT, keyT, value, spread, signed_bias, early, sim_w)
            product_key_ffn(nc, x, stats, xnT, ident, early, sim_w)
            feature_attention(nc, x, stats, xnT, ident, eps, keyT, value, spread, signed_bias, early)
        expert_ffn(nc, io, x, stats, xnT, ident, eps, out, early)


def kernel(**inputs):
    import numpy as np
    import concourse.bacc as bacc
    from concourse.bass_utils import run_bass_kernel_spmd as run

    a = {k: np.asarray(v) for k, v in inputs.items()}
    rows = np.arange(P)
    pairs = np.concatenate([
        a["L1_ffn_We_gate"].reshape(PAIRS, 2, D, MOE_F).transpose(2, 0, 1, 3).reshape(D, PAIRS, P),
        a["L1_ffn_We_up"].reshape(PAIRS, 2, D, MOE_F).transpose(2, 0, 1, 3).reshape(D, PAIRS, P),
        a["L1_ffn_We_down"].reshape(PAIRS, P, D).transpose(1, 0, 2)], axis=2)
    shared = np.zeros((P, 3 * P), np.float32)
    shared[:, 0:MOE_F] = a["L1_ffn_Ws_gate"]
    shared[:, P:P + MOE_F] = a["L1_ffn_Ws_up"]
    shared[0:MOE_F, 2 * P:2 * P + D] = a["L1_ffn_Ws_down"]
    laid = {
        "x": a["x"].reshape(TILES, P, D).transpose(1, 0, 2),
        "ctxT": a["ctx_1024"].reshape(CTX, D).T,
        "WqT": a["L0_xattn_Wq"].T.reshape(8, P, D).transpose(1, 0, 2),
        "Wk": a["L0_xattn_Wk"],
        "Wv": a["L0_xattn_Wv"],
        "Wo": a["L0_xattn_Wo"].reshape(8, P, D).transpose(1, 0, 2),
        "ffn_wq": a["L0_ffn_Wq"].reshape(2, SIM_HEADS, 64, D).transpose(0, 2, 1, 3).reshape(P, SIM_HEADS, D),
        "keysT": a["L0_ffn_keys"].transpose(2, 3, 0, 1).reshape(P, SIM_HEADS, SUBKEYS),
        "downT": a["L0_ffn_down_embed"].T,
        "up": a["L0_ffn_up_embed"].reshape(E_CHUNKS, P, D).transpose(1, 0, 2),
        "wgT": a["L0_ffn_Wg"].T,
        "wuT": a["L0_ffn_Wu"].T,
        "wdT": a["L0_ffn_Wd"].T.reshape(INTER // P, P, D).transpose(1, 0, 2),
        "fm": np.tile(a["L1_xattn_fm_w"].T, (16, 1)),
        "fb": np.tile(a["L1_xattn_fm_b"], 16).reshape(P, 1),
        "fcT": a["L1_xattn_fc_w"].T.reshape(2, P, D).transpose(1, 0, 2),
        "fcb": np.tile(a["L1_xattn_fc_b"], (P, 1)),
        "gate_w": a["L1_ffn_gate_w"].T,
        "bias": np.tile(a["L1_ffn_gate_bias"], (P, 1)),
        "pairs": pairs.reshape(D, PAIRS * 3 * P),
        "shared": shared,
        "ident": np.eye(P, dtype=np.float32),
        "by16": (rows[:, None] // 16 == np.arange(8)).astype(np.float32),
        "by8": (rows[:, None] // 8 == np.arange(16)).astype(np.float32),
        "sign": (1.0 - 2.0 * (rows[:, None] // 8 % 2)).astype(np.float32),
        "half_id": (rows[:, None] % MOE_E == np.arange(MOE_E)).astype(np.float32),
    }
    laid = {k: np.ascontiguousarray(v) for k, v in laid.items()}
    nc = bacc.Bacc("TRN2", target_bir_lowering=False, num_devices=1)
    io = {k: nc.dram_tensor(f"in_{k}", v.shape, F32, kind="ExternalInput").ap() for k, v in laid.items()}
    out = nc.dram_tensor("out_x", (P, TILES, D), F32, kind="ExternalOutput").ap()
    program(nc, io, out)
    r = run(nc, [{f"in_{k}": v for k, v in laid.items()}], core_ids=[0])
    got = r.results[0]["out_x"]
    return np.ascontiguousarray(got.transpose(1, 0, 2)).reshape(BATCH, SEQ, D)
```
